# Optimizing a Trainium2 kernel written in Bass

```python
import numpy as np
import jax
import jax.numpy as jnp

def _softmax(x, axis=-1):
    return jax.nn.softmax(x, axis=axis)

def _gelu(x):
    return jax.nn.gelu(x, approximate=True)

def _silu(x):
    return jax.nn.silu(x)

def _sigmoid(x):
    return jax.nn.sigmoid(x)

def _layernorm(x, axis=-1, eps=1e-05):
    m = jnp.mean(x, axis=axis, keepdims=True)
    v = jnp.var(x, axis=axis, keepdims=True)
    return (x - m) / jnp.sqrt(v + eps)

def _scatter_add(tgt, idx, src, axis=0):
    return tgt.at[idx].add(src)

def _segment_sum(src, seg, n):
    return jax.ops.segment_sum(src, seg, n)
kernel_name = 'mk_gnn_resnorm_d4_gnn_r32_7fbdf9'

def setup_inputs(seed: int=0):
    np.random.seed(seed)
    _w = jnp.asarray

    def _rec_inputs():
        import jax
        import jax.numpy as jnp
        _gk = jax.random.key(seed)
        x = -0.0003713 + 1 * jax.random.normal(jax.random.fold_in(_gk, 1), (50000, 128), jnp.float32)
        src = jax.random.randint(jax.random.fold_in(_gk, 2), (25000,), 0, 50000, jnp.int32)
        dst = jnp.minimum((50000 * jax.random.uniform(jax.random.fold_in(_gk, 3), (25000,)) ** 2.0).astype(jnp.int32), 49999)
        _o = jnp.argsort(dst, stable=True)
        src = src[_o]
        dst = dst[_o]
        edge_attr_128 = 0.000143583 + 1.00013 * jax.random.normal(jax.random.fold_in(_gk, 12), (25000, 128), jnp.float32)
        edge_attr_2 = -0.000414295 + 0.999828 * jax.random.normal(jax.random.fold_in(_gk, 13), (25000, 2), jnp.float32)
        edge_weight = jax.random.uniform(jax.random.fold_in(_gk, 15), (25000,), jnp.float32, 0.0, 999.998)
        node_vec = jax.random.uniform(jax.random.fold_in(_gk, 16), (50000,), jnp.float32, 0.0, 999.994)
        return (x, src, dst, edge_attr_128, edge_attr_2, edge_weight, node_vec)
    x, src, dst, edge_attr_128, edge_attr_2, edge_weight, node_vec = _rec_inputs()

    def _L0_gnn_setup():
        import jax, jax.numpy as jnp
        import numpy as np
        N, E = (3125, 20000)
        D_IN = 128
        D_OUT = 128
        H, C = (2, 64)
        MSG = 128
        TD = 128
        EDGE_DIM = MSG + TD

        def _forward(x, last_update, t, msg, w_time, b_time, W_q, b_q, W_k, b_k, W_v, b_v, W_e, W_skip, b_skip, edge_index):
            src, dst = (edge_index[0], edge_index[1])
            n = x.shape[0]
            rel_t = last_update[src] - t
            rel_t_enc = jnp.cos(rel_t[:, None] * w_time + b_time)
            edge_attr = jnp.concatenate([msg, rel_t_enc], axis=-1)
            q = (x @ W_q + b_q).reshape(n, H, C)[dst]
            k = (x @ W_k + b_k)[src].reshape(-1, H, C)
            v = (x @ W_v + b_v)[src].reshape(-1, H, C)
            e = (edge_attr @ W_e).reshape(-1, H, C)
            k = k + e
            alpha = jnp.einsum('ehc,ehc->eh', q, k) / jnp.sqrt(jnp.float32(C))
            m = jax.ops.segment_max(alpha, dst, num_segments=n)
            ea = jnp.exp(alpha - m[dst])
            denom = jax.ops.segment_sum(ea, dst, num_segments=n)
            attn = ea / (denom[dst] + 1e-16)
            out_e = (v + e) * attn[:, :, None]
            out = jax.ops.segment_sum(out_e, dst, num_segments=n)
            out = out.reshape(n, H * C)
            return out + x @ W_skip + b_skip
        key = jax.random.key(seed)
        ks = jax.random.split(key, 16)
        s_in = 1.0 / np.sqrt(D_IN)
        s_e = 1.0 / np.sqrt(EDGE_DIM)
        return {'x': jax.random.normal(ks[0], (N, D_IN), jnp.float32), 'last_update': jax.random.uniform(ks[1], (N,), jnp.float32, 0.0, 1000.0), 't': jax.random.uniform(ks[2], (E,), jnp.float32, 0.0, 1000.0), 'msg': jax.random.normal(ks[3], (E, MSG), jnp.float32), 'w_time': jax.random.normal(ks[4], (TD,), jnp.float32), 'b_time': jax.random.normal(ks[5], (TD,), jnp.float32) * 0.1, 'W_q': jax.random.normal(ks[6], (D_IN, H * C), jnp.float32) * s_in, 'b_q': jnp.zeros((H * C,), jnp.float32), 'W_k': jax.random.normal(ks[7], (D_IN, H * C), jnp.float32) * s_in, 'b_k': jnp.zeros((H * C,), jnp.float32), 'W_v': jax.random.normal(ks[8], (D_IN, H * C), jnp.float32) * s_in, 'b_v': jnp.zeros((H * C,), jnp.float32), 'W_e': jax.random.normal(ks[9], (EDGE_DIM, H * C), jnp.float32) * s_e, 'W_skip': jax.random.normal(ks[10], (D_IN, H * C), jnp.float32) * s_in, 'b_skip': jnp.zeros((H * C,), jnp.float32), 'edge_index': jax.random.randint(ks[11], (2, E), 0, N, jnp.int64)}
    _L0_gnn_all = _L0_gnn_setup()
    _L0_gnn_in = {k: v for k, v in _L0_gnn_all.items() if k in ('w_time', 'b_time', 'W_q', 'b_q', 'W_k', 'b_k', 'W_v', 'b_v', 'W_e', 'W_skip', 'b_skip')}
    del _L0_gnn_all

    def _L1_gnn_setup():
        import jax, jax.numpy as jnp
        import numpy as np
        N = 50000
        E = 25000
        D = 128

        def _lin(key, fan_in, fan_out):
            kw, kb = jax.random.split(key)
            s = 1.0 / np.sqrt(fan_in)
            W = jax.random.uniform(kw, (fan_in, fan_out), jnp.float32, -s, s)
            b = jax.random.uniform(kb, (fan_out,), jnp.float32, -s, s)
            return (W, b)
        key = jax.random.key(seed)
        ks = jax.random.split(key, 8)
        x = jax.random.normal(ks[0], (N, D), jnp.float32)
        edge_index = jax.random.randint(ks[1], (2, E), 0, N, dtype=jnp.int64)
        W1, b1 = _lin(ks[2], D, D)
        Wr1, br1 = _lin(ks[3], D, D)
        W2, b2 = _lin(ks[4], D, D)
        Wr2, br2 = _lin(ks[5], D, D)
        W3, b3 = _lin(ks[6], D, D)
        return dict(x=x, W1=W1, b1=b1, Wr1=Wr1, br1=br1, W2=W2, b2=b2, Wr2=Wr2, br2=br2, W3=W3, b3=b3, edge_index=edge_index)
    _L1_gnn_all = _L1_gnn_setup()
    _L1_gnn_in = {k: v for k, v in _L1_gnn_all.items() if k in ('W1', 'b1', 'Wr1', 'br1', 'W2', 'b2', 'Wr2', 'br2', 'W3', 'b3')}
    del _L1_gnn_all

    def _L2_gnn_setup():
        import jax, jax.numpy as jnp
        import numpy as np
        N_NODES = 50000
        N_EDGES = 15625
        D = 128
        RRELU_SLOPE = (1.0 / 8.0 + 1.0 / 3.0) / 2.0

        def _leaky(x):
            return jnp.where(x >= 0, x, x * RRELU_SLOPE)

        def _layer(h, e, src, dst, W1, W2, W3):
            n = h.shape[0]
            msg = (h[src] + e) @ W1.T
            deg = jax.ops.segment_sum(jnp.ones(src.shape[0], h.dtype), dst, num_segments=n)
            agg = jax.ops.segment_sum(msg, dst, num_segments=n)
            neigh = agg / jnp.maximum(deg, 1.0)[:, None]
            iso = (deg == 0)[:, None]
            self_msg = jnp.where(iso, h @ W3.T, h @ W2.T)
            return _leaky(neigh + self_msg)
        key = jax.random.key(seed)
        ks = jax.random.split(key, 10)
        inp = {'node_feats': jax.random.normal(ks[0], (N_NODES, D), dtype=jnp.float32), 'edge_feats': jax.random.normal(ks[1], (N_EDGES, D), dtype=jnp.float32), 'src': jax.random.randint(ks[2], (N_EDGES,), 0, N_NODES, dtype=jnp.int32), 'dst': jax.random.randint(ks[3], (N_EDGES,), 0, N_NODES, dtype=jnp.int32)}
        scale = 1.0 / np.sqrt(D)
        for i, name in enumerate(['W1_0', 'W2_0', 'W3_0', 'W1_1', 'W2_1', 'W3_1']):
            inp[name] = jax.random.uniform(ks[4 + i], (D, D), dtype=jnp.float32, minval=-scale, maxval=scale)
        return inp
    _L2_gnn_all = _L2_gnn_setup()
    _L2_gnn_in = {k: v for k, v in _L2_gnn_all.items() if k in ('W1_0', 'W2_0', 'W3_0', 'W1_1', 'W2_1', 'W3_1')}
    del _L2_gnn_all

    def _L3_gnn_setup():
        import jax, jax.numpy as jnp
        import numpy as np
        N_NODES = 50000
        N_EDGES = 25000
        D = 128
        ED = 2
        key = jax.random.key(seed)
        ks = jax.random.split(key, 7)
        return {'h': jax.random.normal(ks[0], (N_NODES, D), dtype=jnp.float32), 'e': jax.random.normal(ks[1], (N_EDGES, ED), dtype=jnp.float32), 'src': jax.random.randint(ks[2], (N_EDGES,), 0, N_NODES), 'dst': jax.random.randint(ks[3], (N_EDGES,), 0, N_NODES), 'w_edge': jax.random.normal(ks[4], (ED, ED), dtype=jnp.float32), 'w_attn': jax.random.normal(ks[5], (1, 2 * D + ED), dtype=jnp.float32) * 0.1, 'w_e2n': jax.random.normal(ks[6], (D, ED), dtype=jnp.float32)}
    _L3_gnn_all = _L3_gnn_setup()
    _L3_gnn_in = {k: v for k, v in _L3_gnn_all.items() if k in ('w_edge', 'w_attn', 'w_e2n')}
    del _L3_gnn_all
    return {'x': x, 'src': src, 'dst': dst, 'edge_attr_128': edge_attr_128, 'edge_attr_2': edge_attr_2, 'edge_weight': edge_weight, 'node_vec': node_vec, 'L0_gnn_w_time': _L0_gnn_in['w_time'], 'L0_gnn_b_time': _L0_gnn_in['b_time'], 'L0_gnn_W_q': _L0_gnn_in['W_q'], 'L0_gnn_b_q': _L0_gnn_in['b_q'], 'L0_gnn_W_k': _L0_gnn_in['W_k'], 'L0_gnn_b_k': _L0_gnn_in['b_k'], 'L0_gnn_W_v': _L0_gnn_in['W_v'], 'L0_gnn_b_v': _L0_gnn_in['b_v'], 'L0_gnn_W_e': _L0_gnn_in['W_e'], 'L0_gnn_W_skip': _L0_gnn_in['W_skip'], 'L0_gnn_b_skip': _L0_gnn_in['b_skip'], 'L1_gnn_W1': _L1_gnn_in['W1'], 'L1_gnn_b1': _L1_gnn_in['b1'], 'L1_gnn_Wr1': _L1_gnn_in['Wr1'], 'L1_gnn_br1': _L1_gnn_in['br1'], 'L1_gnn_W2': _L1_gnn_in['W2'], 'L1_gnn_b2': _L1_gnn_in['b2'], 'L1_gnn_Wr2': _L1_gnn_in['Wr2'], 'L1_gnn_br2': _L1_gnn_in['br2'], 'L1_gnn_W3': _L1_gnn_in['W3'], 'L1_gnn_b3': _L1_gnn_in['b3'], 'L2_gnn_W1_0': _L2_gnn_in['W1_0'], 'L2_gnn_W2_0': _L2_gnn_in['W2_0'], 'L2_gnn_W3_0': _L2_gnn_in['W3_0'], 'L2_gnn_W1_1': _L2_gnn_in['W1_1'], 'L2_gnn_W2_1': _L2_gnn_in['W2_1'], 'L2_gnn_W3_1': _L2_gnn_in['W3_1'], 'L3_gnn_w_edge': _L3_gnn_in['w_edge'], 'L3_gnn_w_attn': _L3_gnn_in['w_attn'], 'L3_gnn_w_e2n': _L3_gnn_in['w_e2n']}

def reference(x, src, dst, edge_attr_128, edge_attr_2, edge_weight, node_vec, L0_gnn_w_time, L0_gnn_b_time, L0_gnn_W_q, L0_gnn_b_q, L0_gnn_W_k, L0_gnn_b_k, L0_gnn_W_v, L0_gnn_b_v, L0_gnn_W_e, L0_gnn_W_skip, L0_gnn_b_skip, L1_gnn_W1, L1_gnn_b1, L1_gnn_Wr1, L1_gnn_br1, L1_gnn_W2, L1_gnn_b2, L1_gnn_Wr2, L1_gnn_br2, L1_gnn_W3, L1_gnn_b3, L2_gnn_W1_0, L2_gnn_W2_0, L2_gnn_W3_0, L2_gnn_W1_1, L2_gnn_W2_1, L2_gnn_W3_1, L3_gnn_w_edge, L3_gnn_w_attn, L3_gnn_w_e2n):
    import jax
    import jax.numpy as jnp

    def _L0_gnn_ref(x, last_update, t, msg, w_time, b_time, W_q, b_q, W_k, b_k, W_v, b_v, W_e, W_skip, b_skip, edge_index):
        import jax, jax.numpy as jnp
        import numpy as np
        N, E = (3125, 20000)
        D_IN = 128
        D_OUT = 128
        H, C = (2, 64)
        MSG = 128
        TD = 128
        EDGE_DIM = MSG + TD

        def _forward(x, last_update, t, msg, w_time, b_time, W_q, b_q, W_k, b_k, W_v, b_v, W_e, W_skip, b_skip, edge_index):
            src, dst = (edge_index[0], edge_index[1])
            n = x.shape[0]
            rel_t = last_update[src] - t
            rel_t_enc = jnp.cos(rel_t[:, None] * w_time + b_time)
            edge_attr = jnp.concatenate([msg, rel_t_enc], axis=-1)
            q = (x @ W_q + b_q).reshape(n, H, C)[dst]
            k = (x @ W_k + b_k)[src].reshape(-1, H, C)
            v = (x @ W_v + b_v)[src].reshape(-1, H, C)
            e = (edge_attr @ W_e).reshape(-1, H, C)
            k = k + e
            alpha = jnp.einsum('ehc,ehc->eh', q, k) / jnp.sqrt(jnp.float32(C))
            m = jax.ops.segment_max(alpha, dst, num_segments=n)
            ea = jnp.exp(alpha - m[dst])
            denom = jax.ops.segment_sum(ea, dst, num_segments=n)
            attn = ea / (denom[dst] + 1e-16)
            out_e = (v + e) * attn[:, :, None]
            out = jax.ops.segment_sum(out_e, dst, num_segments=n)
            out = out.reshape(n, H * C)
            return out + x @ W_skip + b_skip
        return _forward(x, last_update, t, msg, w_time, b_time, W_q, b_q, W_k, b_k, W_v, b_v, W_e, W_skip, b_skip, edge_index)

    def _L1_gnn_ref(x, W1, b1, Wr1, br1, W2, b2, Wr2, br2, W3, b3, edge_index):
        import jax, jax.numpy as jnp
        import numpy as np
        N = 50000
        E = 25000
        D = 128

        def _lin(key, fan_in, fan_out):
            kw, kb = jax.random.split(key)
            s = 1.0 / np.sqrt(fan_in)
            W = jax.random.uniform(kw, (fan_in, fan_out), jnp.float32, -s, s)
            b = jax.random.uniform(kb, (fan_out,), jnp.float32, -s, s)
            return (W, b)
        src, dst = (edge_index[0], edge_index[1])
        n = x.shape[0]
        ones = jnp.ones(src.shape[0], x.dtype)
        deg_out = jax.ops.segment_sum(ones, src, num_segments=n)
        deg_in = jax.ops.segment_sum(ones, dst, num_segments=n)
        ns = jnp.clip(deg_out, 1.0) ** (-0.5)
        nd = jnp.clip(deg_in, 1.0) ** (-0.5)

        def conv(h, W, b):
            msg = h[src] * ns[src, None]
            agg = jax.ops.segment_sum(msg, dst, num_segments=n)
            return agg * nd[:, None] @ W + b
        h1 = jax.nn.relu(conv(x, W1, b1)) + (x @ Wr1 + br1)
        h2 = jax.nn.relu(conv(h1, W2, b2)) + (h1 @ Wr2 + br2)
        out = conv(h2, W3, b3)
        return out

    def _L2_gnn_ref(node_feats, edge_feats, src, dst, W1_0, W2_0, W3_0, W1_1, W2_1, W3_1):
        import jax, jax.numpy as jnp
        import numpy as np
        N_NODES = 50000
        N_EDGES = 15625
        D = 128
        RRELU_SLOPE = (1.0 / 8.0 + 1.0 / 3.0) / 2.0

        def _leaky(x):
            return jnp.where(x >= 0, x, x * RRELU_SLOPE)

        def _layer(h, e, src, dst, W1, W2, W3):
            n = h.shape[0]
            msg = (h[src] + e) @ W1.T
            deg = jax.ops.segment_sum(jnp.ones(src.shape[0], h.dtype), dst, num_segments=n)
            agg = jax.ops.segment_sum(msg, dst, num_segments=n)
            neigh = agg / jnp.maximum(deg, 1.0)[:, None]
            iso = (deg == 0)[:, None]
            self_msg = jnp.where(iso, h @ W3.T, h @ W2.T)
            return _leaky(neigh + self_msg)
        h = _layer(node_feats, edge_feats, src, dst, W1_0, W2_0, W3_0)
        h = _layer(h, edge_feats, src, dst, W1_1, W2_1, W3_1)
        return h

    def _L3_gnn_ref(h, e, src, dst, w_edge, w_attn, w_e2n):
        import jax, jax.numpy as jnp
        import numpy as np
        N_NODES = 50000
        N_EDGES = 25000
        D = 128
        ED = 2
        n = h.shape[0]
        ex = e @ w_edge.T
        z2 = jnp.concatenate([h[src], h[dst], ex], axis=1)
        a = jax.nn.leaky_relu(z2 @ w_attn.T, negative_slope=0.01)[:, 0]
        ez = ex @ w_e2n.T
        a_max = jax.ops.segment_max(a, dst, num_segments=n)
        a_exp = jnp.exp(a - a_max[dst])
        denom = jax.ops.segment_sum(a_exp, dst, num_segments=n)
        attn = a_exp / jnp.maximum(denom[dst], jnp.asarray(1e-16, a_exp.dtype))
        return jax.ops.segment_sum(attn[:, None] * ez, dst, num_segments=n)
    edge_index = jnp.stack([src, dst])
    x = _layernorm(x + _L0_gnn_ref(x, node_vec, edge_weight, edge_attr_128, L0_gnn_w_time, L0_gnn_b_time, L0_gnn_W_q, L0_gnn_b_q, L0_gnn_W_k, L0_gnn_b_k, L0_gnn_W_v, L0_gnn_b_v, L0_gnn_W_e, L0_gnn_W_skip, L0_gnn_b_skip, edge_index), axis=-1)
    x = _layernorm(x + _L1_gnn_ref(x, L1_gnn_W1, L1_gnn_b1, L1_gnn_Wr1, L1_gnn_br1, L1_gnn_W2, L1_gnn_b2, L1_gnn_Wr2, L1_gnn_br2, L1_gnn_W3, L1_gnn_b3, edge_index), axis=-1)
    x = _layernorm(x + _L2_gnn_ref(x, edge_attr_128, src, dst, L2_gnn_W1_0, L2_gnn_W2_0, L2_gnn_W3_0, L2_gnn_W1_1, L2_gnn_W2_1, L2_gnn_W3_1), axis=-1)
    x = _layernorm(x + _L3_gnn_ref(x, edge_attr_2, src, dst, L3_gnn_w_edge, L3_gnn_w_attn, L3_gnn_w_e2n), axis=-1)
    return x

_drawn_inputs = setup_inputs


def setup_inputs(seed=0):
    import zlib

    import numpy as np

    out = dict(_drawn_inputs(seed))
    spreads = {'L0_gnn_b_q': (0.0, 0.8),
     'L0_gnn_b_k': (0.0, 0.8),
     'L0_gnn_b_v': (0.0, 0.419),
     'L0_gnn_b_skip': (0.0, 0.1)}
    factors = {'L0_gnn_b_time': 4.863,
     'L1_gnn_W1': 2.833,
     'L1_gnn_b1': 8.0,
     'L1_gnn_br1': 7.296,
     'L1_gnn_W2': 2.755,
     'L1_gnn_b2': 8.0,
     'L1_gnn_br2': 4.496}
    for name, (base, spread) in spreads.items():
        noise = np.random.default_rng([zlib.crc32(name.encode()), seed]).standard_normal(out[name].shape)
        drawn = base * np.exp(spread * noise) if base else spread * noise
        out[name] = jnp.asarray(drawn.astype(out[name].dtype))
    for name, factor in factors.items():
        out[name] = (out[name] * factor).astype(out[name].dtype)
    return out
```

```python
from contextlib import ExitStack

import numpy as np

import concourse.bass as bass
from concourse import mybir

F32 = mybir.dt.float32
BF16 = mybir.dt.bfloat16
I32 = mybir.dt.int32
ALU = mybir.AluOpType
ACT = mybir.ActivationFunctionType
AX = mybir.AxisListType

N = 50000
E = 25000
D = 128
P = 128
TILES = 200
SLOTS = TILES * P
K = 4
GROUPS = TILES // K
PAIRS = GROUPS // 2
G = K * P
LOAD_P = E // TILES
HI = (N + P) // P
TABLE = HI * P
REC = 8
ROW = D + REC
NONE = SLOTS
FAR = 1 << 20
EPS = 1e-5
SLOPE = (1.0 / 8.0 + 1.0 / 3.0) / 2.0
BIG = 1e38
TWO_PI_HI = 6.28125
TWO_PI_LO = float(2 * np.pi - 6.28125)
ROUND = 12582912.0
PI_IN = 3.1415925


class Signal:

    def __init__(self, nc, ctx, name, step=1):
        self.sem = ctx.enter_context(nc.semaphore(name))
        self.step, self.base = step, 0

    def at(self, events):
        return events * self.step + self.base

    def spent(self, events):
        self.base += events * self.step


def comes(events):
    return not (isinstance(events, int) and events <= 0)


class Steps:

    def __init__(self, nc, ctx, name):
        self.sem = ctx.enter_context(nc.semaphore(name))
        self.base, self.i, self.j, self.per = 0, 0, 0, 0

    def begin(self, i):
        self.i, self.j = i, 0

    def one(self):
        self.j += 1
        return self.sem

    def so_far(self):
        if isinstance(self.i, int) and self.i == 0:
            return self.base + self.j
        return self.i * self.per + (self.base + self.j)

    def end(self, rounds):
        self.base += rounds * self.per if rounds else self.j
        self.i, self.j = 0, 0


def pairs(eng, steps, body, rounds=PAIRS):
    if steps:
        steps.begin(0)
    body(0)
    if steps:
        steps.per = steps.j
    with eng.Fori(1, rounds - 1) as i:
        if steps:
            steps.begin(i)
        body(i)
    if steps:
        assert steps.j == steps.per
        steps.begin(rounds - 1)
    body(rounds - 1)
    if steps:
        steps.end(rounds)


def graph_kernel(nc, a, out):
    ctx = ExitStack()
    with ctx:
        def sb(name, shape, dt=F32, c=ctx):
            return c.enter_context(nc.sbuf_tensor(name, shape, dt))

        def dram(name, shape, dt=F32):
            return nc.dram_tensor(name, shape, dt, kind="Internal").ap()

        def signal(name, step=1):
            return Signal(nc, ctx, name, step)

        rows_d = dram("rows_d", [SLOTS, ROW])
        table_d = dram("table_d", [TABLE, 4])
        same_d = dram("same_d", [GROUPS, P, G])
        carry_d = dram("carry_d", [GROUPS, G])
        node_d = dram("node_d", [1, SLOTS + 2])
        val_d = dram("val_d", [2, SLOTS])
        seg_d = dram("seg_d", [2, SLOTS])
        v_d = dram("v_d", [SLOTS, D])
        xbd_d = dram("xbd_d", [SLOTS, D])
        xbs_d = dram("xbs_d", [SLOTS, D])
        x1d_d = dram("x1d_d", [SLOTS, D])
        x1s_d = dram("x1s_d", [SLOTS, D])
        x1g_d = dram("x1g_d", [SLOTS, D])
        agg1_d = dram("agg1_d", [SLOTS + 8, D])
        agg2_d = dram("agg2_d", [SLOTS + 8, D])
        h1_d = dram("h1_d", [SLOTS, D])
        x2d_d = dram("x2d_d", [SLOTS, D])
        x2s_d = dram("x2s_d", [SLOTS, D])
        x2g_d = dram("x2g_d", [SLOTS, D])
        g1d_d = dram("g1d_d", [SLOTS, D])
        g1s_d = dram("g1s_d", [SLOTS, D])
        x3d_d = dram("x3d_d", [SLOTS, D])
        za_d = dram("za_d", [SLOTS, 2])

        ident = sb("ident", [P, P])
        ident_b = sb("ident_b", [P, P], BF16)
        ones = sb("ones", [P, P])
        below = sb("below", [P, P])
        upto = sb("upto", [P, P])
        above = sb("above", [P, P])
        last_lane = sb("last_lane", [P, P])
        recs = sb("recs", [P, TILES, REC])
        dst_next = sb("dst_next", [P, TILES + 1])
        src_tab = sb("src_tab", [P, TILES, 4])
        src_id = sb("src_id", [P, TILES], I32)
        dst_id = sb("dst_id", [P, TILES], I32)
        src_row = sb("src_row", [P, TILES], I32)
        out_row = sb("out_row", [P, TILES], I32)
        ns = sb("ns", [P, TILES])
        nd = sb("nd", [P, TILES])
        inv_deg = sb("inv_deg", [P, TILES])
        alpha = sb("alpha", [P, 2, TILES])
        segmax = sb("segmax", [P, 2, TILES])

        steps_v = Steps(nc, ctx, "vector_steps")
        steps_a = Steps(nc, ctx, "scalar_steps")
        steps_g = Steps(nc, ctx, "pool_steps")
        issued = ctx.enter_context(nc.semaphore("pool_issue"))
        consts = signal("consts")
        once_in = signal("once_in", 16)
        once_out = signal("once_out", 16)
        rows_in = [signal(f"rows_in{h}", 16) for h in range(2)]
        gathered = [signal(f"gathered{h}", 16) for h in range(2)]
        scattered = [signal(f"scattered{h}", 16) for h in range(2)]
        stored = [signal(f"stored{h}", 16) for h in range(2)]
        inputs_read = signal("inputs_read")
        pe_read = signal("pe_read")
        results = signal("results")

        with nc.Block() as block:
            @block.gpsimd
            def _(pool):
                for m in (ident, ident_b, last_lane):
                    pool.memset(m[:, :], 0.0).then_inc(steps_g.one(), 1)
                for m in (ones, below, upto, above):
                    pool.memset(m[:, :], 1.0).then_inc(steps_g.one(), 1)
                pool.wait_ge(steps_g.sem, steps_g.so_far())
                for m in (ident, ident_b):
                    pool.affine_select(out=m[:, :], in_=m[:, :], compare_op=ALU.not_equal, fill=1.0,
                                                   base=0, pattern=[[-1, P]], channel_multiplier=1).then_inc(steps_g.one(), 1)
                pool.affine_select(out=below[:, :], in_=below[:, :], compare_op=ALU.is_gt, fill=0.0,
                                               base=0, pattern=[[-1, P]], channel_multiplier=1).then_inc(steps_g.one(), 1)
                pool.affine_select(out=upto[:, :], in_=upto[:, :], compare_op=ALU.is_ge, fill=0.0,
                                               base=0, pattern=[[-1, P]], channel_multiplier=1).then_inc(steps_g.one(), 1)
                pool.affine_select(out=above[:, :], in_=above[:, :], compare_op=ALU.is_gt, fill=0.0,
                                               base=0, pattern=[[1, P]], channel_multiplier=-1).then_inc(steps_g.one(), 1)
                pool.affine_select(out=last_lane[:, :], in_=last_lane[:, :], compare_op=ALU.not_equal,
                                               fill=1.0, base=-(P - 1), pattern=[[0, P]], channel_multiplier=1).then_inc(steps_g.one(), 1)
                pool.wait_ge(steps_g.sem, steps_g.so_far())
                steps_g.end(0)

        with ExitStack() as st:
            given = sb("given", [P, TILES, REC], F32, st)
            node_i = sb("node_i", [P, 2, TILES], I32, st)
            part_i = sb("part_i", [P, 4, TILES], I32, st)
            part_f = sb("part_f", [P, 4, TILES], F32, st)
            lanes_i = sb("lanes_i", [P, HI], I32, st)
            lanes = sb("lanes", [P, HI], F32, st)
            ew = sb("ew", [P, TILES], F32, st)
            e2 = sb("e2", [P, TILES, 2], F32, st)
            count = sb("count", [P, 2, HI], F32, st)
            start = sb("start", [P, HI], F32, st)
            cols = sb("cols", [P, 4, 8], F32, st)
            hot_lo = sb("hot_lo", [P, 8, 2, P], BF16, st)
            hot_hi = sb("hot_hi", [P, 8, 2, HI + 1], BF16, st)
            hot_ready = signal("hot_ready")
            hot_used = signal("hot_used")
            counted = signal("counted")
            added = signal("added")

            ps = ExitStack()
            with ps, nc.Block() as block:
                c_ps = [ps.enter_context(nc.psum_tensor(f"c_ps{s}", [P, 512], F32)) for s in range(2)]

                @block.sync
                def _(sp):
                    sp.wait_ge(consts.sem, consts.at(1))
                    sp.dma_start(node_i[0:LOAD_P, 0, :], a["dst"].rearrange("(p t) -> p t", t=TILES)).then_inc(once_in.sem, 16)
                    sp.dma_start(node_i[0:LOAD_P, 1, :], a["src"].rearrange("(p t) -> p t", t=TILES)).then_inc(once_in.sem, 16)
                    sp.dma_start(ew[0:LOAD_P, :], a["edge_weight"].rearrange("(p t) -> p t", t=TILES)).then_inc(once_in.sem, 16)
                    sp.dma_start(e2[0:LOAD_P, :, :], a["edge_attr_2"].rearrange("(p t) c -> p t c", t=TILES)).then_inc(once_in.sem, 16)

                @block.gpsimd
                def _(pool):
                    pool.iota(lanes_i[:, :], pattern=[[1, HI]], base=0, channel_multiplier=0).then_inc(steps_g.one(), 1)
                    pool.wait_ge(steps_g.sem, steps_g.so_far())
                    steps_g.end(0)

                @block.vector
                def _(dve):
                    dve.memset(node_i[:, :, :], N).then_inc(steps_v.one(), 1)
                    dve.memset(ew[:, :], 0.0).then_inc(steps_v.one(), 1)
                    dve.memset(e2[:, :, :], 0.0).then_inc(steps_v.one(), 1)
                    dve.memset(given[:, :, :], 0.0).then_inc(steps_v.one(), 1)
                    dve.wait_ge(steps_v.sem, steps_v.so_far())
                    dve.memset(count[:, :, :], 0.0).then_inc(consts.sem, 1)
                    dve.wait_ge(once_in.sem, once_in.at(4))
                    for s in range(2):
                        dve.tensor_single_scalar(part_i[:, 2 * s, :], node_i[:, s, :], P - 1, ALU.bitwise_and).then_inc(steps_v.one(), 1)
                        dve.tensor_single_scalar(part_i[:, 2 * s + 1, :], node_i[:, s, :], 7, ALU.logical_shift_right).then_inc(steps_v.one(), 1)
                    dve.wait_ge(steps_g.sem, steps_g.base)
                    dve.tensor_copy(lanes[:, :], lanes_i[:, :]).then_inc(steps_v.one(), 1)
                    dve.tensor_copy(given[:, :, 0], node_i[:, 1, :]).then_inc(steps_v.one(), 1)
                    dve.tensor_copy(given[:, :, 1], node_i[:, 0, :]).then_inc(steps_v.one(), 1)
                    dve.tensor_copy(given[:, :, 2], ew[:, :]).then_inc(steps_v.one(), 1)
                    dve.tensor_copy(given[:, :, 3:5], e2[:, :, :]).then_inc(steps_v.one(), 1)
                    dve.wait_ge(steps_v.sem, steps_v.so_far())
                    dve.tensor_copy(part_f[:, :, :], part_i[:, :, :]).then_inc(steps_v.one(), 1)
                    dve.wait_ge(steps_v.sem, steps_v.so_far())
                    steps_v.end(0)

                    def body(i):
                        if comes(i * 8):
                            dve.wait_ge(hot_used.sem, hot_used.at(i * 8))
                        dve.tensor_scalar(cols[:, :, :], part_f[:, :, bass.ds(i * 8, 8)], 0.0, None, ALU.add).then_inc(steps_v.one(), 1)
                        dve.wait_ge(steps_v.sem, steps_v.so_far())
                        for k in range(8):
                            for s in range(2):
                                dve.tensor_scalar(hot_lo[:, k, s, :], lanes[:, 0:P], cols[:, 2 * s, k:k + 1], None, ALU.is_equal)
                                hot = dve.tensor_scalar(hot_hi[:, k, s, 0:HI], lanes[:, :], cols[:, 2 * s + 1, k:k + 1], None, ALU.is_equal)
                                hot.then_inc(hot_ready.sem, 1)
                        dve.wait_ge(hot_used.sem, hot_used.at(i * 8 + 8))
                        for s in range(2):
                            dve.tensor_tensor(count[:, s, :], count[:, s, :], c_ps[s][:, 0:HI], ALU.add).then_inc(steps_v.one(), 1)
                        dve.wait_ge(steps_v.sem, steps_v.so_far())
                        dve.sem_inc(added.sem, 1)
                    pairs(dve, steps_v, body)

                @block.tensor
                def _(pe):
                    def body(i):
                        if comes(i):
                            pe.wait_ge(added.sem, added.at(i))
                        for k in range(8):
                            pe.wait_ge(hot_ready.sem, hot_ready.at(i * 16 + 2 * k + 2))
                            for s in range(2):
                                mm = pe.matmul(c_ps[s][:, 0:HI], hot_lo[:, k, s, :], hot_hi[:, k, s, 0:HI],
                                               start=(k == 0), stop=(k == 7))
                            mm.then_inc(hot_used.sem, 1)
                    pairs(pe, None, body)
            for s, n in ((consts, 1), (once_in, 4), (hot_ready, 2 * TILES), (hot_used, TILES), (added, PAIRS)):
                s.spent(n)

            total = sb("total", [P, HI], F32, st)
            upto_hi = sb("upto_hi", [P, HI], F32, st)
            ones_hi = sb("ones_hi", [P, HI], F32, st)
            place_i = sb("place_i", [P, HI], I32, st)
            tile_f = sb("tile_f", [P, HI], F32, st)
            head = sb("head", [P, HI], F32, st)
            has = sb("has", [P, HI], F32, st)
            vec = sb("vec", [P, 4, P], F32, st)
            tab = sb("tab", [P, 4, P, 4], F32, st)
            CH = [(c, min(P, HI - c * P)) for c in range(4)]
            FULL = (N // P) - 3 * P
            turned = signal("turned")
            turned_out = signal("turned_out")
            ps = ExitStack()
            with ps, nc.Block() as block:
                tot_ps = ps.enter_context(nc.psum_tensor("tot_ps", [P, 512], F32))
                pre_ps = ps.enter_context(nc.psum_tensor("pre_ps", [P, 512], F32))
                tr_ps = [ps.enter_context(nc.psum_tensor(f"tr_ps{s}", [P, 512], F32)) for s in range(3)]

                @block.sync
                def _(sp):
                    sp.wait_ge(consts.sem, consts.at(1))
                    sp.dma_start(vec[:, 0:3, :], a["node_vec"][0:3 * P * P].rearrange("(c p l) -> p c l", c=3, l=P)).then_inc(once_in.sem, 16)
                    sp.dma_start(vec[0:FULL, 3, :], a["node_vec"][3 * P * P:(3 * P + FULL) * P].rearrange("(p l) -> p l", l=P)).then_inc(once_in.sem, 16)
                    sp.dma_start(vec[FULL:FULL + 1, 3, 0:N % P], a["node_vec"][(3 * P + FULL) * P:N].rearrange("(p l) -> p l", p=1)).then_inc(once_in.sem, 16)
                    sp.wait_ge(results.sem, results.at(1))
                    for c, w in CH:
                        sp.dma_start(table_d[c * P * P:(c * P + w) * P, :].rearrange("(p l) f -> p (l f)", l=P),
                                     tab[0:w, c, :, :].rearrange("p l f -> p (l f)")).then_inc(once_out.sem, 16)
                    sp.wait_ge(once_out.sem, once_out.at(4))

                @block.tensor
                def _(pe):
                    pe.matmul(tot_ps[:, 0:HI], ones[:, :], count[:, 0, :], start=True, stop=True)
                    pe.matmul(pre_ps[:, 0:HI], above[:, :], count[:, 0, :], start=True, stop=True).then_inc(turned.sem, 1)
                    pe.wait_ge(turned_out.sem, turned_out.at(1))
                    for s, m in enumerate((head[:, :], count[:, 0, :], count[:, 1, :])):
                        for c, w in CH:
                            mm = pe.transpose(tr_ps[s][0:w, c * P:(c + 1) * P], m[:, c * P:c * P + w], ident[:, :])
                        mm.then_inc(turned.sem, 1)

                @block.vector
                def _(dve):
                    dve.memset(vec[:, :, :], 0.0).then_inc(steps_v.one(), 1)
                    dve.memset(ones_hi[:, :], 1.0).then_inc(steps_v.one(), 1)
                    dve.wait_ge(steps_v.sem, steps_v.so_far())
                    dve.sem_inc(consts.sem, 1)
                    dve.wait_ge(turned.sem, turned.at(1))
                    dve.tensor_copy(total[:, :], tot_ps[:, 0:HI]).then_inc(steps_v.one(), 1)
                    dve.wait_ge(steps_v.sem, steps_v.so_far())
                    dve.tensor_tensor_scan(upto_hi[:, :], total[:, :], ones_hi[:, :], 0.0, ALU.add, ALU.mult).then_inc(steps_v.one(), 1)
                    dve.wait_ge(steps_v.sem, steps_v.so_far())
                    dve.tensor_tensor(start[:, :], upto_hi[:, :], total[:, :], ALU.subtract).then_inc(steps_v.one(), 1)
                    dve.wait_ge(steps_v.sem, steps_v.so_far())
                    dve.tensor_tensor(start[:, :], start[:, :], pre_ps[:, 0:HI], ALU.add).then_inc(steps_v.one(), 1)
                    dve.wait_ge(steps_v.sem, steps_v.so_far())
                    dve.tensor_copy(place_i[:, :], start[:, :]).then_inc(steps_v.one(), 1)
                    dve.wait_ge(steps_v.sem, steps_v.so_far())
                    dve.tensor_single_scalar(place_i[:, :], place_i[:, :], 7, ALU.logical_shift_right).then_inc(steps_v.one(), 1)
                    dve.wait_ge(steps_v.sem, steps_v.so_far())
                    dve.tensor_copy(tile_f[:, :], place_i[:, :]).then_inc(steps_v.one(), 1)
                    dve.tensor_scalar(has[:, :], count[:, 0, :], 0.5, None, ALU.is_ge).then_inc(steps_v.one(), 1)
                    dve.wait_ge(steps_v.sem, steps_v.so_far())
                    dve.scalar_tensor_tensor(head[:, :], tile_f[:, :], -2.0 * P, start[:, :], ALU.mult, ALU.add).then_inc(steps_v.one(), 1)
                    dve.wait_ge(steps_v.sem, steps_v.so_far())
                    dve.tensor_scalar(head[:, :], head[:, :], float((TILES - 1) * P - NONE), None, ALU.add).then_inc(steps_v.one(), 1)
                    dve.wait_ge(steps_v.sem, steps_v.so_far())
                    dve.tensor_tensor(head[:, :], head[:, :], has[:, :], ALU.mult).then_inc(steps_v.one(), 1)
                    dve.wait_ge(steps_v.sem, steps_v.so_far())
                    dve.tensor_scalar(head[:, :], head[:, :], float(NONE), None, ALU.add).then_inc(turned_out.sem, 1)
                    dve.wait_ge(once_in.sem, once_in.at(3))
                    dve.tensor_copy(tab[:, :, :, 3], vec[:, :, :])
                    for s in range(3):
                        dve.wait_ge(turned.sem, turned.at(2 + s))
                        for c, w in CH:
                            dve.tensor_copy(tab[0:w, c, :, s], tr_ps[s][0:w, c * P:(c + 1) * P]).then_inc(steps_v.one(), 1)
                    dve.wait_ge(steps_v.sem, steps_v.so_far())
                    dve.sem_inc(results.sem, 1)
                    steps_v.end(0)
            for s, n in ((consts, 1), (once_in, 3), (once_out, 4), (turned, 4), (turned_out, 1), (results, 1)):
                s.spent(n)

            row = sb("row", [P, 2, K, ROW], F32, st)
            lo_t = sb("lo_t", [P, 2, P], F32, st)
            run = sb("run", [P, 2, HI], F32, st)
            junk = sb("junk", [P, HI], F32, st)
            junk_r = sb("junk_r", [P, P], F32, st)
            colk = sb("colk", [P, 2, 3, K], F32, st)
            colb = sb("colb", [P, 2, K, P], F32, st)
            base = sb("base", [P, 2, K], F32, st)
            rank = sb("rank", [P, 2, K], F32, st)
            place = sb("place", [P, 2, K], F32, st)
            tile_i = sb("tile_i", [P, 2, K], I32, st)
            tile_k = sb("tile_k", [P, 2, K], F32, st)
            slot_i = sb("slot_i", [P, 2, K], I32, st)
            hot_t = signal("hot_t")
            run_sb = signal("run_sb")
            based = signal("based")
            base_read = signal("base_read")
            along = signal("along")
            ps = ExitStack()
            with ps, nc.Block() as block:
                t_ps = [ps.enter_context(nc.psum_tensor(f"t_ps{s}", [P, 1024], BF16)) for s in range(2)]
                r_ps = [ps.enter_context(nc.psum_tensor(f"r_ps{s}", [P, 512], F32)) for s in range(2)]
                a_ps = [ps.enter_context(nc.psum_tensor(f"a_ps{s}", [P, 512], F32)) for s in range(2)]
                run_ps = ps.enter_context(nc.psum_tensor("run_ps", [P, 512], F32))
                msg_v = a["edge_attr_128"].rearrange("(p t) d -> p t d", t=TILES)

                @block.sync
                def _(sp):
                    sp.wait_ge(consts.sem, consts.at(1))

                    def body(i):
                        for h in range(2):
                            if comes(i * K):
                                sp.wait_ge(scattered[h].sem, scattered[h].at(i * K))
                            sp.sem_inc(issued, 1)
                            sp.dma_start(row[0:LOAD_P, h, :, 0:D], msg_v[:, bass.ds(i * 2 * K + h * K, K), :]).then_inc(rows_in[h].sem, 16)
                    pairs(sp, None, body)

                @block.gpsimd
                def _(pool):
                    def body(i):
                        for h in range(2):
                            pool.wait_ge(results.sem, results.at(i * 2 + h + 1))
                            pool.wait_ge(rows_in[h].sem, rows_in[h].at(i + 1))
                            pool.sem_inc(issued, 1)
                            for k in range(K):
                                pool.indirect_dma_start(
                                    out=rows_d[:, :], out_offset=bass.IndirectOffsetOnAxis(ap=slot_i[:, h, k:k + 1], axis=0),
                                    in_=row[:, h, k, :], in_offset=None,
                                    bounds_check=SLOTS - 1, oob_is_err=False).then_inc(scattered[h].sem, 16)
                    pairs(pool, None, body)
                    for h in range(2):
                        pool.wait_ge(scattered[h].sem, scattered[h].at(PAIRS * K))

                @block.vector
                def _(dve):
                    dve.memset(row[:, :, :, :], 0.0).then_inc(steps_v.one(), 1)
                    dve.wait_ge(steps_v.sem, steps_v.so_far())
                    dve.sem_inc(consts.sem, 1)
                    steps_v.end(0)

                    def body(i):
                        for h in range(2):
                            if comes((i * 2 + h) * K - K):
                                dve.wait_ge(hot_used.sem, hot_used.at((i * 2 + h) * K - K))
                            dve.tensor_scalar(colk[:, h, 0, :], given[:, bass.ds(i * 2 * K + h * K, K), 1], 0.0, None, ALU.add).then_inc(steps_v.one(), 1)
                            dve.tensor_scalar(colk[:, h, 1:3, :], part_f[:, 0:2, bass.ds(i * 2 * K + h * K, K)], 0.0, None, ALU.add).then_inc(steps_v.one(), 1)
                            dve.wait_ge(steps_v.sem, steps_v.so_far())
                            dve.tensor_copy(colb[:, h, :, :], colk[:, h, 0, :].unsqueeze(2).to_broadcast([P, K, P])).then_inc(steps_v.one(), 1)
                            for k in range(K):
                                dve.tensor_scalar(hot_lo[:, 4 * h + k, 0, :], lanes[:, 0:P], colk[:, h, 1, k:k + 1], None, ALU.is_equal).then_inc(steps_v.one(), 1)
                                dve.tensor_scalar(hot_hi[:, 4 * h + k, 0, 0:HI], lanes[:, :], colk[:, h, 2, k:k + 1], None, ALU.is_equal).then_inc(hot_ready.sem, 1)
                            for k in range(K):
                                dve.wait_ge(along.sem, along.at((i * 2 + h) * K + k + 1))
                                dve.scalar_tensor_tensor(junk_r[:, :], r_ps[k % 2][:, 0:P], colk[:, h, 0, k:k + 1], below[:, :],
                                                                     ALU.is_equal, ALU.mult, accum_out=rank[:, h, k:k + 1]).then_inc(steps_v.one(), 1)
                                dve.wait_ge(based.sem, based.at((i * 2 + h) * K + k + 1))
                                dve.tensor_tensor_reduce(out=junk[:, :], in0=a_ps[k % 2][:, 0:HI], in1=hot_hi[:, 4 * h + k, 0, 0:HI],
                                                                     scale=1.0, scalar=0.0, op0=ALU.mult, op1=ALU.add,
                                                                     accum_out=base[:, h, k:k + 1]).then_inc(steps_v.one(), 1)
                                dve.wait_ge(steps_v.sem, steps_v.so_far())
                                dve.sem_inc(base_read.sem, 1)
                            dve.tensor_tensor(place[:, h, :], base[:, h, :], rank[:, h, :], ALU.add).then_inc(steps_v.one(), 1)
                            dve.wait_ge(steps_v.sem, steps_v.so_far())
                            dve.tensor_copy(tile_i[:, h, :], place[:, h, :]).then_inc(steps_v.one(), 1)
                            dve.wait_ge(steps_v.sem, steps_v.so_far())
                            dve.tensor_single_scalar(tile_i[:, h, :], tile_i[:, h, :], 7, ALU.logical_shift_right).then_inc(steps_v.one(), 1)
                            dve.wait_ge(steps_v.sem, steps_v.so_far())
                            dve.tensor_copy(tile_k[:, h, :], tile_i[:, h, :]).then_inc(steps_v.one(), 1)
                            dve.wait_ge(steps_v.sem, steps_v.so_far())
                            dve.scalar_tensor_tensor(place[:, h, :], tile_k[:, h, :], -2.0 * P, place[:, h, :], ALU.mult, ALU.add).then_inc(steps_v.one(), 1)
                            dve.wait_ge(steps_v.sem, steps_v.so_far())
                            if comes(i * K):
                                dve.wait_ge(scattered[h].sem, scattered[h].at(i * K))
                            dve.tensor_scalar(slot_i[:, h, :], place[:, h, :], float((TILES - 1) * P), None, ALU.add).then_inc(steps_v.one(), 1)
                            dve.tensor_scalar(row[:, h, :, D:ROW], given[:, bass.ds(i * 2 * K + h * K, K), :], 0.0, None, ALU.add).then_inc(steps_v.one(), 1)
                            dve.wait_ge(steps_v.sem, steps_v.so_far())
                            dve.sem_inc(results.sem, 1)
                    pairs(dve, steps_v, body)

                @block.tensor
                def _(pe):
                    pe.matmul(run_ps[:, 0:HI], ident[:, :], start[:, :], start=True, stop=True, skip_group_check=True).then_inc(turned.sem, 1)

                    def body(i):
                        for h in range(2):
                            for k in range(K):
                                n = (i * 2 + h) * K + k
                                pe.wait_ge(hot_ready.sem, hot_ready.at(n + 1))
                                if comes(n - 1):
                                    pe.wait_ge(base_read.sem, base_read.at(n - 1))
                                pe.transpose(t_ps[k % 2][:, 0:P], hot_lo[:, 4 * h + k, 0, :], ident_b[:, :]).then_inc(hot_t.sem, 1)
                                pe.matmul(r_ps[k % 2][:, 0:P], colb[:, h, k, :], ident[:, :], start=True, stop=True).then_inc(along.sem, 1)
                                pe.wait_ge(run_sb.sem, run_sb.at(n + 1))
                                pe.matmul(a_ps[k % 2][:, 0:HI], lo_t[:, k % 2, :], run[:, k % 2, :], start=True, stop=True).then_inc(based.sem, 1)
                                pe.matmul(run_ps[:, 0:HI], hot_lo[:, 4 * h + k, 0, :], hot_hi[:, 4 * h + k, 0, 0:HI],
                                          start=False, stop=True, skip_group_check=True).then_inc(hot_used.sem, 1)
                    pairs(pe, None, body)

                @block.scalar
                def _(act):
                    act.wait_ge(turned.sem, turned.at(1))

                    def body(i):
                        for h in range(2):
                            for k in range(K):
                                n = (i * 2 + h) * K + k
                                if comes(n - 1):
                                    act.wait_ge(based.sem, based.at(n - 1))
                                act.wait_ge(hot_t.sem, hot_t.at(n + 1))
                                act.copy(lo_t[:, k % 2, :], t_ps[k % 2][:, 0:P]).then_inc(steps_a.one(), 1)
                                if comes(n):
                                    act.wait_ge(hot_used.sem, hot_used.at(n))
                                act.copy(run[:, k % 2, :], run_ps[:, 0:HI]).then_inc(steps_a.one(), 1)
                                act.wait_ge(steps_a.sem, steps_a.so_far())
                                act.sem_inc(run_sb.sem, 1)
                    pairs(act, steps_a, body)
            for s, n in ((consts, 1), (rows_in[0], PAIRS), (rows_in[1], PAIRS), (scattered[0], PAIRS * K), (scattered[1], PAIRS * K),
                         (results, GROUPS), (hot_ready, TILES), (hot_used, TILES), (along, TILES), (based, TILES), (base_read, TILES),
                         (turned, 1), (hot_t, TILES), (run_sb, TILES)):
                s.spent(n)

        with ExitStack() as st:
            heads = sb("heads", [P, TILES], F32, st)
            last_dst = sb("last_dst", [P, TILES], F32, st)
            tabk = sb("tabk", [P, 2, K, 4], F32, st)
            idx = sb("idx", [P, 2, K], I32, st)
            dcol = sb("dcol", [P, 2, K], F32, st)
            dbef = sb("dbef", [P, 2, K], F32, st)
            drow = sb("drow", [P, 2, K, P], F32, st)
            same = sb("same", [P, 2, K, P], F32, st)
            carry = sb("carry", [1, 2, K, P], F32, st)
            eqs = sb("eqs", [P, 2, K], F32, st)
            slots_known = signal("slots_known")
            along4 = signal("along4")
            ps = ExitStack()
            with ps, nc.Block() as block:
                l_ps = ps.enter_context(nc.psum_tensor("l_ps", [P, 512], F32))
                e_ps = [ps.enter_context(nc.psum_tensor(f"e_ps{s}", [P, 512], F32)) for s in range(2)]

                @block.sync
                def _(sp):
                    sp.dma_start(recs[:, :, :], rows_d[:, D:ROW].rearrange("(t p) f -> p t f", p=P)).then_inc(once_in.sem, 16)

                    def body(i):
                        for h in range(2):
                            sp.wait_ge(results.sem, results.at(i * 2 + h + 1))
                            sp.sem_inc(issued, 1)
                            sp.dma_start(same_d[bass.ds(i * 2 + h, 1), :, :].rearrange("g p m -> p (g m)"),
                                         same[:, h, :, :].rearrange("p k m -> p (k m)")).then_inc(stored[h].sem, 16)
                            sp.dma_start(carry_d[bass.ds(i * 2 + h, 1), :],
                                         carry[0:1, h, :, :].rearrange("p k m -> p (k m)")).then_inc(stored[h].sem, 16)
                    pairs(sp, None, body)
                    for h in range(2):
                        sp.wait_ge(stored[h].sem, stored[h].at(2 * PAIRS))

                @block.gpsimd
                def _(pool):
                    pool.wait_ge(slots_known.sem, slots_known.at(1))

                    def body(i):
                        for h in range(2):
                            if comes(i * K):
                                pool.wait_ge(gathered[h].sem, gathered[h].at(i * K))
                            if comes(i * 2 + h - 1):
                                pool.wait_ge(inputs_read.sem, inputs_read.at(i * 2 + h - 1))
                            pool.sem_inc(issued, 1)
                            pool.tensor_copy(idx[:, h, :], src_id[:, bass.ds(i * 2 * K + h * K, K)]).then_inc(steps_g.one(), 1)
                            pool.wait_ge(steps_g.sem, steps_g.so_far())
                            pool.sem_inc(issued, 1)
                            for k in range(K):
                                pool.indirect_dma_start(
                                    out=tabk[:, h, k, :], out_offset=None, in_=table_d[:, :],
                                    in_offset=bass.IndirectOffsetOnAxis(ap=idx[:, h, k:k + 1], axis=0),
                                    bounds_check=TABLE - 1, oob_is_err=False).then_inc(gathered[h].sem, 16)
                    pairs(pool, steps_g, body)

                @block.vector
                def _(dve):
                    dve.wait_ge(once_in.sem, once_in.at(1))
                    dve.memset(dst_next[:, 0:1], -1.0).then_inc(steps_v.one(), 1)
                    dve.tensor_copy(dst_next[:, 1:TILES + 1], recs[:, :, 1]).then_inc(steps_v.one(), 1)
                    dve.tensor_copy(src_id[:, :], recs[:, :, 0]).then_inc(steps_v.one(), 1)
                    dve.tensor_copy(dst_id[:, :], recs[:, :, 1]).then_inc(steps_v.one(), 1)
                    dve.wait_ge(steps_v.sem, steps_v.so_far())
                    dve.sem_inc(slots_known.sem, 1)
                    steps_v.end(0)

                    def body(i):
                        for h in range(2):
                            n = i * 2 + h
                            if comes(n - 1):
                                dve.wait_ge(along4.sem, along4.at(n - 1))
                            dve.tensor_scalar(dcol[:, h, :], dst_next[:, bass.ds(n * K + 1, K)], 0.0, None, ALU.add).then_inc(steps_v.one(), 1)
                            dve.tensor_scalar(dbef[:, h, :], dst_next[:, bass.ds(n * K, K)], 0.0, None, ALU.add).then_inc(steps_v.one(), 1)
                            dve.wait_ge(steps_v.sem, steps_v.so_far())
                            dve.tensor_copy(drow[:, h, :, :], dcol[:, h, :].unsqueeze(2).to_broadcast([P, K, P])).then_inc(hot_ready.sem, 1)
                            if comes(2 * i):
                                dve.wait_ge(stored[h].sem, stored[h].at(2 * i))
                            dve.wait_ge(along4.sem, along4.at(n + 1))
                            for k in range(K):
                                dve.scalar_tensor_tensor(same[:, h, k, :], e_ps[h][:, k * P:(k + 1) * P], dcol[:, h, k:k + 1], upto[:, :],
                                                                     ALU.is_equal, ALU.mult, accum_out=eqs[:, h, k:k + 1]).then_inc(steps_v.one(), 1)
                                dve.tensor_scalar(carry[0:1, h, k, :], e_ps[h][0:1, k * P:(k + 1) * P], dbef[0:1, h, k:k + 1], None, ALU.is_equal).then_inc(steps_v.one(), 1)
                            dve.wait_ge(steps_v.sem, steps_v.so_far())
                            dve.sem_inc(results.sem, 1)
                            dve.tensor_scalar(heads[:, bass.ds(n * K, K)], eqs[:, h, :], 0.0, None, ALU.add).then_inc(steps_v.one(), 1)
                            dve.wait_ge(gathered[h].sem, gathered[h].at((i + 1) * K))
                            dve.tensor_scalar(src_tab[:, bass.ds(n * K, K), :], tabk[:, h, :, :], 0.0, None, ALU.add).then_inc(inputs_read.sem, 1)
                    pairs(dve, steps_v, body)
                    dve.wait_ge(inputs_read.sem, inputs_read.at(GROUPS))
                    dve.wait_ge(turned.sem, turned.at(1))
                    dve.memset(last_dst[:, TILES - 1:TILES], -1.0).then_inc(steps_v.one(), 1)
                    dve.tensor_copy(last_dst[:, 0:TILES - 1], l_ps[:, 1:TILES]).then_inc(steps_v.one(), 1)
                    dve.tensor_scalar(heads[:, :], heads[:, :], 1.5, None, ALU.is_lt).then_inc(steps_v.one(), 1)
                    dve.wait_ge(steps_v.sem, steps_v.so_far())
                    dve.tensor_tensor(last_dst[:, :], last_dst[:, :], dst_next[:, 1:TILES + 1], ALU.not_equal).then_inc(steps_v.one(), 1)
                    dve.wait_ge(steps_v.sem, steps_v.so_far())
                    dve.tensor_tensor(heads[:, :], heads[:, :], last_dst[:, :], ALU.mult).then_inc(steps_v.one(), 1)
                    dve.wait_ge(steps_v.sem, steps_v.so_far())
                    dve.tensor_scalar(last_dst[:, :], dst_next[:, 1:TILES + 1], -float(FAR), None, ALU.add).then_inc(steps_v.one(), 1)
                    dve.wait_ge(steps_v.sem, steps_v.so_far())
                    dve.tensor_tensor(heads[:, :], heads[:, :], last_dst[:, :], ALU.mult).then_inc(steps_v.one(), 1)
                    dve.wait_ge(steps_v.sem, steps_v.so_far())
                    dve.tensor_scalar(out_row[:, :], heads[:, :], float(FAR), None, ALU.add).then_inc(steps_v.one(), 1)
                    dve.tensor_copy(src_row[:, :], src_tab[:, :, 0]).then_inc(steps_v.one(), 1)
                    dve.wait_ge(turned_out.sem, turned_out.at(1))
                    dve.reciprocal(ns[:, :], ns[:, :]).then_inc(steps_v.one(), 1)
                    dve.wait_ge(steps_v.sem, steps_v.so_far())
                    steps_v.end(0)

                @block.tensor
                def _(pe):
                    pe.wait_ge(slots_known.sem, slots_known.at(1))
                    pe.matmul(l_ps[:, 0:TILES], last_lane[:, :], dst_next[:, 1:TILES + 1], start=True, stop=True).then_inc(turned.sem, 1)

                    def body(i):
                        for h in range(2):
                            if comes(i * 2 + h - 1):
                                pe.wait_ge(results.sem, results.at(i * 2 + h - 1))
                            pe.wait_ge(hot_ready.sem, hot_ready.at(i * 2 + h + 1))
                            for k in range(K):
                                mm = pe.matmul(e_ps[h][:, k * P:(k + 1) * P], drow[:, h, k, :], ident[:, :], start=True, stop=True)
                            mm.then_inc(along4.sem, 1)
                    pairs(pe, None, body)

                @block.scalar
                def _(act):
                    act.wait_ge(inputs_read.sem, inputs_read.at(GROUPS))
                    act.activation(ns[:, :], src_tab[:, :, 2], ACT.Sqrt).then_inc(turned_out.sem, 1)
            for s, n in ((once_in, 1), (results, GROUPS), (stored[0], 2 * PAIRS), (stored[1], 2 * PAIRS), (slots_known, 1),
                         (gathered[0], PAIRS * K), (gathered[1], PAIRS * K), (inputs_read, GROUPS), (along4, GROUPS),
                         (hot_ready, GROUPS), (turned, 1), (turned_out, 1)):
                s.spent(n)

        def tile_rows(table, n, width=D):
            return table[bass.ds(n * G, G), 0:width].rearrange("(k p) d -> p k d", p=P)

        def gather(pool, i, h, jobs, idx, per):
            n = i * 2 + h
            if comes(i * K * per):
                pool.wait_ge(gathered[h].sem, gathered[h].at(i * K * per))
            pool.sem_inc(issued, 1)
            for j, (cols_ap, _, _, _) in enumerate(jobs):
                pool.tensor_copy(idx[:, h, j, :], cols_ap[:, bass.ds(n * K, K)]).then_inc(steps_g.one(), 1)
            pool.wait_ge(steps_g.sem, steps_g.so_far())
            pool.sem_inc(issued, 1)
            for j, (_, table, bound, dest) in enumerate(jobs):
                for k in range(K):
                    pool.indirect_dma_start(
                        out=dest[:, k, :], out_offset=None, in_=table,
                        in_offset=bass.IndirectOffsetOnAxis(ap=idx[:, h, j, k:k + 1], axis=0),
                        bounds_check=bound - 1, oob_is_err=False).then_inc(gathered[h].sem, 16)

        with ExitStack() as st:
            w_kvs = sb("w_kvs", [P, 3 * D], F32, st)
            w_qs = sb("w_qs", [P, 2 * D], F32, st)
            w_msg = sb("w_msg", [P, 2 * D], F32, st)
            w_cos = sb("w_cos", [P, 2 * D], F32, st)
            b_kvs = sb("b_kvs", [P, 3 * D], F32, st)
            b_qs = sb("b_qs", [P, 2 * D], F32, st)
            w_time = sb("w_time", [P, D], F32, st)
            b_time = sb("b_time", [P, K, D], F32, st)
            rel = sb("rel", [P, TILES], F32, st)
            relk = sb("relk", [P, 2, K], F32, st)
            idx = sb("idx2", [P, 2, 2, K], I32, st)
            xs = sb("xs", [P, 2, K, D], F32, st)
            xd = sb("xd", [P, 2, K, D], F32, st)
            msg = sb("msg", [P, 2, K, D], F32, st)
            turn = sb("turn", [P, K, D], F32, st)
            arg = sb("arg", [P, K, D], F32, st)
            whole = sb("whole", [P, K, D], F32, st)
            cosv = sb("cosv", [P, K, D], F32, st)
            xs_t = sb("xs_t", [P, 2, G], F32, st)
            xd_t = sb("xd_t", [P, 2, G], F32, st)
            msg_t = sb("msg_t", [P, 2, G], F32, st)
            cos_t = sb("cos_t", [P, 2, G], F32, st)
            kvs = sb("kvs", [P, 2, K, 3 * D], F32, st)
            qs = sb("qs", [P, 2, K, 2 * D], F32, st)
            prod = sb("prod", [P, K * 2, 64], F32, st)
            dots = sb("dots", [P, K, 2], F32, st)
            scaled = signal("scaled")
            scaled_read = signal("scaled_read")
            arg_ready = signal("arg_ready")
            cos_ready = signal("cos_ready")
            turned4 = signal("turned4")
            turned4_out = signal("turned4_out")
            made = signal("made")
            made_read = signal("made_read")
            ps = ExitStack()
            with ps, nc.Block() as block:
                x_ps = [ps.enter_context(nc.psum_tensor(f"x_ps{s}", [P, 512], F32)) for s in range(4)]
                kv_ps = [ps.enter_context(nc.psum_tensor(f"kv_ps{s}", [P, 512], F32)) for s in range(2)]
                q_ps = [ps.enter_context(nc.psum_tensor(f"q_ps{s}", [P, 512], F32)) for s in range(2)]
                WEIGHTS = [
                    (w_kvs[:, 0:D], a["L0_gnn_W_k"]), (w_kvs[:, D:2 * D], a["L0_gnn_W_v"]), (w_kvs[:, 2 * D:3 * D], a["L0_gnn_W_skip"]),
                    (w_qs[:, 0:D], a["L0_gnn_W_q"]), (w_qs[:, D:2 * D], a["L0_gnn_W_skip"]),
                    (w_msg[:, 0:D], a["L0_gnn_W_e"][0:D, :]), (w_msg[:, D:2 * D], a["L0_gnn_W_e"][0:D, :]),
                    (w_cos[:, 0:D], a["L0_gnn_W_e"][D:2 * D, :]), (w_cos[:, D:2 * D], a["L0_gnn_W_e"][D:2 * D, :]),
                    (b_kvs[:, 0:D], a["L0_gnn_b_k"].partition_broadcast(P)), (b_kvs[:, D:2 * D], a["L0_gnn_b_v"].partition_broadcast(P)),
                    (b_kvs[:, 2 * D:3 * D], a["L0_gnn_b_skip"].partition_broadcast(P)),
                    (b_qs[:, 0:D], a["L0_gnn_b_q"].partition_broadcast(P)), (b_qs[:, D:2 * D], a["L0_gnn_b_skip"].partition_broadcast(P)),
                    (w_time[:, :], a["L0_gnn_w_time"].partition_broadcast(P)),
                ] + [(b_time[:, k, :], a["L0_gnn_b_time"].partition_broadcast(P)) for k in range(K)]

                @block.sync
                def _(sp):
                    for to, w in WEIGHTS:
                        sp.dma_start(to, w).then_inc(once_in.sem, 16)

                    def body(i):
                        for h in range(2):
                            n = i * 2 + h
                            if comes(n - 1):
                                sp.wait_ge(pe_read.sem, pe_read.at(n - 1))
                            sp.sem_inc(issued, 1)
                            sp.dma_start(msg[:, h, :, :], tile_rows(rows_d, n)).then_inc(rows_in[h].sem, 16)
                            if not (isinstance(n, int) and n == 0):
                                store(sp, n - 1, 1 - h)

                    def store(sp, n, h):
                        sp.wait_ge(results.sem, results.at(n + 1))
                        sp.sem_inc(issued, 1)
                        sp.dma_start(tile_rows(v_d, n), kvs[:, h, :, D:2 * D]).then_inc(stored[h].sem, 16)
                        sp.dma_start(tile_rows(xbs_d, n), kvs[:, h, :, 2 * D:3 * D]).then_inc(stored[h].sem, 16)
                        sp.dma_start(tile_rows(xbd_d, n), qs[:, h, :, D:2 * D]).then_inc(stored[h].sem, 16)
                    pairs(sp, None, body)
                    store(sp, GROUPS - 1, 1)
                    for h in range(2):
                        sp.wait_ge(stored[h].sem, stored[h].at(3 * PAIRS))

                @block.gpsimd
                def _(pool):
                    pool.wait_ge(consts.sem, consts.at(1))
                    pool.sem_inc(issued, 1)

                    def body(i):
                        for h in range(2):
                            n = i * 2 + h
                            if comes(n - 1):
                                pool.wait_ge(inputs_read.sem, inputs_read.at(n - 1))
                            if comes(n - 1):
                                pool.wait_ge(pe_read.sem, pe_read.at(n - 1))
                            pool.sem_inc(issued, 1)
                            gather(pool, i, h, [(src_id, a["x"][:, :], N, xs[:, h, :, :]), (dst_id, a["x"][:, :], N, xd[:, h, :, :])], idx, 2)
                    pairs(pool, steps_g, body)

                @block.vector
                def _(dve):
                    dve.memset(xs[:, :, :, :], 0.0).then_inc(steps_v.one(), 1)
                    dve.memset(xd[:, :, :, :], 0.0).then_inc(steps_v.one(), 1)
                    dve.tensor_tensor(rel[:, :], src_tab[:, :, 3], recs[:, :, 2], ALU.subtract).then_inc(steps_v.one(), 1)
                    dve.wait_ge(steps_v.sem, steps_v.so_far())
                    dve.sem_inc(consts.sem, 1)
                    dve.wait_ge(once_in.sem, once_in.at(len(WEIGHTS)))
                    dve.sem_inc(issued, 1)
                    steps_v.end(0)

                    def body(i):
                        for h in range(2):
                            n = i * 2 + h
                            if comes(n - 1):
                                dve.wait_ge(scaled.sem, scaled.at(n - 1))
                            dve.tensor_scalar(relk[:, h, :], rel[:, bass.ds(n * K, K)], 0.0, None, ALU.add).then_inc(arg_ready.sem, 1)
                            dve.wait_ge(scaled.sem, scaled.at(n + 1))
                            dve.tensor_tensor(arg[:, :, :], turn[:, :, :], b_time[:, :, :], ALU.add).then_inc(steps_v.one(), 1)
                            dve.wait_ge(steps_v.sem, steps_v.so_far())
                            dve.tensor_scalar(whole[:, :, :], arg[:, :, :], float(1 / (2 * np.pi)), 0.25, ALU.mult, ALU.add).then_inc(steps_v.one(), 1)
                            dve.wait_ge(steps_v.sem, steps_v.so_far())
                            dve.tensor_scalar(whole[:, :, :], whole[:, :, :], ROUND, ROUND, ALU.add, ALU.subtract).then_inc(steps_v.one(), 1)
                            dve.wait_ge(steps_v.sem, steps_v.so_far())
                            dve.scalar_tensor_tensor(arg[:, :, :], whole[:, :, :], -TWO_PI_HI, arg[:, :, :], ALU.mult, ALU.add).then_inc(steps_v.one(), 1)
                            dve.wait_ge(steps_v.sem, steps_v.so_far())
                            dve.scalar_tensor_tensor(arg[:, :, :], whole[:, :, :], -TWO_PI_LO, arg[:, :, :], ALU.mult, ALU.add).then_inc(steps_v.one(), 1)
                            dve.wait_ge(steps_v.sem, steps_v.so_far())
                            dve.tensor_scalar(arg[:, :, :], arg[:, :, :], float(np.pi / 2), PI_IN, ALU.add, ALU.min).then_inc(steps_v.one(), 1)
                            dve.wait_ge(steps_v.sem, steps_v.so_far())
                            if comes(n):
                                dve.wait_ge(cos_ready.sem, cos_ready.at(n))
                            dve.tensor_scalar(turn[:, :, :], arg[:, :, :], -PI_IN, None, ALU.max).then_inc(scaled_read.sem, 1)
                            if comes(3 * i):
                                dve.wait_ge(stored[h].sem, stored[h].at(3 * i))
                            for k in range(K):
                                dve.wait_ge(made.sem, made.at(n * K + k + 1))
                                dve.tensor_tensor(kvs[:, h, k, :], kv_ps[k % 2][:, 0:3 * D], b_kvs[:, :], ALU.add).then_inc(steps_v.one(), 1)
                                dve.tensor_tensor(qs[:, h, k, :], q_ps[k % 2][:, 0:2 * D], b_qs[:, :], ALU.add).then_inc(made_read.sem, 1)
                            if comes(n * K + K):
                                dve.wait_ge(made_read.sem, made_read.at(n * K + K))
                            dve.wait_ge(steps_v.sem, steps_v.so_far())
                            dve.tensor_tensor(prod[:, :, :].rearrange("p (k a) c -> p k (a c)", k=K), kvs[:, h, :, 0:D], qs[:, h, :, 0:D], ALU.mult).then_inc(steps_v.one(), 1)
                            dve.tensor_tensor(kvs[:, h, :, 2 * D:3 * D], kvs[:, h, :, 2 * D:3 * D], xs[:, h, :, :], ALU.add).then_inc(steps_v.one(), 1)
                            dve.tensor_tensor(qs[:, h, :, D:2 * D], qs[:, h, :, D:2 * D], xd[:, h, :, :], ALU.add).then_inc(steps_v.one(), 1)
                            dve.wait_ge(steps_v.sem, steps_v.so_far())
                            dve.sem_inc(results.sem, 1)
                            dve.sem_inc(inputs_read.sem, 1)
                            dve.tensor_reduce(dots[:, :, :].rearrange("p k a -> p (k a)"), prod[:, :, :], AX.X, ALU.add).then_inc(steps_v.one(), 1)
                            dve.wait_ge(steps_v.sem, steps_v.so_far())
                            dve.tensor_scalar(alpha[:, :, bass.ds(n * K, K)], dots[:, :, :].rearrange("p k a -> p a k"), 0.125, None, ALU.mult).then_inc(steps_v.one(), 1)
                    pairs(dve, steps_v, body)

                @block.scalar
                def _(act):
                    def body(i):
                        for h in range(2):
                            n = i * 2 + h
                            act.wait_ge(arg_ready.sem, arg_ready.at(n + 1))
                            if not (isinstance(n, int) and n == 0):
                                if comes(n):
                                    act.wait_ge(cos_ready.sem, cos_ready.at(n))
                            for k in range(K):
                                last = act.activation(turn[:, k, :], w_time[:, :], ACT.Copy, scale=relk[:, h, k:k + 1])
                            last.then_inc(scaled.sem, 1)
                            for s, to in ((0, msg_t), (1, xs_t), (2, xd_t)):
                                act.wait_ge(turned4.sem, turned4.at(n * 4 + s + 1))
                                act.copy(to[:, h, :], x_ps[s][:, :]).then_inc(turned4_out.sem, 1)
                            act.wait_ge(scaled_read.sem, scaled_read.at(n + 1))
                            if comes(n * 4):
                                act.wait_ge(turned4.sem, turned4.at(n * 4))
                            act.activation(cosv[:, :, :], turn[:, :, :], ACT.Sin).then_inc(cos_ready.sem, 1)
                            if comes(n * 4 + 4):
                                act.wait_ge(turned4.sem, turned4.at(n * 4 + 4))
                            act.copy(cos_t[:, h, :], x_ps[3][:, :]).then_inc(turned4_out.sem, 1)
                    act.wait_ge(once_in.sem, once_in.at(len(WEIGHTS)))
                    pairs(act, None, body)

                @block.tensor
                def _(pe):
                    pe.wait_ge(once_in.sem, once_in.at(len(WEIGHTS)))

                    def body(i):
                        for h in range(2):
                            n = i * 2 + h
                            pe.wait_ge(rows_in[h].sem, rows_in[h].at(i + 1))
                            for s, rows in ((0, msg), (1, xs), (2, xd)):
                                if s == 1:
                                    pe.wait_ge(gathered[h].sem, gathered[h].at((i + 1) * 2 * K))
                                if comes((n - 1) * 4 + s + 1):
                                    pe.wait_ge(turned4_out.sem, turned4_out.at((n - 1) * 4 + s + 1))
                                for k in range(K):
                                    mm = pe.transpose(x_ps[s][:, k * P:(k + 1) * P], rows[:, h, k, :], ident[:, :])
                                mm.then_inc(turned4.sem, 1)
                            pe.sem_inc(issued, 1)
                            pe.wait_ge(cos_ready.sem, cos_ready.at(n + 1))
                            if comes(n * 4):
                                pe.wait_ge(turned4_out.sem, turned4_out.at(n * 4))
                            for k in range(K):
                                mm = pe.transpose(x_ps[3][:, k * P:(k + 1) * P], cosv[:, k, :], ident[:, :])
                            mm.then_inc(turned4.sem, 1)
                            if comes(n * 4 + 4):
                                pe.wait_ge(turned4_out.sem, turned4_out.at(n * 4 + 4))
                            for k in range(K):
                                t = slice(k * P, (k + 1) * P)
                                if comes(n * K + k - 1):
                                    pe.wait_ge(made_read.sem, made_read.at(n * K + k - 1))
                                pe.matmul(kv_ps[k % 2][:, 0:3 * D], xs_t[:, h, t], w_kvs[:, :], start=True, stop=False)
                                pe.matmul(kv_ps[k % 2][:, 0:2 * D], msg_t[:, h, t], w_msg[:, :], start=False, stop=False)
                                pe.matmul(kv_ps[k % 2][:, 0:2 * D], cos_t[:, h, t], w_cos[:, :], start=False, stop=True)
                                pe.matmul(q_ps[k % 2][:, 0:2 * D], xd_t[:, h, t], w_qs[:, :], start=True, stop=True).then_inc(made.sem, 1)
                            pe.drain().then_inc(pe_read.sem, 1)
                    pairs(pe, None, body)
            for s, n in ((consts, 1), (once_in, len(WEIGHTS)), (pe_read, GROUPS), (rows_in[0], PAIRS), (rows_in[1], PAIRS), (results, GROUPS),
                         (stored[0], 3 * PAIRS), (stored[1], 3 * PAIRS), (inputs_read, GROUPS), (gathered[0], 2 * K * PAIRS), (gathered[1], 2 * K * PAIRS),
                         (scaled, GROUPS), (scaled_read, GROUPS), (arg_ready, GROUPS), (cos_ready, GROUPS), (turned4, 4 * GROUPS),
                         (turned4_out, 4 * GROUPS), (made, TILES), (made_read, TILES)):
                s.spent(n)

        def by_segment(values, heads_n, largest, result, once_node):
            half = TILES // 2
            CUT = SLOTS // 8
            parts = [(v, c) for v in range(heads_n) for c in range(2)]
            extra = 2 if once_node else 0
            with ExitStack() as st:
                rows = sb(f"rows{signal.n}", [half, 6, P], F32, st)
                flipped = sb(f"flip{signal.n}", [half, 6, P], F32, st)
                ends = sb(f"ends{signal.n}", [1, 2], F32, st)
                signal.n += 1
                with ExitStack() as ps, nc.Block() as block:
                    f_ps = [ps.enter_context(nc.psum_tensor(f"f_ps{s}_{signal.n}", [P, 512], F32)) for s in range(2)]

                    @block.tensor
                    def _(pe):
                        for s, (v, c) in enumerate(parts):
                            mm = pe.transpose(f_ps[0][0:half, s * P:(s + 1) * P], values[:, v, c * half:(c + 1) * half], ident[:, :])
                        for c in range(extra):
                            mm = pe.transpose(f_ps[1][0:half, c * P:(c + 1) * P], dst_next[:, 1 + c * half:1 + (c + 1) * half], ident[:, :])
                        mm.then_inc(turned.sem, 1)

                    @block.vector
                    def _(dve):
                        dve.memset(ends[:, :], -1.0).then_inc(steps_v.one(), 1)
                        dve.wait_ge(turned.sem, turned.at(1))
                        for s in range(len(parts)):
                            dve.tensor_copy(rows[:, s, ::-1], f_ps[0][0:half, s * P:(s + 1) * P]).then_inc(steps_v.one(), 1)
                        for c in range(extra):
                            dve.tensor_copy(rows[:, 4 + c, ::-1], f_ps[1][0:half, c * P:(c + 1) * P]).then_inc(steps_v.one(), 1)
                        dve.wait_ge(steps_v.sem, steps_v.so_far())
                        dve.sem_inc(results.sem, 1)
                        steps_v.end(0)

                    @block.sync
                    def _(sp):
                        sp.wait_ge(results.sem, results.at(1))
                        for s, (v, c) in enumerate(parts):
                            sp.dma_start(val_d[v, c * half * P:(c + 1) * half * P].rearrange("(t p) -> t p", p=P), rows[:, s, :]).then_inc(once_out.sem, 16)
                        for c in range(extra):
                            sp.dma_start(node_d[0, 1 + c * half * P:1 + (c + 1) * half * P].rearrange("(t p) -> t p", p=P), rows[:, 4 + c, :]).then_inc(once_out.sem, 16)
                        if extra:
                            sp.dma_start(node_d[0:1, 0:1], ends[0:1, 0:1]).then_inc(once_out.sem, 16)
                            sp.dma_start(node_d[0:1, SLOTS + 1:SLOTS + 2], ends[0:1, 1:2]).then_inc(once_out.sem, 16)
                        sp.wait_ge(once_out.sem, once_out.at(len(parts) + 2 * extra))
                for s, m in ((turned, 1), (results, 1), (once_out, len(parts) + 2 * extra)):
                    s.spent(m)

            with ExitStack() as st:
                whole_v = sb(f"whole_v{signal.n}", [heads_n, SLOTS], F32, st)
                node = sb(f"node{signal.n}", [heads_n, 2, CUT + 2], F32, st)
                flag = sb(f"flag{signal.n}", [heads_n, CUT], F32, st)
                other = sb(f"other{signal.n}", [heads_n, CUT], F32, st)
                done = sb(f"done{signal.n}", [heads_n, 2, CUT], F32, st)
                signal.n += 1
                order = ([("up", c) for c in range(8)] if largest else []) + [("back", c) for c in reversed(range(8))]
                with nc.Block() as block:
                    @block.sync
                    def _(sp):
                        sp.dma_start(whole_v[:, :], val_d[0:heads_n, :]).then_inc(once_in.sem, 16)
                        for j, (way, c) in enumerate(order):
                            sp.wait_ge(inputs_read.sem, inputs_read.at(j - 1))
                            sp.dma_start(node[:, j % 2, :], node_d[0, c * CUT:(c + 1) * CUT + 2].partition_broadcast(heads_n)).then_inc(rows_in[j % 2].sem, 16)

                    @block.scalar
                    def _(act):
                        for j, c in enumerate(reversed(range(8))):
                            act.wait_ge(results.sem, results.at(j + 1))
                            act.dma_start(seg_d[0:heads_n, c * CUT:(c + 1) * CUT], done[:, j % 2, :]).then_inc(stored[j % 2].sem, 16)
                        for h in range(2):
                            act.wait_ge(stored[h].sem, stored[h].at(4))

                    @block.vector
                    def _(dve):
                        dve.wait_ge(once_in.sem, once_in.at(1))
                        back = 0
                        for j, (way, c) in enumerate(order):
                            cut = slice(c * CUT, (c + 1) * CUT)
                            dve.wait_ge(rows_in[j % 2].sem, rows_in[j % 2].at(j // 2 + 1))
                            here, before, after = node[:, j % 2, 1:CUT + 1], node[:, j % 2, 0:CUT], node[:, j % 2, 2:CUT + 2]
                            if way == "up":
                                dve.tensor_tensor(flag[:, :], here, before, ALU.is_equal).then_inc(steps_v.one(), 1)
                                dve.wait_ge(steps_v.sem, steps_v.so_far())
                                dve.tensor_scalar(flag[:, :], flag[:, :], -1.0, BIG, ALU.add, ALU.mult).then_inc(steps_v.one(), 1)
                                dve.wait_ge(steps_v.sem, steps_v.so_far())
                                begin = -BIG if c == 0 else whole_v[:, c * CUT - 1:c * CUT]
                                dve.tensor_tensor_scan(whole_v[:, cut], flag[:, :], whole_v[:, cut], begin, ALU.add, ALU.max).then_inc(steps_v.one(), 1)
                                dve.wait_ge(steps_v.sem, steps_v.so_far())
                                dve.sem_inc(inputs_read.sem, 1)
                            else:
                                dve.tensor_tensor(flag[:, :], here, after, ALU.is_equal).then_inc(steps_v.one(), 1)
                                dve.wait_ge(steps_v.sem, steps_v.so_far())
                                dve.sem_inc(inputs_read.sem, 1)
                                dve.tensor_scalar(other[:, :], flag[:, :], -1.0, 1.0, ALU.mult, ALU.add).then_inc(steps_v.one(), 1)
                                dve.wait_ge(steps_v.sem, steps_v.so_far())
                                dve.tensor_tensor(other[:, :], other[:, :], whole_v[:, cut], ALU.mult).then_inc(steps_v.one(), 1)
                                dve.wait_ge(steps_v.sem, steps_v.so_far())
                                dve.wait_ge(stored[back % 2].sem, stored[back % 2].at(back // 2))
                                begin = 0.0 if back == 0 else done[:, (back - 1) % 2, 0:1]
                                dve.tensor_tensor_scan(done[:, back % 2, ::-1], flag[:, ::-1], other[:, ::-1], begin, ALU.mult, ALU.add).then_inc(steps_v.one(), 1)
                                dve.wait_ge(steps_v.sem, steps_v.so_far())
                                dve.sem_inc(results.sem, 1)
                                back += 1
                        steps_v.end(0)
                for s, m in ((once_in, 1), (inputs_read, len(order)), (rows_in[0], len(order) // 2), (rows_in[1], len(order) // 2),
                             (results, 8), (stored[0], 4), (stored[1], 4)):
                    s.spent(m)

            with ExitStack() as st:
                rows = sb(f"rows{signal.n}", [half, 4, P], F32, st)
                flipped = sb(f"flip{signal.n}", [half, 4, P], F32, st)
                signal.n += 1
                with ExitStack() as ps, nc.Block() as block:
                    g_ps = ps.enter_context(nc.psum_tensor(f"g_ps_{signal.n}", [P, 512], F32))

                    @block.sync
                    def _(sp):
                        for s, (v, c) in enumerate(parts):
                            sp.dma_start(rows[:, s, :], seg_d[v, c * half * P:(c + 1) * half * P].rearrange("(t p) -> t p", p=P)).then_inc(once_in.sem, 16)

                    @block.vector
                    def _(dve):
                        dve.wait_ge(once_in.sem, once_in.at(len(parts)))
                        for s in range(len(parts)):
                            dve.tensor_copy(flipped[:, s, :], rows[:, s, ::-1]).then_inc(steps_v.one(), 1)
                        dve.wait_ge(steps_v.sem, steps_v.so_far())
                        dve.sem_inc(results.sem, 1)
                        dve.wait_ge(turned.sem, turned.at(1))
                        for s, (v, c) in enumerate(parts):
                            dve.tensor_copy(result[:, v, c * half:(c + 1) * half], g_ps[:, s * half:(s + 1) * half]).then_inc(steps_v.one(), 1)
                        dve.wait_ge(steps_v.sem, steps_v.so_far())
                        steps_v.end(0)

                    @block.tensor
                    def _(pe):
                        pe.wait_ge(results.sem, results.at(1))
                        for s in range(len(parts)):
                            mm = pe.transpose(g_ps[:, s * half:(s + 1) * half], flipped[:, s, :], ident[0:half, 0:half])
                        mm.then_inc(turned.sem, 1)
                for s, m in ((once_in, len(parts)), (turned, 1), (results, 1)):
                    s.spent(m)

        signal.n = 0
        by_segment(alpha, 2, True, segmax, True)

        def norm(dve, y, to, stats, moments, spread, tiles, of, steps):
            for k in range(tiles):
                dve.bn_stats(stats[:, k, :], y(k)).then_inc(steps.one(), 1)
            dve.wait_ge(steps.sem, steps.so_far())
            dve.sem_inc(issued, 1)
            for k in range(tiles):
                dve.bn_aggr(moments[:, k, :], stats[:, k, :]).then_inc(steps.one(), 1)
            dve.wait_ge(steps.sem, steps.so_far())
            dve.tensor_scalar(spread[:, 0:tiles], moments[:, 0:tiles, 1], EPS, None, ALU.add).then_inc(steps.one(), 1)
            dve.wait_ge(steps.sem, steps.so_far())
            dve.sem_inc(varied.sem, 1)
            dve.wait_ge(rooted.sem, rooted.at(of))
            dve.reciprocal(spread[:, 0:tiles], spread[:, 0:tiles]).then_inc(steps.one(), 1)
            dve.wait_ge(steps.sem, steps.so_far())
            for k in range(tiles):
                dve.tensor_scalar(to(k), y(k), moments[:, k, 0:1], spread[:, k:k + 1], ALU.subtract, ALU.mult).then_inc(steps.one(), 1)

        varied = signal("varied")
        rooted = signal("rooted")

        with ExitStack() as st:
            w = sb("w", [P, 2, K, D], F32, st)
            xbd = sb("xbd", [P, 2, K, D], F32, st)
            xbs = sb("xbs", [P, 2, K, D], F32, st)
            same = sb("same_c", [P, 2, G], F32, st)
            carry = sb("carry_c", [1, 2, G], F32, st)
            wk = sb("wk", [P, K, 2], F32, st)
            terms = sb("terms", [P, 2, K, D + 3], F32, st)
            sums = sb("sums", [P, 2, K, D + 3], F32, st)
            den = sb("den", [P, K, 2], F32, st)
            y = sb("y", [P, K, D], F32, st)
            stats = sb("stats", [P, 2 * K, 6], F32, st)
            moments = sb("moments", [P, 2 * K, 2], F32, st)
            spread = sb("spread", [P, 2 * K], F32, st)
            x1 = sb("x1", [P, 2, 2 * K, D], F32, st)
            terms_ready = signal("terms_ready")
            summed = signal("summed")
            sums_out = signal("sums_out")
            with ExitStack() as ps, nc.Block() as block:
                s_ps = [ps.enter_context(nc.psum_tensor(f"s_ps{s}", [P, 512], F32)) for s in range(K)]
                IN = 5

                @block.sync
                def _(sp):
                    def body(i):
                        for h in range(2):
                            n = i * 2 + h
                            if comes(n - 1):
                                sp.wait_ge(pe_read.sem, pe_read.at(n - 1))
                            sp.sem_inc(issued, 1)
                            if comes(n - 1):
                                sp.wait_ge(inputs_read.sem, inputs_read.at(n - 1))
                            sp.sem_inc(issued, 1)
                            sp.dma_start(w[:, h, :, :], tile_rows(v_d, n)).then_inc(rows_in[h].sem, 16)
                            sp.dma_start(xbd[:, h, :, :], tile_rows(xbd_d, n)).then_inc(rows_in[h].sem, 16)
                            sp.dma_start(xbs[:, h, :, :], tile_rows(xbs_d, n)).then_inc(rows_in[h].sem, 16)
                            sp.dma_start(same[:, h, :], same_d[bass.ds(n, 1), :, :].rearrange("g p m -> p (g m)")).then_inc(rows_in[h].sem, 16)
                            sp.dma_start(carry[0:1, h, :], carry_d[bass.ds(n, 1), :]).then_inc(rows_in[h].sem, 16)
                            if not (isinstance(n, int) and n == 0):
                                store(sp, n - 1, 1 - h)

                    def store(sp, n, h):
                        sp.wait_ge(results.sem, results.at(n + 1))
                        sp.sem_inc(issued, 1)
                        sp.dma_start(tile_rows(x1d_d, n), x1[:, h, 0:K, :]).then_inc(stored[h].sem, 16)
                        sp.dma_start(tile_rows(x1s_d, n), x1[:, h, K:2 * K, :]).then_inc(stored[h].sem, 16)
                    pairs(sp, None, body)
                    store(sp, GROUPS - 1, 1)
                    for h in range(2):
                        sp.wait_ge(stored[h].sem, stored[h].at(2 * PAIRS))

                @block.tensor
                def _(pe):
                    def body(i):
                        for h in range(2):
                            n = i * 2 + h
                            pe.wait_ge(rows_in[h].sem, rows_in[h].at(IN * (i + 1)))
                            pe.wait_ge(terms_ready.sem, terms_ready.at(n + 1))
                            for k in range(K):
                                t = slice(k * P, (k + 1) * P)
                                before = sums[0:1, h, k - 1, :] if k else sums[0:1, 1 - h, K - 1, :]
                                if comes(n * K + k):
                                    pe.wait_ge(sums_out.sem, sums_out.at(n * K + k))
                                pe.matmul(s_ps[k][:, 0:D + 3], same[:, h, t], terms[:, h, k, :], start=True, stop=False)
                                pe.matmul(s_ps[k][:, 0:D + 3], carry[0:1, h, t], before, start=False, stop=True).then_inc(summed.sem, 1)
                            pe.drain().then_inc(pe_read.sem, 1)
                    pairs(pe, None, body)

                @block.vector
                def _(dve):
                    dve.tensor_tensor(segmax[:, :, :], alpha[:, :, :], segmax[:, :, :], ALU.subtract).then_inc(steps_v.one(), 1)
                    dve.memset(sums[:, :, :, :], 0.0).then_inc(steps_v.one(), 1)
                    dve.memset(terms[:, :, :, :], 1.0).then_inc(steps_v.one(), 1)
                    dve.wait_ge(steps_v.sem, steps_v.so_far())
                    dve.sem_inc(consts.sem, 1)
                    dve.wait_ge(cos_ready.sem, cos_ready.at(1))
                    dve.sem_inc(issued, 1)
                    steps_v.end(0)

                    def body(i):
                        for h in range(2):
                            n = i * 2 + h
                            dve.wait_ge(rows_in[h].sem, rows_in[h].at(IN * (i + 1)))
                            dve.wait_ge(steps_v.sem, steps_v.so_far())
                            dve.tensor_scalar(wk[:, :, :].rearrange("p k a -> p a k"), alpha[:, :, bass.ds(n * K, K)], 0.0, None, ALU.add).then_inc(steps_v.one(), 1)
                            dve.wait_ge(steps_v.sem, steps_v.so_far())
                            if comes(n - 1):
                                dve.wait_ge(pe_read.sem, pe_read.at(n - 1))
                            dve.tensor_tensor(terms[:, h, :, 0:D].rearrange("p k (a c) -> p k a c", a=2),
                                                          w[:, h, :, :].rearrange("p k (a c) -> p k a c", a=2),
                                                          wk[:, :, :].unsqueeze(3).to_broadcast([P, K, 2, 64]), ALU.mult).then_inc(steps_v.one(), 1)
                            dve.tensor_copy(terms[:, h, :, D:D + 2], wk[:, :, :]).then_inc(steps_v.one(), 1)
                            dve.wait_ge(steps_v.sem, steps_v.so_far())
                            dve.sem_inc(terms_ready.sem, 1)
                            for k in range(K):
                                dve.wait_ge(summed.sem, summed.at(n * K + k + 1))
                                dve.tensor_copy(sums[:, h, k, :], s_ps[k][:, 0:D + 3]).then_inc(sums_out.sem, 1)
                            if comes(n * K + K):
                                dve.wait_ge(sums_out.sem, sums_out.at(n * K + K))
                            dve.tensor_scalar(den[:, :, :], sums[:, h, :, D:D + 2], 1e-16, None, ALU.add).then_inc(steps_v.one(), 1)
                            dve.tensor_scalar(inv_deg[:, bass.ds(n * K, K)], sums[:, h, :, D + 2], 0.0, None, ALU.add).then_inc(steps_v.one(), 1)
                            dve.wait_ge(steps_v.sem, steps_v.so_far())
                            dve.reciprocal(den[:, :, :], den[:, :, :]).then_inc(steps_v.one(), 1)
                            dve.wait_ge(steps_v.sem, steps_v.so_far())
                            dve.tensor_tensor(y[:, :, :].rearrange("p k (a c) -> p k a c", a=2),
                                                          sums[:, h, :, 0:D].rearrange("p k (a c) -> p k a c", a=2),
                                                          den[:, :, :].unsqueeze(3).to_broadcast([P, K, 2, 64]), ALU.mult).then_inc(steps_v.one(), 1)
                            dve.wait_ge(steps_v.sem, steps_v.so_far())
                            dve.tensor_tensor(y[:, :, :], y[:, :, :], xbd[:, h, :, :], ALU.add).then_inc(steps_v.one(), 1)
                            dve.wait_ge(steps_v.sem, steps_v.so_far())
                            if comes(2 * i):
                                dve.wait_ge(stored[h].sem, stored[h].at(2 * i))
                            norm(dve, lambda k: y[:, k, :] if k < K else xbs[:, h, k - K, :], lambda k: x1[:, h, k, :],
                                 stats, moments, spread, 2 * K, n + 1, steps_v)
                            dve.wait_ge(steps_v.sem, steps_v.so_far())
                            dve.sem_inc(results.sem, 1)
                            dve.sem_inc(inputs_read.sem, 1)
                    pairs(dve, steps_v, body)
                    dve.reciprocal(inv_deg[:, :], inv_deg[:, :]).then_inc(steps_v.one(), 1)
                    dve.wait_ge(steps_v.sem, steps_v.so_far())
                    dve.sem_inc(turned.sem, 1)
                    steps_v.end(0)

                @block.scalar
                def _(act):
                    act.wait_ge(consts.sem, consts.at(1))
                    act.activation(alpha[:, :, :], segmax[:, :, :], ACT.Exp).then_inc(cos_ready.sem, 1)

                    def body(i):
                        for h in range(2):
                            act.wait_ge(varied.sem, varied.at(i * 2 + h + 1))
                            act.activation(spread[:, :], spread[:, :], ACT.Sqrt).then_inc(rooted.sem, 1)
                    pairs(act, None, body)
                    act.wait_ge(turned.sem, turned.at(1))
                    act.activation(nd[:, :], inv_deg[:, :], ACT.Sqrt).then_inc(cos_ready.sem, 1)
            for s, m in ((pe_read, GROUPS), (inputs_read, GROUPS), (rows_in[0], IN * PAIRS), (rows_in[1], IN * PAIRS), (results, GROUPS),
                         (stored[0], 2 * PAIRS), (stored[1], 2 * PAIRS), (terms_ready, GROUPS), (summed, TILES), (sums_out, TILES),
                         (consts, 1), (cos_ready, 2), (turned, 1), (varied, GROUPS), (rooted, GROUPS)):
                s.spent(m)

        weights = {}
        w_small = sb("w_small", [P, 6])
        attn_in = sb("attn_in", [P, 3, TILES])
        seg_z = sb("seg_z", [P, 1, TILES])
        logits = sb("logits", [P, 1, TILES])
        seg_a = sb("seg_a", [P, 1, TILES])
        edge_x = sb("edge_x", [P, 2, TILES])
        wctx = ExitStack()

        def weight(name):
            weights[name] = sb("w_" + name, [P, D], F32, wctx)
            return weights[name], a[name]

        def bias(name):
            weights[name] = sb("b_" + name, [P, K, D], F32, wctx)
            return [(weights[name][:, k, :], a[name].partition_broadcast(P)) for k in range(K)]

        to_load = [weight(w) for w in ("L1_gnn_W1", "L1_gnn_Wr1", "L1_gnn_W2", "L1_gnn_Wr2", "L1_gnn_W3",
                                       "L2_gnn_W1_0", "L2_gnn_W2_0", "L2_gnn_W3_0", "L2_gnn_W1_1", "L2_gnn_W2_1", "L2_gnn_W3_1")]
        to_load = [(t[:, :], w[:, :]) for t, w in to_load]
        for w in ("L1_gnn_b1", "L1_gnn_br1", "L1_gnn_b2", "L1_gnn_br2", "L1_gnn_b3"):
            to_load += bias(w)
        w_attn = sb("w_attn", [P, 2, K, D], F32, wctx)
        to_load += [(w_attn[:, s, k, :], a["L3_gnn_w_attn"][0, s * D:(s + 1) * D].partition_broadcast(P)) for s in range(2) for k in range(K)]
        to_load += [(w_small[:, 0:4], a["L3_gnn_w_edge"].rearrange("a b -> (a b)").partition_broadcast(P)),
                    (w_small[:, 4:6], a["L3_gnn_w_attn"][0, 2 * D:2 * D + 2].partition_broadcast(P))]
        zero_rows = sb("zero_rows", [8, D], F32, wctx)
        with nc.Block() as block:
            @block.vector
            def _(dve):
                dve.memset(zero_rows[:, :], 0.0).then_inc(consts.sem, 1)

            @block.sync
            def _(sp):
                for to, w in to_load:
                    sp.dma_start(to, w).then_inc(once_in.sem, 16)
                sp.wait_ge(once_in.sem, once_in.at(len(to_load)))
                sp.wait_ge(consts.sem, consts.at(1))
                for t in (agg1_d, agg2_d):
                    sp.dma_start(t[SLOTS:SLOTS + 8, :], zero_rows[:, :]).then_inc(once_out.sem, 16)
                sp.wait_ge(once_out.sem, once_out.at(2))
        consts.spent(1)
        once_in.spent(len(to_load))
        once_out.spent(2)

        rows_b = [signal(f"rows_b{h}", 16) for h in range(2)]
        stored_g = [signal(f"stored_g{h}", 16) for h in range(2)]
        steps_f = Steps(nc, ctx, "finish_steps")
        chained = signal("chained")
        product = signal("product")
        side_turned = signal("side_turned")
        side_turned_out = signal("side_turned_out")
        side = signal("side")
        side_out = signal("side_out")

        def conv(tag, loads_a, loads_b, job, store_gathered, turns, w_main, terms, finish, outs, normed, extra=()):
            with ExitStack() as st:
                buf = {}
                for key, _ in loads_a + loads_b + outs + [(job[2], None)] + [(key, None) for key in extra]:
                    if key not in buf:
                        buf[key] = sb(f"{key}_{tag}", [P, 2, K, D], F32, st)
                same = sb(f"same_{tag}", [P, 2, G], F32, st)
                carry = sb(f"carry_{tag}", [P, 2, G], F32, st)
                idx = sb(f"idx_{tag}", [P, 2, 1, K], I32, st)
                term = sb(f"term_{tag}", [P, 2, K, D], F32, st)
                agg_t = sb(f"agg_t_{tag}", [P, 2, K, P], F32, st)
                row_t = sb(f"row_t_{tag}", [P, 2, G], F32, st)
                buf["term"] = term
                for j in range(len(turns)):
                    buf[f"m{j}"] = sb(f"m{j}_{tag}", [P, 2, K, D], F32, st)
                for key in ("t1", "t2"):
                    buf[key] = sb(f"{key}_{tag}", [P, K, D], F32, st)
                buf["y"] = sb(f"y_{tag}", [P, 2 * K, D], F32, st)
                stats = sb(f"stats_{tag}", [P, 2 * K, 6], F32, st)
                moments = sb(f"moments_{tag}", [P, 2 * K, 2], F32, st)
                spread = sb(f"spread_{tag}", [P, 2 * K], F32, st)
                buf["norm"] = (stats, moments, spread)
                NA, NB, NT, NO = len(loads_a) + 2, len(loads_b), len(turns), len(outs)
                last_n = GROUPS - 1

                def is_n(n, value):
                    return isinstance(n, int) and n == value

                with ExitStack() as ps, nc.Block() as block:
                    agg_ps = [ps.enter_context(nc.psum_tensor(f"agg_ps{s}_{tag}", [P, 512], F32)) for s in range(2)]
                    out_ps = [ps.enter_context(nc.psum_tensor(f"out_ps{s}_{tag}", [P, 512], F32)) for s in range(2)]
                    t_ps = [ps.enter_context(nc.psum_tensor(f"t_ps{s}_{tag}", [P, 512], F32)) for s in range(2)]
                    m_ps = [ps.enter_context(nc.psum_tensor(f"m_ps{s}_{tag}", [P, 512], F32)) for s in range(2)]
                    buf["out"] = out_ps

                    @block.sync
                    def _(sp):
                        def load_b(n, h):
                            if comes(n - 1):
                                sp.wait_ge(results.sem, results.at(n - 1))
                            sp.sem_inc(issued, 1)
                            for key, table in loads_b:
                                sp.dma_start(buf[key][:, h, :, :], tile_rows(table, n)).then_inc(rows_b[h].sem, 16)

                        def store(n, h):
                            sp.wait_ge(results.sem, results.at(n + 1))
                            sp.sem_inc(issued, 1)
                            for key, table in outs:
                                sp.dma_start(tile_rows(table, n), buf[key][:, h, :, :]).then_inc(stored[h].sem, 16)

                        def store_g(n, h):
                            sp.wait_ge(terms_ready.sem, terms_ready.at(n + 1))
                            sp.sem_inc(issued, 1)
                            sp.dma_start(tile_rows(store_gathered, n), buf[job[2]][:, h, :, :]).then_inc(stored_g[h].sem, 16)

                        def body(i):
                            for h in range(2):
                                n = i * 2 + h
                                if comes(n - 1):
                                    sp.wait_ge(inputs_read.sem, inputs_read.at(n - 1))
                                sp.sem_inc(issued, 1)
                                if comes(n - 1):
                                    sp.wait_ge(pe_read.sem, pe_read.at(n - 1))
                                sp.sem_inc(issued, 1)
                                if store_gathered is not None:
                                    if comes(i):
                                        sp.wait_ge(stored_g[h].sem, stored_g[h].at(i))
                                    sp.sem_inc(issued, 1)
                                for key, table in loads_a:
                                    sp.dma_start(buf[key][:, h, :, :], tile_rows(table, n)).then_inc(rows_in[h].sem, 16)
                                sp.dma_start(same[:, h, :], same_d[bass.ds(n, 1), :, :].rearrange("g p m -> p (g m)")).then_inc(rows_in[h].sem, 16)
                                sp.dma_start(carry[:, h, :], carry_d[bass.ds(n, 1), :].rearrange("g m -> (g m)").partition_broadcast(P)).then_inc(rows_in[h].sem, 16)
                                if not is_n(n, 0):
                                    if store_gathered is not None:
                                        store_g(n - 1, 1 - h)
                                    load_b(n - 1, 1 - h)
                                if not (isinstance(n, int) and n < 2):
                                    store(n - 2, h)
                        pairs(sp, None, body)
                        if store_gathered is not None:
                            store_g(last_n, 1)
                            for h in range(2):
                                sp.wait_ge(stored_g[h].sem, stored_g[h].at(PAIRS))
                        load_b(last_n, 1)
                        for n in range(last_n - 1, last_n + 1):
                            store(n, n % 2)
                        for h in range(2):
                            sp.wait_ge(stored[h].sem, stored[h].at(NO * PAIRS))

                    @block.gpsimd
                    def _(pool):
                        def body(i):
                            for h in range(2):
                                n = i * 2 + h
                                if comes(n - 1):
                                    pool.wait_ge(inputs_read.sem, inputs_read.at(n - 1))
                                if comes(n - 1):
                                    pool.wait_ge(pe_read.sem, pe_read.at(n - 1))
                                pool.sem_inc(issued, 1)
                                pool.wait_ge(rows_in[h].sem, rows_in[h].at(NA * (i + 1)))
                                if store_gathered is not None:
                                    if comes(i):
                                        pool.wait_ge(stored_g[h].sem, stored_g[h].at(i))
                                pool.sem_inc(issued, 1)
                                gather(pool, i, h, [(src_row, job[0], job[1], buf[job[2]][:, h, :, :])], idx, 1)
                        pairs(pool, steps_g, body)

                    @block.tensor
                    def _(pe):
                        def turn(i, h, n):
                            pe.wait_ge(rows_in[h].sem, rows_in[h].at(NA * (i + 1)))
                            pe.wait_ge(gathered[h].sem, gathered[h].at(K * (i + 1)))
                            for j, (key, w) in enumerate(turns):
                                for k in range(K):
                                    mm = pe.transpose(t_ps[j][:, k * P:(k + 1) * P], buf[key][:, h, k, :], ident[:, :])
                                mm.then_inc(side_turned.sem, 1)
                            for j, (key, w) in enumerate(turns):
                                pe.wait_ge(side_turned_out.sem, side_turned_out.at(n * NT + j + 1))
                                if comes((n - 1) * NT + j + 1):
                                    pe.wait_ge(side_out.sem, side_out.at((n - 1) * NT + j + 1))
                                for k in range(K):
                                    mm = pe.matmul(m_ps[j][:, k * D:(k + 1) * D], turn_t[j][:, k * P:(k + 1) * P], weights[w][:, :], start=True, stop=True)
                                mm.then_inc(side.sem, 1)

                        def body(i):
                            for h in range(2):
                                n = i * 2 + h
                                pe.wait_ge(terms_ready.sem, terms_ready.at(n + 1))
                                pe.wait_ge(rows_in[h].sem, rows_in[h].at(NA * (i + 1)))
                                for k in range(K):
                                    mm = pe.matmul(agg_ps[h][:, k * P:(k + 1) * P], term[:, h, k, :], same[:, h, k * P:(k + 1) * P], start=True, stop=True)
                                mm.then_inc(summed.sem, 1)
                                if turns and not is_n(n, last_n):
                                    turn(i if h == 0 else i + 1, 1 - h, n + 1)
                                pe.wait_ge(chained.sem, chained.at(n + 1))
                                for k in range(K):
                                    mm = pe.matmul(out_ps[h][:, k * D:(k + 1) * D], agg_t[:, h, k, :], weights[w_main][:, :], start=True, stop=True)
                                mm.then_inc(product.sem, 1)
                                pe.drain().then_inc(pe_read.sem, 1)
                        if turns:
                            turn(0, 0, 0)
                        pairs(pe, None, body)

                    @block.scalar
                    def _(act):
                        def copies(n, h):
                            for j in range(NT):
                                if comes((n - 1) * NT + j + 1):
                                    act.wait_ge(side.sem, side.at((n - 1) * NT + j + 1))
                                act.wait_ge(side_turned.sem, side_turned.at(n * NT + j + 1))
                                act.copy(turn_t[j][:, :], t_ps[j][:, :]).then_inc(side_turned_out.sem, 1)
                            for j in range(NT):
                                if comes(n - 1):
                                    act.wait_ge(results.sem, results.at(n - 1))
                                act.wait_ge(side.sem, side.at(n * NT + j + 1))
                                act.copy(buf[f"m{j}"][:, h, :, :].rearrange("p k d -> p (k d)"), m_ps[j][:, :]).then_inc(side_out.sem, 1)

                        def root(n):
                            act.wait_ge(varied.sem, varied.at(n + 1))
                            act.activation(spread[:, :], spread[:, :], ACT.Sqrt).then_inc(rooted.sem, 1)

                        def body(i):
                            for h in range(2):
                                n = i * 2 + h
                                if normed and not is_n(n, 0):
                                    root(n - 1)
                                if turns and not is_n(n, last_n):
                                    copies(n + 1, 1 - h)
                        if turns:
                            copies(0, 0)
                        if turns or normed:
                            pairs(act, None, body)
                        if normed:
                            root(last_n)

                    @block.vector
                    def _(dve):
                        dve.memset(agg_t[:, :, :, :], 0.0).then_inc(steps_v.one(), 1)
                        dve.wait_ge(steps_v.sem, steps_v.so_far())
                        steps_v.end(0)

                        def finish_group(i, h, n):
                            if NB:
                                dve.wait_ge(rows_b[h].sem, rows_b[h].at(NB * (i + 1)))
                            dve.wait_ge(product.sem, product.at(n + 1))
                            if comes(NO * i):
                                dve.wait_ge(stored[h].sem, stored[h].at(NO * i))
                            steps_f.begin(n)
                            if comes(n):
                                dve.wait_ge(steps_f.sem, steps_f.so_far())
                            finish(dve, buf, h, n)
                            dve.wait_ge(steps_f.sem, steps_f.so_far())
                            dve.sem_inc(results.sem, 1)
                            if is_n(n, 0):
                                steps_f.per = steps_f.j
                            assert steps_f.j == steps_f.per

                        def body(i):
                            for h in range(2):
                                n = i * 2 + h
                                dve.wait_ge(steps_v.sem, steps_v.so_far())
                                dve.wait_ge(rows_in[h].sem, rows_in[h].at(NA * (i + 1)))
                                dve.wait_ge(gathered[h].sem, gathered[h].at(K * (i + 1)))
                                if turns:
                                    dve.wait_ge(side_out.sem, side_out.at((n + 1) * NT))
                                if comes(n - 1):
                                    dve.wait_ge(pe_read.sem, pe_read.at(n - 1))
                                terms(dve, buf, h, n)
                                dve.wait_ge(steps_v.sem, steps_v.so_far())
                                dve.sem_inc(terms_ready.sem, 1)
                                if not is_n(n, 0):
                                    finish_group(i if h else i - 1, 1 - h, n - 1)
                                dve.wait_ge(summed.sem, summed.at(n + 1))
                                for k in range(K):
                                    before = agg_t[:, h, k - 1, 0:1] if k else agg_t[:, 1 - h, K - 1, 0:1]
                                    dve.scalar_tensor_tensor(agg_t[:, h, k, :], carry[:, h, k * P:(k + 1) * P], before,
                                                                         agg_ps[h][:, k * P:(k + 1) * P], ALU.mult, ALU.add).then_inc(steps_v.one(), 1)
                                    dve.wait_ge(steps_v.sem, steps_v.so_far())
                                dve.sem_inc(chained.sem, 1)
                                dve.sem_inc(inputs_read.sem, 1)
                        pairs(dve, steps_v, body)
                        finish_group(PAIRS - 1, 1, last_n)
                        steps_f.end(GROUPS)
                counts = [(inputs_read, GROUPS), (pe_read, GROUPS), (rows_in[0], NA * PAIRS), (rows_in[1], NA * PAIRS), (results, GROUPS),
                          (stored[0], NO * PAIRS), (stored[1], NO * PAIRS), (gathered[0], K * PAIRS), (gathered[1], K * PAIRS),
                          (rows_b[0], NB * PAIRS), (rows_b[1], NB * PAIRS), (terms_ready, GROUPS), (summed, GROUPS), (chained, GROUPS),
                          (product, GROUPS), (side_turned, NT * GROUPS), (side_turned_out, NT * GROUPS), (side, NT * GROUPS), (side_out, NT * GROUPS)]
                if store_gathered is not None:
                    counts += [(stored_g[0], PAIRS), (stored_g[1], PAIRS)]
                if normed:
                    counts += [(varied, GROUPS), (rooted, GROUPS)]
                for s, m in counts:
                    s.spent(m)

        turn_t = [sb(f"turn_t{j}", [P, G], F32, wctx) for j in range(2)]

        def per_slot(cols, n):
            return cols[:, bass.ds(n * K, K)].unsqueeze(2).to_broadcast([P, K, D])

        def out_rows(buf, h):
            return buf["out"][h][:, :].rearrange("p (k d) -> p k d", k=K)

        def add(dve, steps, to, x, y, op=ALU.add):
            dve.tensor_tensor(to, x, y, op).then_inc(steps.one(), 1)
            dve.wait_ge(steps.sem, steps.so_far())

        def leaky(dve, steps, to, x):
            dve.scalar_tensor_tensor(to, x, SLOPE, x, ALU.mult, ALU.max).then_inc(steps.one(), 1)
            dve.wait_ge(steps.sem, steps.so_far())

        def norm_two(dve, buf, n, h, first, second):
            y = buf["y"]
            stats, moments, spread = buf["norm"]
            norm(dve, lambda k: y[:, k, :], lambda k: buf[first][:, h, k, :] if k < K else buf[second][:, h, k - K, :],
                 stats, moments, spread, 2 * K, n + 1, steps_f)

        def terms_1(dve, buf, h, n):
            dve.tensor_tensor(buf["term"][:, h, :, :], buf["x"][:, h, :, :], per_slot(ns, n), ALU.mult).then_inc(steps_v.one(), 1)

        def scaled_out(dve, buf, h, n):
            dve.tensor_tensor(buf["o"][:, h, :, :], out_rows(buf, h), per_slot(nd, n), ALU.mult).then_inc(steps_f.one(), 1)

        conv("c1", [("x", x1s_d)], [], (x1d_d[:, :], SLOTS, "x"), x1g_d, [], "L1_gnn_W1", terms_1, scaled_out, [("o", agg1_d)], False)

        def hidden(b, br):
            def terms(dve, buf, h, n):
                add(dve, steps_v, buf["t1"][:, :, :], buf["a"][:, h, :, :], weights[b][:, :, :])
                dve.scalar_tensor_tensor(buf["t2"][:, :, :], buf["t1"][:, :, :], 0.0, buf["m0"][:, h, :, :], ALU.max, ALU.add).then_inc(steps_v.one(), 1)
                dve.wait_ge(steps_v.sem, steps_v.so_far())
                add(dve, steps_v, buf["a"][:, h, :, :], buf["t2"][:, :, :], weights[br][:, :, :])
                add(dve, steps_v, buf["term"][:, h, :, :], buf["a"][:, h, :, :], per_slot(ns, n), ALU.mult)
            return terms

        conv("c2", [("x", x1g_d)], [], (agg1_d[:, :], SLOTS + 8, "a"), h1_d, [("x", "L1_gnn_Wr1")], "L1_gnn_W2",
             hidden("L1_gnn_b1", "L1_gnn_br1"), scaled_out, [("o", agg2_d)], False)

        def finish_3(dve, buf, h, n):
            y = buf["y"]
            dve.tensor_tensor(y[:, 0:K, :], out_rows(buf, h), per_slot(nd, n), ALU.mult).then_inc(steps_f.one(), 1)
            add(dve, steps_f, y[:, K:2 * K, :], buf["xg"][:, h, :, :], weights["L1_gnn_b3"][:, :, :])
            add(dve, steps_f, y[:, 0:K, :], y[:, 0:K, :], weights["L1_gnn_b3"][:, :, :])
            add(dve, steps_f, y[:, 0:K, :], y[:, 0:K, :], buf["xd"][:, h, :, :])
            norm_two(dve, buf, n, h, "o", "os")

        conv("c3", [("x", h1_d)], [("xd", x1d_d), ("xg", x1g_d)], (agg2_d[:, :], SLOTS + 8, "a"), None, [("x", "L1_gnn_Wr2")], "L1_gnn_W3",
             hidden("L1_gnn_b2", "L1_gnn_br2"), finish_3, [("o", x2d_d), ("os", x2s_d)], True)

        def terms_e(dve, buf, h, n):
            add(dve, steps_v, buf["term"][:, h, :, :], buf["x"][:, h, :, :], buf["e"][:, h, :, :])

        def finish_4(dve, buf, h, n):
            y = buf["y"]
            add(dve, steps_f, y[:, 0:K, :], out_rows(buf, h), per_slot(inv_deg, n), ALU.mult)
            add(dve, steps_f, y[:, 0:K, :], y[:, 0:K, :], buf["m1"][:, h, :, :])
            leaky(dve, steps_f, buf["o"][:, h, :, :], y[:, 0:K, :])
            leaky(dve, steps_f, buf["os"][:, h, :, :], buf["m0"][:, h, :, :])

        conv("c4", [("x", x2s_d), ("e", rows_d), ("d", x2d_d)], [], (x2d_d[:, :], SLOTS, "x"), x2g_d,
             [("x", "L2_gnn_W3_0"), ("d", "L2_gnn_W2_0")], "L2_gnn_W1_0", terms_e, finish_4, [("o", g1d_d), ("os", g1s_d)], False)

        dotw = sb("dotw", [P, 2 * K, D], F32, wctx)
        dotk = sb("dotk", [P, 2 * K], F32, wctx)

        def finish_5(dve, buf, h, n):
            y = buf["y"]
            add(dve, steps_f, y[:, 0:K, :], out_rows(buf, h), per_slot(inv_deg, n), ALU.mult)
            add(dve, steps_f, y[:, 0:K, :], y[:, 0:K, :], buf["m1"][:, h, :, :])
            leaky(dve, steps_f, y[:, 0:K, :], y[:, 0:K, :])
            leaky(dve, steps_f, y[:, K:2 * K, :], buf["m0"][:, h, :, :])
            add(dve, steps_f, y[:, 0:K, :], y[:, 0:K, :], buf["xd"][:, h, :, :])
            add(dve, steps_f, y[:, K:2 * K, :], y[:, K:2 * K, :], buf["xg"][:, h, :, :])
            norm_two(dve, buf, n, h, "o", "x3s")
            dve.wait_ge(steps_f.sem, steps_f.so_far())
            dve.tensor_tensor(dotw[:, 0:K, :], buf["x3s"][:, h, :, :], w_attn[:, 0, :, :], ALU.mult).then_inc(steps_f.one(), 1)
            add(dve, steps_f, dotw[:, K:2 * K, :], buf["o"][:, h, :, :], w_attn[:, 0, :, :], ALU.mult)
            dve.tensor_reduce(dotk[:, :], dotw[:, :, :], AX.X, ALU.add).then_inc(steps_f.one(), 1)
            dve.wait_ge(steps_f.sem, steps_f.so_far())
            dve.tensor_scalar(attn_in[:, 0:2, bass.ds(n * K, K)], dotk[:, :].rearrange("p (s k) -> p s k", s=2), 0.0, None, ALU.add).then_inc(steps_f.one(), 1)
            add(dve, steps_f, dotw[:, 0:K, :], buf["o"][:, h, :, :], w_attn[:, 1, :, :], ALU.mult)
            dve.tensor_reduce(dotk[:, 0:K], dotw[:, 0:K, :], AX.X, ALU.add).then_inc(steps_f.one(), 1)
            dve.wait_ge(steps_f.sem, steps_f.so_far())
            dve.tensor_scalar(attn_in[:, 2, bass.ds(n * K, K)], dotk[:, 0:K], 0.0, None, ALU.add).then_inc(steps_f.one(), 1)

        conv("c5", [("x", g1s_d), ("e", rows_d), ("d", g1d_d)], [("xd", x2d_d), ("xg", x2g_d)], (g1d_d[:, :], SLOTS, "x"), None,
             [("x", "L2_gnn_W3_1"), ("d", "L2_gnn_W2_1")], "L2_gnn_W1_1", terms_e, finish_5, [("o", x3d_d)], True, extra=("x3s",))

        D_GROUPS = 2 * (-(-N // (2 * G)))
        D_PAIRS = D_GROUPS // 2
        with ExitStack() as st:
            w_skip = sb("w_skip", [P, D], F32, st)
            b_skip = sb("b_skip", [P, K, D], F32, st)
            x = sb("x_n", [P, 2, K, D], F32, st)
            x_t = sb("x_t_n", [P, 2, G], F32, st)
            y = sb("y_n", [P, 2, K, D], F32, st)
            x1 = sb("x1_n", [P, 2, K, D], F32, st)
            x2 = sb("x2_n", [P, 2, K, D], F32, st)
            g1 = sb("g1_n", [P, 2, K, D], F32, st)
            x4 = sb("x4_n", [P, 2, K, D], F32, st)
            stats = sb("stats_n", [P, 2, K, 6], F32, st)
            moments = sb("moments_n", [P, 2, K, 2], F32, st)
            spread = sb("spread_n", [P, 2, K], F32, st)
            ready = signal("ready")

            def rows_of(table, n):
                at = N - G if isinstance(n, int) and n == D_GROUPS - 1 else n * G
                return table[bass.ds(at, G), :].rearrange("(k p) d -> p k d", p=P)

            with ExitStack() as ps, nc.Block() as block:
                nt_ps = [ps.enter_context(nc.psum_tensor(f"nt_ps{s}", [P, 512], F32)) for s in range(2)]
                nm_ps = [ps.enter_context(nc.psum_tensor(f"nm_ps{s}", [P, 512], F32)) for s in range(2)]

                @block.sync
                def _(sp):
                    sp.dma_start(w_skip[:, :], a["L0_gnn_W_skip"][:, :]).then_inc(once_in.sem, 16)
                    for k in range(K):
                        sp.dma_start(b_skip[:, k, :], a["L0_gnn_b_skip"].partition_broadcast(P)).then_inc(once_in.sem, 16)

                    def body(i):
                        for h in range(2):
                            if not (isinstance(i, int) and i == 0):
                                if comes((i - 1) * 6 + h + 1):
                                    sp.wait_ge(varied.sem, varied.at((i - 1) * 6 + h + 1))
                                sp.sem_inc(issued, 1)
                            sp.dma_start(x[:, h, :, :], rows_of(a["x"], i * 2 + h)).then_inc(rows_in[h].sem, 16)
                        for h in range(2):
                            if not (isinstance(i, int) and i == 0):
                                store(i - 1, h)

                    def store(i, h):
                        n = i * 2 + h
                        sp.wait_ge(results.sem, results.at(n + 1))
                        sp.sem_inc(issued, 1)
                        if isinstance(n, int) and n == D_GROUPS - 1:
                            sp.wait_ge(stored[0].sem, stored[0].at(D_PAIRS))
                        sp.dma_start(rows_of(out, n), x4[:, h, :, :]).then_inc(stored[h].sem, 16)
                    pairs(sp, None, body, D_PAIRS)
                    store(D_PAIRS - 1, 0)
                    store(D_PAIRS - 1, 1)
                    for h in range(2):
                        sp.wait_ge(stored[h].sem, stored[h].at(D_PAIRS))

                @block.tensor
                def _(pe):
                    pe.wait_ge(once_in.sem, once_in.at(1 + K))

                    def body(i):
                        for s, (rows, w) in enumerate(((x, w_skip), (x2, weights["L2_gnn_W3_0"]), (g1, weights["L2_gnn_W3_1"]))):
                            for h in range(2):
                                if s == 0:
                                    pe.wait_ge(rows_in[h].sem, rows_in[h].at(i + 1))
                                else:
                                    if comes(i * 4 + (s - 1) * 2 + h + 1):
                                        pe.wait_ge(ready.sem, ready.at(i * 4 + (s - 1) * 2 + h + 1))
                                if comes(i * 6 + s * 2 + h - 1):
                                    pe.wait_ge(side_turned_out.sem, side_turned_out.at(i * 6 + s * 2 + h - 1))
                                for k in range(K):
                                    mm = pe.transpose(nt_ps[h][:, k * P:(k + 1) * P], rows[:, h, k, :], ident[:, :])
                                mm.then_inc(side_turned.sem, 1)
                            for h in range(2):
                                pe.wait_ge(side_turned_out.sem, side_turned_out.at(i * 6 + s * 2 + h + 1))
                                if s == 0:
                                    if comes(i * 6):
                                        pe.wait_ge(varied.sem, varied.at(i * 6))
                                for k in range(K):
                                    mm = pe.matmul(nm_ps[h][:, k * D:(k + 1) * D], x_t[:, h, k * P:(k + 1) * P], w[:, :], start=True, stop=True)
                                mm.then_inc(side.sem, 1)
                    pairs(pe, None, body, D_PAIRS)

                @block.scalar
                def _(act):
                    def body(i):
                        def copies(s):
                            for h in range(2):
                                act.wait_ge(side_turned.sem, side_turned.at(i * 6 + s * 2 + h + 1))
                                if comes(i * 6 + s * 2 + h - 1):
                                    act.wait_ge(side.sem, side.at(i * 6 + s * 2 + h - 1))
                                act.copy(x_t[:, h, :], nt_ps[h][:, :]).then_inc(side_turned_out.sem, 1)

                        def roots(r):
                            for h in range(2):
                                act.wait_ge(varied.sem, varied.at(i * 6 + r * 2 + h + 1))
                                act.activation(spread[:, h, :], spread[:, h, :], ACT.Sqrt).then_inc(rooted.sem, 1)
                        copies(0)
                        roots(0)
                        roots(1)
                        copies(1)
                        copies(2)
                        roots(2)
                    pairs(act, None, body, D_PAIRS)

                @block.vector
                def _(dve):
                    dve.wait_ge(once_in.sem, once_in.at(1 + K))
                    dve.sem_inc(issued, 1)

                    def body(i):
                        def moment(h, double=False):
                            for k in range(K):
                                dve.bn_stats(stats[:, h, k, :], y[:, h, k, :]).then_inc(steps_v.one(), 1)
                            dve.wait_ge(steps_v.sem, steps_v.so_far())
                            dve.sem_inc(issued, 1)
                            for k in range(K):
                                dve.bn_aggr(moments[:, h, k, :], stats[:, h, k, :]).then_inc(steps_v.one(), 1)
                            dve.wait_ge(steps_v.sem, steps_v.so_far())
                            factor, rest = (1.0 + EPS, EPS * EPS) if double else (1.0, EPS)
                            dve.tensor_scalar(spread[:, h, :], moments[:, h, :, 1], factor, rest, ALU.mult, ALU.add).then_inc(steps_v.one(), 1)
                            dve.wait_ge(steps_v.sem, steps_v.so_far())
                            dve.sem_inc(varied.sem, 1)

                        def normed_to(r, h, to):
                            dve.wait_ge(rooted.sem, rooted.at(i * 6 + r * 2 + h + 1))
                            dve.reciprocal(spread[:, h, :], spread[:, h, :]).then_inc(steps_v.one(), 1)
                            dve.wait_ge(steps_v.sem, steps_v.so_far())
                            for k in range(K):
                                dve.tensor_scalar(to[:, h, k, :], y[:, h, k, :], moments[:, h, k, 0:1], spread[:, h, k:k + 1], ALU.subtract, ALU.mult).then_inc(steps_v.one(), 1)
                            dve.wait_ge(steps_v.sem, steps_v.so_far())

                        def made_rows(h):
                            return nm_ps[h][:, :].rearrange("p (k d) -> p k d", k=K)

                        dve.wait_ge(steps_v.sem, steps_v.so_far())
                        for h in range(2):
                            dve.wait_ge(rows_in[h].sem, rows_in[h].at(i + 1))
                            dve.wait_ge(side.sem, side.at(i * 6 + h + 1))
                            add(dve, steps_v, y[:, h, :, :], made_rows(h), x[:, h, :, :])
                            add(dve, steps_v, y[:, h, :, :], y[:, h, :, :], b_skip[:, :, :])
                            moment(h)
                        for h in range(2):
                            normed_to(0, h, x1)
                            add(dve, steps_v, y[:, h, :, :], x1[:, h, :, :], weights["L1_gnn_b3"][:, :, :])
                            moment(h)
                        for h in range(2):
                            normed_to(1, h, x2)
                            dve.sem_inc(ready.sem, 1)
                        for h in range(2):
                            dve.wait_ge(side.sem, side.at(i * 6 + 2 + h + 1))
                            dve.tensor_copy(y[:, h, :, :], made_rows(h)).then_inc(steps_v.one(), 1)
                            dve.wait_ge(steps_v.sem, steps_v.so_far())
                            leaky(dve, steps_v, g1[:, h, :, :], y[:, h, :, :])
                            dve.sem_inc(ready.sem, 1)
                        for h in range(2):
                            dve.wait_ge(side.sem, side.at(i * 6 + 4 + h + 1))
                            dve.tensor_copy(x1[:, h, :, :], made_rows(h)).then_inc(steps_v.one(), 1)
                            dve.wait_ge(steps_v.sem, steps_v.so_far())
                            leaky(dve, steps_v, y[:, h, :, :], x1[:, h, :, :])
                            add(dve, steps_v, y[:, h, :, :], y[:, h, :, :], x2[:, h, :, :])
                            moment(h, True)
                        for h in range(2):
                            if comes(i):
                                dve.wait_ge(stored[h].sem, stored[h].at(i))
                            normed_to(2, h, x4)
                            dve.sem_inc(results.sem, 1)
                    pairs(dve, steps_v, body, D_PAIRS)
            for s, m in ((once_in, 1 + K), (rows_in[0], D_PAIRS), (rows_in[1], D_PAIRS), (results, D_GROUPS), (stored[0], D_PAIRS),
                         (stored[1], D_PAIRS), (varied, 6 * D_PAIRS), (rooted, 6 * D_PAIRS), (ready, 4 * D_PAIRS), (side, 6 * D_PAIRS),
                         (side_turned, 6 * D_PAIRS), (side_turned_out, 6 * D_PAIRS)):
                s.spent(m)

        wctx.close()
        by_segment(attn_in[:, 2:3, :], 1, False, seg_z, False)
        with ExitStack() as st:
            pair_z = sb("pair_z", [P, TILES, 2], F32, st)
            src_z = sb("src_z", [P, TILES], F32, st)
            under = sb("under", [P, 2, K, 2], F32, st)
            idx = sb("idx_z", [P, 2, 1, K], I32, st)
            part = sb("part", [P, TILES], F32, st)
            with nc.Block() as block:
                @block.sync
                def _(sp):
                    sp.wait_ge(results.sem, results.at(1))
                    sp.dma_start(za_d[:, :].rearrange("(t p) c -> p t c", p=P), pair_z[:, :, :]).then_inc(once_out.sem, 16)
                    sp.wait_ge(once_out.sem, once_out.at(1))

                @block.gpsimd
                def _(pool):
                    pool.wait_ge(once_out.sem, once_out.at(1))
                    pool.sem_inc(issued, 1)

                    def body(i):
                        for h in range(2):
                            n = i * 2 + h
                            pool.wait_ge(ready.sem, ready.at(n + 1))
                            pool.sem_inc(issued, 1)
                            gather(pool, i, h, [(src_row, za_d[:, :], SLOTS, under[:, h, :, :])], idx, 1)
                    pairs(pool, steps_g, body)

                @block.vector
                def _(dve):
                    dve.tensor_copy(pair_z[:, :, 0], attn_in[:, 1, :]).then_inc(steps_v.one(), 1)
                    dve.tensor_copy(pair_z[:, :, 1], attn_in[:, 2, :]).then_inc(steps_v.one(), 1)
                    dve.memset(under[:, :, :, :], 0.0).then_inc(steps_v.one(), 1)
                    dve.wait_ge(steps_v.sem, steps_v.so_far())
                    dve.sem_inc(results.sem, 1)
                    for c in range(2):
                        dve.tensor_scalar(part[:, :], recs[:, :, 4], w_small[:, 2 * c + 1:2 * c + 2], None, ALU.mult).then_inc(steps_v.one(), 1)
                        dve.wait_ge(steps_v.sem, steps_v.so_far())
                        dve.scalar_tensor_tensor(edge_x[:, c, :], recs[:, :, 3], w_small[:, 2 * c:2 * c + 1], part[:, :], ALU.mult, ALU.add).then_inc(steps_v.one(), 1)
                        dve.wait_ge(steps_v.sem, steps_v.so_far())
                    dve.scalar_tensor_tensor(logits[:, 0, :], edge_x[:, 0, :], w_small[:, 4:5], seg_z[:, 0, :], ALU.mult, ALU.add).then_inc(steps_v.one(), 1)
                    dve.wait_ge(steps_v.sem, steps_v.so_far())
                    dve.scalar_tensor_tensor(logits[:, 0, :], edge_x[:, 1, :], w_small[:, 5:6], logits[:, 0, :], ALU.mult, ALU.add).then_inc(steps_v.one(), 1)
                    dve.wait_ge(steps_v.sem, steps_v.so_far())
                    steps_v.end(0)

                    def take(i, h, n):
                        dve.wait_ge(gathered[h].sem, gathered[h].at(K * (i + 1)))
                        dve.tensor_scalar(src_z[:, bass.ds(n * K, K)], under[:, h, :, 0], 0.0, None, ALU.add).then_inc(inputs_read.sem, 1)

                    def body(i):
                        for h in range(2):
                            n = i * 2 + h
                            if comes(n - 1):
                                dve.wait_ge(inputs_read.sem, inputs_read.at(n - 1))
                            dve.tensor_scalar(under[:, h, :, 0], attn_in[:, 0, bass.ds(n * K, K)], 0.0, None, ALU.add).then_inc(ready.sem, 1)
                            if not (isinstance(n, int) and n == 0):
                                take(i if h else i - 1, 1 - h, n - 1)
                    pairs(dve, None, body)
                    take(PAIRS - 1, 1, GROUPS - 1)
                    dve.wait_ge(inputs_read.sem, inputs_read.at(GROUPS))
                    add(dve, steps_v, logits[:, 0, :], logits[:, 0, :], src_z[:, :])
                    dve.scalar_tensor_tensor(logits[:, 0, :], logits[:, 0, :], 0.01, logits[:, 0, :], ALU.mult, ALU.max).then_inc(steps_v.one(), 1)
                    dve.wait_ge(steps_v.sem, steps_v.so_far())
                    steps_v.end(0)
            for s, m in ((results, 1), (once_out, 1), (ready, GROUPS), (gathered[0], K * PAIRS), (gathered[1], K * PAIRS), (inputs_read, GROUPS)):
                s.spent(m)
        by_segment(logits, 1, True, seg_a, False)

        with ExitStack() as st:
            w_e2n = sb("w_e2n", [P, 2], F32, st)
            e2n_row = sb("e2n_row", [P, 2, P], F32, st)
            e2n = sb("e2n", [P, 2, D], F32, st)
            trio = sb("trio", [P, TILES, 3], F32, st)
            prob = sb("prob", [P, TILES], F32, st)
            same = sb("same_z", [P, 2, G], F32, st)
            carry = sb("carry_z", [1, 2, G], F32, st)
            x3 = sb("x3_z", [P, 2, K, D], F32, st)
            terms = sb("terms_z", [P, 2, K, 4], F32, st)
            sums = sb("sums_z", [P, 2, K, 4], F32, st)
            den = sb("den_z", [P, K], F32, st)
            mean2 = sb("mean2", [P, K, 2], F32, st)
            y = sb("y_z", [P, K, D], F32, st)
            x4 = sb("x4_z", [P, 2, K, D], F32, st)
            stats = sb("stats_z", [P, K, 6], F32, st)
            moments = sb("moments_z", [P, K, 2], F32, st)
            spread = sb("spread_z", [P, K], F32, st)
            idx = sb("idx_o", [P, 2, K], I32, st)
            with ExitStack() as ps, nc.Block() as block:
                z_ps = [ps.enter_context(nc.psum_tensor(f"z_ps{s}", [P, 512], F32)) for s in range(K)]
                wz_ps = ps.enter_context(nc.psum_tensor("wz_ps", [P, 512], F32))
                IN = 3

                @block.sync
                def _(sp):
                    sp.dma_start(w_e2n[:, :], a["L3_gnn_w_e2n"][:, :]).then_inc(once_in.sem, 16)

                    def body(i):
                        for h in range(2):
                            n = i * 2 + h
                            if comes(n - 1):
                                sp.wait_ge(pe_read.sem, pe_read.at(n - 1))
                            sp.sem_inc(issued, 1)
                            if comes(n - 1):
                                sp.wait_ge(inputs_read.sem, inputs_read.at(n - 1))
                            sp.sem_inc(issued, 1)
                            sp.dma_start(x3[:, h, :, :], tile_rows(x3d_d, n)).then_inc(rows_in[h].sem, 16)
                            sp.dma_start(same[:, h, :], same_d[bass.ds(n, 1), :, :].rearrange("g p m -> p (g m)")).then_inc(rows_in[h].sem, 16)
                            sp.dma_start(carry[0:1, h, :], carry_d[bass.ds(n, 1), :]).then_inc(rows_in[h].sem, 16)
                    pairs(sp, None, body)

                @block.gpsimd
                def _(pool):
                    def body(i):
                        for h in range(2):
                            n = i * 2 + h
                            pool.wait_ge(results.sem, results.at(n + 1))
                            if comes(K * i):
                                pool.wait_ge(scattered[h].sem, scattered[h].at(K * i))
                            pool.sem_inc(issued, 1)
                            pool.tensor_copy(idx[:, h, :], out_row[:, bass.ds(n * K, K)]).then_inc(steps_g.one(), 1)
                            pool.wait_ge(steps_g.sem, steps_g.so_far())
                            pool.sem_inc(issued, 1)
                            for k in range(K):
                                pool.indirect_dma_start(
                                    out=out[:, :], out_offset=bass.IndirectOffsetOnAxis(ap=idx[:, h, k:k + 1], axis=0),
                                    in_=x4[:, h, k, :], in_offset=None,
                                    bounds_check=N - 1, oob_is_err=False).then_inc(scattered[h].sem, 16)
                    pairs(pool, steps_g, body)
                    for h in range(2):
                        pool.wait_ge(scattered[h].sem, scattered[h].at(K * PAIRS))

                @block.tensor
                def _(pe):
                    pe.wait_ge(ready.sem, ready.at(1))
                    for c in range(2):
                        mm = pe.matmul(wz_ps[:, c * D:(c + 1) * D], e2n_row[:, c, :], ident[:, :], start=True, stop=True)
                    mm.then_inc(turned.sem, 1)

                    def body(i):
                        for h in range(2):
                            n = i * 2 + h
                            pe.wait_ge(rows_in[h].sem, rows_in[h].at(IN * (i + 1)))
                            pe.wait_ge(terms_ready.sem, terms_ready.at(n + 1))
                            for k in range(K):
                                t = slice(k * P, (k + 1) * P)
                                before = sums[0:1, h, k - 1, :] if k else sums[0:1, 1 - h, K - 1, :]
                                if comes(n * K + k):
                                    pe.wait_ge(sums_out.sem, sums_out.at(n * K + k))
                                pe.matmul(z_ps[k][:, 0:4], same[:, h, t], terms[:, h, k, :], start=True, stop=False)
                                pe.matmul(z_ps[k][:, 0:4], carry[0:1, h, t], before, start=False, stop=True).then_inc(summed.sem, 1)
                            pe.drain().then_inc(pe_read.sem, 1)
                    pairs(pe, None, body)

                @block.scalar
                def _(act):
                    act.wait_ge(consts.sem, consts.at(1))
                    act.activation(prob[:, :], seg_a[:, 0, :], ACT.Exp).then_inc(cos_ready.sem, 1)

                    def body(i):
                        for h in range(2):
                            act.wait_ge(varied.sem, varied.at(i * 2 + h + 1))
                            act.activation(spread[:, :], spread[:, :], ACT.Sqrt).then_inc(rooted.sem, 1)
                    pairs(act, None, body)

                @block.vector
                def _(dve):
                    add(dve, steps_v, seg_a[:, 0, :], logits[:, 0, :], seg_a[:, 0, :], ALU.subtract)
                    dve.sem_inc(consts.sem, 1)
                    dve.wait_ge(once_in.sem, once_in.at(1))
                    dve.tensor_copy(e2n_row[:, :, :], w_e2n[:, :].unsqueeze(2).to_broadcast([P, 2, P])).then_inc(steps_v.one(), 1)
                    dve.memset(sums[:, :, :, :], 0.0).then_inc(steps_v.one(), 1)
                    dve.memset(terms[:, :, :, :], 0.0).then_inc(steps_v.one(), 1)
                    dve.wait_ge(steps_v.sem, steps_v.so_far())
                    dve.sem_inc(ready.sem, 1)
                    dve.wait_ge(turned.sem, turned.at(1))
                    dve.tensor_copy(e2n[:, :, :].rearrange("p c d -> p (c d)"), wz_ps[:, 0:2 * D]).then_inc(steps_v.one(), 1)
                    dve.wait_ge(cos_ready.sem, cos_ready.at(1))
                    for c in range(2):
                        dve.tensor_tensor(trio[:, :, c], edge_x[:, c, :], prob[:, :], ALU.mult).then_inc(steps_v.one(), 1)
                    dve.tensor_copy(trio[:, :, 2], prob[:, :]).then_inc(steps_v.one(), 1)
                    dve.wait_ge(steps_v.sem, steps_v.so_far())
                    steps_v.end(0)

                    def body(i):
                        for h in range(2):
                            n = i * 2 + h
                            if comes(n - 1):
                                dve.wait_ge(pe_read.sem, pe_read.at(n - 1))
                            dve.wait_ge(steps_v.sem, steps_v.so_far())
                            dve.tensor_scalar(terms[:, h, :, 0:3], trio[:, bass.ds(n * K, K), :], 0.0, None, ALU.add).then_inc(steps_v.one(), 1)
                            dve.wait_ge(steps_v.sem, steps_v.so_far())
                            dve.sem_inc(terms_ready.sem, 1)
                            for k in range(K):
                                dve.wait_ge(summed.sem, summed.at(n * K + k + 1))
                                dve.tensor_copy(sums[:, h, k, :], z_ps[k][:, 0:4]).then_inc(sums_out.sem, 1)
                            if comes(n * K + K):
                                dve.wait_ge(sums_out.sem, sums_out.at(n * K + K))
                            dve.wait_ge(rows_in[h].sem, rows_in[h].at(IN * (i + 1)))
                            dve.tensor_scalar(den[:, :], sums[:, h, :, 2], 1e-16, None, ALU.max).then_inc(steps_v.one(), 1)
                            dve.wait_ge(steps_v.sem, steps_v.so_far())
                            dve.reciprocal(den[:, :], den[:, :]).then_inc(steps_v.one(), 1)
                            dve.wait_ge(steps_v.sem, steps_v.so_far())
                            add(dve, steps_v, mean2[:, :, :], sums[:, h, :, 0:2], den[:, :].unsqueeze(2).to_broadcast([P, K, 2]), ALU.mult)
                            for c in range(2):
                                for k in range(K):
                                    under_row = x3[:, h, k, :] if c == 0 else y[:, k, :]
                                    dve.scalar_tensor_tensor(y[:, k, :], e2n[:, c, :], mean2[:, k, c:c + 1], under_row, ALU.mult, ALU.add).then_inc(steps_v.one(), 1)
                                dve.wait_ge(steps_v.sem, steps_v.so_far())
                            if comes(K * i):
                                dve.wait_ge(scattered[h].sem, scattered[h].at(K * i))
                            norm(dve, lambda k: y[:, k, :], lambda k: x4[:, h, k, :], stats, moments, spread, K, n + 1, steps_v)
                            dve.wait_ge(steps_v.sem, steps_v.so_far())
                            dve.sem_inc(results.sem, 1)
                            dve.sem_inc(inputs_read.sem, 1)
                    pairs(dve, steps_v, body)


_OUT = ((N, D), "float32")
_TURNED = ["L2_gnn_W1_0", "L2_gnn_W2_0", "L2_gnn_W3_0", "L2_gnn_W1_1", "L2_gnn_W2_1", "L2_gnn_W3_1"]


def kernel(**inputs):
    import concourse.bacc as _bacc
    from concourse.bass_utils import run_bass_kernel_spmd as _run

    nc = _bacc.Bacc("TRN2", target_bir_lowering=False, num_devices=1)
    arrays, a = {}, {}
    for name, x in inputs.items():
        x = np.ascontiguousarray(np.asarray(x).T if name in _TURNED else x)
        arrays[f"in_{name}"] = x
        a[name] = nc.dram_tensor(f"in_{name}", x.shape, mybir.dt.from_np(x.dtype), kind="ExternalInput").ap()
    out = nc.dram_tensor("out_0", _OUT[0], F32, kind="ExternalOutput").ap()
    graph_kernel(nc, a, out)
    r = _run(nc, [arrays], core_ids=[0])
    return r.results[0]["out_0"]
```

```python
from contextlib import ExitStack

import numpy as np

import concourse.bass as bass
from concourse import mybir

F32 = mybir.dt.float32
BF16 = mybir.dt.bfloat16
I32 = mybir.dt.int32
ALU = mybir.AluOpType
ACT = mybir.ActivationFunctionType
AX = mybir.AxisListType

N = 50000
E = 25000
D = 128
P = 128
TILES = 200
SLOTS = TILES * P
K = 4
GROUPS = TILES // K
PAIRS = GROUPS // 2
SLOTS_IN = 4
G = K * P
LOAD_P = E // TILES
HI = (N + P) // P
TABLE = HI * P
REC = 8
ROW = D + REC
NONE = SLOTS
FAR = 1 << 20
EPS = 1e-5
SLOPE = (1.0 / 8.0 + 1.0 / 3.0) / 2.0
BIG = 1e38
TWO_PI_HI = 6.28125
TWO_PI_LO = float(2 * np.pi - 6.28125)
ROUND = 12582912.0
PI_IN = 3.1415925


class Signal:

    def __init__(self, nc, ctx, name, step=1):
        self.sem = ctx.enter_context(nc.semaphore(name))
        self.step, self.base = step, 0

    def at(self, events):
        return events * self.step + self.base

    def spent(self, events):
        self.base += events * self.step


def comes(events):
    return not (isinstance(events, int) and events <= 0)


class Steps:

    def __init__(self, nc, ctx, name):
        self.sem = ctx.enter_context(nc.semaphore(name))
        self.base, self.i, self.j, self.per = 0, 0, 0, 0

    def begin(self, i):
        self.i, self.j = i, 0

    def one(self):
        self.j += 1
        return self.sem

    def so_far(self):
        if isinstance(self.i, int) and self.i == 0:
            return self.base + self.j
        return self.i * self.per + (self.base + self.j)

    def left(self, full):
        self.base += full * self.per + self.j
        self.i, self.j = 0, 0

    def end(self, rounds):
        self.base += rounds * self.per if rounds else self.j
        self.i, self.j = 0, 0


def pairs(eng, steps, body, rounds=PAIRS):
    if steps:
        steps.begin(0)
    body(0)
    if steps:
        steps.per = steps.j
    with eng.Fori(1, rounds - 1) as i:
        if steps:
            steps.begin(i)
        body(i)
    if steps:
        assert steps.j == steps.per
        steps.begin(rounds - 1)
    body(rounds - 1)
    if steps:
        steps.end(rounds)


def rounds(eng, steps, body, slots):
    full, left = GROUPS // slots, GROUPS % slots
    assert left
    if steps:
        steps.begin(0)
    body(0, range(slots))
    if steps:
        steps.per = steps.j
    with eng.Fori(1, full) as i:
        if steps:
            steps.begin(i)
        body(i, range(slots))
    if steps:
        assert steps.j == steps.per
        steps.begin(full)
    body(full, range(left))
    if steps:
        steps.left(full)


def graph_kernel(nc, a, out):
    ctx = ExitStack()
    with ctx:
        def sb(name, shape, dt=F32, c=ctx):
            return c.enter_context(nc.sbuf_tensor(name, shape, dt))

        def dram(name, shape, dt=F32):
            return nc.dram_tensor(name, shape, dt, kind="Internal").ap()

        def signal(name, step=1):
            return Signal(nc, ctx, name, step)

        rows_d = dram("rows_d", [SLOTS, ROW])
        table_d = dram("table_d", [TABLE, 4])
        same_d = dram("same_d", [GROUPS, P, G])
        carry_d = dram("carry_d", [GROUPS, G])
        node_d = dram("node_d", [1, SLOTS + 2])
        val_d = dram("val_d", [2, SLOTS])
        seg_d = dram("seg_d", [2, SLOTS])
        v_d = dram("v_d", [SLOTS, D])
        xbd_d = dram("xbd_d", [SLOTS, D])
        xbs_d = dram("xbs_d", [SLOTS, D])
        x1d_d = dram("x1d_d", [SLOTS, D])
        x1s_d = dram("x1s_d", [SLOTS, D])
        x1g_d = dram("x1g_d", [SLOTS, D])
        agg1_d = dram("agg1_d", [SLOTS + 8, D])
        agg2_d = dram("agg2_d", [SLOTS + 8, D])
        h1_d = dram("h1_d", [SLOTS, D])
        x2d_d = dram("x2d_d", [SLOTS, D])
        x2s_d = dram("x2s_d", [SLOTS, D])
        x2g_d = dram("x2g_d", [SLOTS, D])
        g1d_d = dram("g1d_d", [SLOTS, D])
        g1s_d = dram("g1s_d", [SLOTS, D])
        x3d_d = dram("x3d_d", [SLOTS, D])
        za_d = dram("za_d", [SLOTS, 2])

        ident = sb("ident", [P, P])
        ident_b = sb("ident_b", [P, P], BF16)
        ones = sb("ones", [P, P])
        below = sb("below", [P, P])
        upto = sb("upto", [P, P])
        above = sb("above", [P, P])
        last_lane = sb("last_lane", [P, P])
        recs = sb("recs", [P, TILES, REC])
        dst_next = sb("dst_next", [P, TILES + 1])
        src_tab = sb("src_tab", [P, TILES, 4])
        src_id = sb("src_id", [P, TILES], I32)
        dst_id = sb("dst_id", [P, TILES], I32)
        src_row = sb("src_row", [P, TILES], I32)
        out_row = sb("out_row", [P, TILES], I32)
        ns = sb("ns", [P, TILES])
        nd = sb("nd", [P, TILES])
        inv_deg = sb("inv_deg", [P, TILES])
        alpha = sb("alpha", [P, 2, TILES])
        segmax = sb("segmax", [P, 2, TILES])

        steps_v = Steps(nc, ctx, "vector_steps")
        steps_a = Steps(nc, ctx, "scalar_steps")
        steps_g = Steps(nc, ctx, "pool_steps")
        issued = ctx.enter_context(nc.semaphore("pool_issue"))
        consts = signal("consts")
        once_in = signal("once_in", 16)
        once_out = signal("once_out", 16)
        rows_in = [signal(f"rows_in{h}", 16) for h in range(SLOTS_IN)]
        gathered = [signal(f"gathered{h}", 16) for h in range(SLOTS_IN)]
        scattered = [signal(f"scattered{h}", 16) for h in range(2)]
        stored = [signal(f"stored{h}", 16) for h in range(SLOTS_IN)]
        inputs_read = signal("inputs_read")
        pe_read = signal("pe_read")
        results = signal("results")

        with nc.Block() as block:
            @block.gpsimd
            def _(pool):
                for m in (ident, ident_b, last_lane):
                    pool.memset(m[:, :], 0.0).then_inc(steps_g.one(), 1)
                for m in (ones, below, upto, above):
                    pool.memset(m[:, :], 1.0).then_inc(steps_g.one(), 1)
                pool.wait_ge(steps_g.sem, steps_g.so_far())
                for m in (ident, ident_b):
                    pool.affine_select(out=m[:, :], in_=m[:, :], compare_op=ALU.not_equal, fill=1.0,
                                                   base=0, pattern=[[-1, P]], channel_multiplier=1).then_inc(steps_g.one(), 1)
                pool.affine_select(out=below[:, :], in_=below[:, :], compare_op=ALU.is_gt, fill=0.0,
                                               base=0, pattern=[[-1, P]], channel_multiplier=1).then_inc(steps_g.one(), 1)
                pool.affine_select(out=upto[:, :], in_=upto[:, :], compare_op=ALU.is_ge, fill=0.0,
                                               base=0, pattern=[[-1, P]], channel_multiplier=1).then_inc(steps_g.one(), 1)
                pool.affine_select(out=above[:, :], in_=above[:, :], compare_op=ALU.is_gt, fill=0.0,
                                               base=0, pattern=[[1, P]], channel_multiplier=-1).then_inc(steps_g.one(), 1)
                pool.affine_select(out=last_lane[:, :], in_=last_lane[:, :], compare_op=ALU.not_equal,
                                               fill=1.0, base=-(P - 1), pattern=[[0, P]], channel_multiplier=1).then_inc(steps_g.one(), 1)
                pool.wait_ge(steps_g.sem, steps_g.so_far())
                steps_g.end(0)

        with ExitStack() as st:
            given = sb("given", [P, TILES, REC], F32, st)
            node_i = sb("node_i", [P, 2, TILES], I32, st)
            part_i = sb("part_i", [P, 4, TILES], I32, st)
            part_f = sb("part_f", [P, 4, TILES], F32, st)
            lanes_i = sb("lanes_i", [P, HI], I32, st)
            lanes = sb("lanes", [P, HI], F32, st)
            ew = sb("ew", [P, TILES], F32, st)
            e2 = sb("e2", [P, TILES, 2], F32, st)
            count = sb("count", [P, 2, HI], F32, st)
            start = sb("start", [P, HI], F32, st)
            cols = sb("cols", [P, 4, 8], F32, st)
            hot_lo = sb("hot_lo", [P, 8, 2, P], BF16, st)
            hot_hi = sb("hot_hi", [P, 8, 2, HI + 1], BF16, st)
            hot_ready = signal("hot_ready")
            hot_used = signal("hot_used")
            counted = signal("counted")
            added = signal("added")

            ps = ExitStack()
            with ps, nc.Block() as block:
                c_ps = [ps.enter_context(nc.psum_tensor(f"c_ps{s}", [P, 512], F32)) for s in range(2)]

                @block.sync
                def _(sp):
                    sp.wait_ge(consts.sem, consts.at(1))
                    sp.dma_start(node_i[0:LOAD_P, 0, :], a["dst"].rearrange("(p t) -> p t", t=TILES)).then_inc(once_in.sem, 16)
                    sp.dma_start(node_i[0:LOAD_P, 1, :], a["src"].rearrange("(p t) -> p t", t=TILES)).then_inc(once_in.sem, 16)
                    sp.dma_start(ew[0:LOAD_P, :], a["edge_weight"].rearrange("(p t) -> p t", t=TILES)).then_inc(once_in.sem, 16)
                    sp.dma_start(e2[0:LOAD_P, :, :], a["edge_attr_2"].rearrange("(p t) c -> p t c", t=TILES)).then_inc(once_in.sem, 16)

                @block.gpsimd
                def _(pool):
                    pool.iota(lanes_i[:, :], pattern=[[1, HI]], base=0, channel_multiplier=0).then_inc(steps_g.one(), 1)
                    pool.wait_ge(steps_g.sem, steps_g.so_far())
                    steps_g.end(0)

                @block.vector
                def _(dve):
                    dve.memset(node_i[:, :, :], N).then_inc(steps_v.one(), 1)
                    dve.memset(ew[:, :], 0.0).then_inc(steps_v.one(), 1)
                    dve.memset(e2[:, :, :], 0.0).then_inc(steps_v.one(), 1)
                    dve.memset(given[:, :, :], 0.0).then_inc(steps_v.one(), 1)
                    dve.wait_ge(steps_v.sem, steps_v.so_far())
                    dve.memset(count[:, :, :], 0.0).then_inc(consts.sem, 1)
                    dve.wait_ge(once_in.sem, once_in.at(4))
                    for s in range(2):
                        dve.tensor_single_scalar(part_i[:, 2 * s, :], node_i[:, s, :], P - 1, ALU.bitwise_and).then_inc(steps_v.one(), 1)
                        dve.tensor_single_scalar(part_i[:, 2 * s + 1, :], node_i[:, s, :], 7, ALU.logical_shift_right).then_inc(steps_v.one(), 1)
                    dve.wait_ge(steps_g.sem, steps_g.base)
                    dve.tensor_copy(lanes[:, :], lanes_i[:, :]).then_inc(steps_v.one(), 1)
                    dve.tensor_copy(given[:, :, 0], node_i[:, 1, :]).then_inc(steps_v.one(), 1)
                    dve.tensor_copy(given[:, :, 1], node_i[:, 0, :]).then_inc(steps_v.one(), 1)
                    dve.tensor_copy(given[:, :, 2], ew[:, :]).then_inc(steps_v.one(), 1)
                    dve.tensor_copy(given[:, :, 3:5], e2[:, :, :]).then_inc(steps_v.one(), 1)
                    dve.wait_ge(steps_v.sem, steps_v.so_far())
                    dve.tensor_copy(part_f[:, :, :], part_i[:, :, :]).then_inc(steps_v.one(), 1)
                    dve.wait_ge(steps_v.sem, steps_v.so_far())
                    steps_v.end(0)

                    def body(i):
                        if comes(i * 8):
                            dve.wait_ge(hot_used.sem, hot_used.at(i * 8))
                        dve.tensor_scalar(cols[:, :, :], part_f[:, :, bass.ds(i * 8, 8)], 0.0, None, ALU.add).then_inc(steps_v.one(), 1)
                        dve.wait_ge(steps_v.sem, steps_v.so_far())
                        for k in range(8):
                            for s in range(2):
                                dve.tensor_scalar(hot_lo[:, k, s, :], lanes[:, 0:P], cols[:, 2 * s, k:k + 1], None, ALU.is_equal)
                                hot = dve.tensor_scalar(hot_hi[:, k, s, 0:HI], lanes[:, :], cols[:, 2 * s + 1, k:k + 1], None, ALU.is_equal)
                                hot.then_inc(hot_ready.sem, 1)
                        dve.wait_ge(hot_used.sem, hot_used.at(i * 8 + 8))
                        for s in range(2):
                            dve.tensor_tensor(count[:, s, :], count[:, s, :], c_ps[s][:, 0:HI], ALU.add).then_inc(steps_v.one(), 1)
                        dve.wait_ge(steps_v.sem, steps_v.so_far())
                        dve.sem_inc(added.sem, 1)
                    pairs(dve, steps_v, body)

                @block.tensor
                def _(pe):
                    def body(i):
                        if comes(i):
                            pe.wait_ge(added.sem, added.at(i))
                        for k in range(8):
                            pe.wait_ge(hot_ready.sem, hot_ready.at(i * 16 + 2 * k + 2))
                            for s in range(2):
                                mm = pe.matmul(c_ps[s][:, 0:HI], hot_lo[:, k, s, :], hot_hi[:, k, s, 0:HI],
                                               start=(k == 0), stop=(k == 7))
                            mm.then_inc(hot_used.sem, 1)
                    pairs(pe, None, body)
            for s, n in ((consts, 1), (once_in, 4), (hot_ready, 2 * TILES), (hot_used, TILES), (added, PAIRS)):
                s.spent(n)

            total = sb("total", [P, HI], F32, st)
            upto_hi = sb("upto_hi", [P, HI], F32, st)
            ones_hi = sb("ones_hi", [P, HI], F32, st)
            place_i = sb("place_i", [P, HI], I32, st)
            tile_f = sb("tile_f", [P, HI], F32, st)
            head = sb("head", [P, HI], F32, st)
            has = sb("has", [P, HI], F32, st)
            vec = sb("vec", [P, 4, P], F32, st)
            tab = sb("tab", [P, 4, P, 4], F32, st)
            CH = [(c, min(P, HI - c * P)) for c in range(4)]
            FULL = (N // P) - 3 * P
            turned = signal("turned")
            turned_out = signal("turned_out")
            ps = ExitStack()
            with ps, nc.Block() as block:
                tot_ps = ps.enter_context(nc.psum_tensor("tot_ps", [P, 512], F32))
                pre_ps = ps.enter_context(nc.psum_tensor("pre_ps", [P, 512], F32))
                tr_ps = [ps.enter_context(nc.psum_tensor(f"tr_ps{s}", [P, 512], F32)) for s in range(3)]

                @block.sync
                def _(sp):
                    sp.wait_ge(consts.sem, consts.at(1))
                    sp.dma_start(vec[:, 0:3, :], a["node_vec"][0:3 * P * P].rearrange("(c p l) -> p c l", c=3, l=P)).then_inc(once_in.sem, 16)
                    sp.dma_start(vec[0:FULL, 3, :], a["node_vec"][3 * P * P:(3 * P + FULL) * P].rearrange("(p l) -> p l", l=P)).then_inc(once_in.sem, 16)
                    sp.dma_start(vec[FULL:FULL + 1, 3, 0:N % P], a["node_vec"][(3 * P + FULL) * P:N].rearrange("(p l) -> p l", p=1)).then_inc(once_in.sem, 16)
                    sp.wait_ge(results.sem, results.at(1))
                    for c, w in CH:
                        sp.dma_start(table_d[c * P * P:(c * P + w) * P, :].rearrange("(p l) f -> p (l f)", l=P),
                                     tab[0:w, c, :, :].rearrange("p l f -> p (l f)")).then_inc(once_out.sem, 16)
                    sp.wait_ge(once_out.sem, once_out.at(4))

                @block.tensor
                def _(pe):
                    pe.matmul(tot_ps[:, 0:HI], ones[:, :], count[:, 0, :], start=True, stop=True)
                    pe.matmul(pre_ps[:, 0:HI], above[:, :], count[:, 0, :], start=True, stop=True).then_inc(turned.sem, 1)
                    pe.wait_ge(turned_out.sem, turned_out.at(1))
                    for s, m in enumerate((head[:, :], count[:, 0, :], count[:, 1, :])):
                        for c, w in CH:
                            mm = pe.transpose(tr_ps[s][0:w, c * P:(c + 1) * P], m[:, c * P:c * P + w], ident[:, :])
                        mm.then_inc(turned.sem, 1)

                @block.vector
                def _(dve):
                    dve.memset(vec[:, :, :], 0.0).then_inc(steps_v.one(), 1)
                    dve.memset(ones_hi[:, :], 1.0).then_inc(steps_v.one(), 1)
                    dve.wait_ge(steps_v.sem, steps_v.so_far())
                    dve.sem_inc(consts.sem, 1)
                    dve.wait_ge(turned.sem, turned.at(1))
                    dve.tensor_copy(total[:, :], tot_ps[:, 0:HI]).then_inc(steps_v.one(), 1)
                    dve.wait_ge(steps_v.sem, steps_v.so_far())
                    dve.tensor_tensor_scan(upto_hi[:, :], total[:, :], ones_hi[:, :], 0.0, ALU.add, ALU.mult).then_inc(steps_v.one(), 1)
                    dve.wait_ge(steps_v.sem, steps_v.so_far())
                    dve.tensor_tensor(start[:, :], upto_hi[:, :], total[:, :], ALU.subtract).then_inc(steps_v.one(), 1)
                    dve.wait_ge(steps_v.sem, steps_v.so_far())
                    dve.tensor_tensor(start[:, :], start[:, :], pre_ps[:, 0:HI], ALU.add).then_inc(steps_v.one(), 1)
                    dve.wait_ge(steps_v.sem, steps_v.so_far())
                    dve.tensor_copy(place_i[:, :], start[:, :]).then_inc(steps_v.one(), 1)
                    dve.wait_ge(steps_v.sem, steps_v.so_far())
                    dve.tensor_single_scalar(place_i[:, :], place_i[:, :], 7, ALU.logical_shift_right).then_inc(steps_v.one(), 1)
                    dve.wait_ge(steps_v.sem, steps_v.so_far())
                    dve.tensor_copy(tile_f[:, :], place_i[:, :]).then_inc(steps_v.one(), 1)
                    dve.tensor_scalar(has[:, :], count[:, 0, :], 0.5, None, ALU.is_ge).then_inc(steps_v.one(), 1)
                    dve.wait_ge(steps_v.sem, steps_v.so_far())
                    dve.scalar_tensor_tensor(head[:, :], tile_f[:, :], -2.0 * P, start[:, :], ALU.mult, ALU.add).then_inc(steps_v.one(), 1)
                    dve.wait_ge(steps_v.sem, steps_v.so_far())
                    dve.tensor_scalar(head[:, :], head[:, :], float((TILES - 1) * P - NONE), None, ALU.add).then_inc(steps_v.one(), 1)
                    dve.wait_ge(steps_v.sem, steps_v.so_far())
                    dve.tensor_tensor(head[:, :], head[:, :], has[:, :], ALU.mult).then_inc(steps_v.one(), 1)
                    dve.wait_ge(steps_v.sem, steps_v.so_far())
                    dve.tensor_scalar(head[:, :], head[:, :], float(NONE), None, ALU.add).then_inc(turned_out.sem, 1)
                    dve.wait_ge(once_in.sem, once_in.at(3))
                    dve.tensor_copy(tab[:, :, :, 3], vec[:, :, :])
                    for s in range(3):
                        dve.wait_ge(turned.sem, turned.at(2 + s))
                        for c, w in CH:
                            dve.tensor_copy(tab[0:w, c, :, s], tr_ps[s][0:w, c * P:(c + 1) * P]).then_inc(steps_v.one(), 1)
                    dve.wait_ge(steps_v.sem, steps_v.so_far())
                    dve.sem_inc(results.sem, 1)
                    steps_v.end(0)
            for s, n in ((consts, 1), (once_in, 3), (once_out, 4), (turned, 4), (turned_out, 1), (results, 1)):
                s.spent(n)

            row = sb("row", [P, 2, K, ROW], F32, st)
            lo_t = sb("lo_t", [P, 2, P], F32, st)
            run = sb("run", [P, 2, HI], F32, st)
            junk = sb("junk", [P, HI], F32, st)
            junk_r = sb("junk_r", [P, P], F32, st)
            colk = sb("colk", [P, 2, 3, K], F32, st)
            colb = sb("colb", [P, 2, K, P], F32, st)
            base = sb("base", [P, 2, K], F32, st)
            rank = sb("rank", [P, 2, K], F32, st)
            place = sb("place", [P, 2, K], F32, st)
            tile_i = sb("tile_i", [P, 2, K], I32, st)
            tile_k = sb("tile_k", [P, 2, K], F32, st)
            slot_i = sb("slot_i", [P, 2, K], I32, st)
            hot_t = signal("hot_t")
            run_sb = signal("run_sb")
            based = signal("based")
            base_read = signal("base_read")
            along = signal("along")
            ps = ExitStack()
            with ps, nc.Block() as block:
                t_ps = [ps.enter_context(nc.psum_tensor(f"t_ps{s}", [P, 1024], BF16)) for s in range(2)]
                r_ps = [ps.enter_context(nc.psum_tensor(f"r_ps{s}", [P, 512], F32)) for s in range(2)]
                a_ps = [ps.enter_context(nc.psum_tensor(f"a_ps{s}", [P, 512], F32)) for s in range(2)]
                run_ps = ps.enter_context(nc.psum_tensor("run_ps", [P, 512], F32))
                msg_v = a["edge_attr_128"].rearrange("(p t) d -> p t d", t=TILES)

                @block.sync
                def _(sp):
                    sp.wait_ge(consts.sem, consts.at(1))

                    def body(i):
                        for h in range(2):
                            if comes(i * K):
                                sp.wait_ge(scattered[h].sem, scattered[h].at(i * K))
                            sp.sem_inc(issued, 1)
                            sp.dma_start(row[0:LOAD_P, h, :, 0:D], msg_v[:, bass.ds(i * 2 * K + h * K, K), :]).then_inc(rows_in[h].sem, 16)
                    pairs(sp, None, body)

                @block.gpsimd
                def _(pool):
                    def body(i):
                        for h in range(2):
                            pool.wait_ge(results.sem, results.at(i * 2 + h + 1))
                            pool.wait_ge(rows_in[h].sem, rows_in[h].at(i + 1))
                            pool.sem_inc(issued, 1)
                            for k in range(K):
                                pool.indirect_dma_start(
                                    out=rows_d[:, :], out_offset=bass.IndirectOffsetOnAxis(ap=slot_i[:, h, k:k + 1], axis=0),
                                    in_=row[:, h, k, :], in_offset=None,
                                    bounds_check=SLOTS - 1, oob_is_err=False).then_inc(scattered[h].sem, 16)
                    pairs(pool, None, body)
                    for h in range(2):
                        pool.wait_ge(scattered[h].sem, scattered[h].at(PAIRS * K))

                @block.vector
                def _(dve):
                    dve.memset(row[:, :, :, :], 0.0).then_inc(steps_v.one(), 1)
                    dve.wait_ge(steps_v.sem, steps_v.so_far())
                    dve.sem_inc(consts.sem, 1)
                    steps_v.end(0)

                    def body(i):
                        for h in range(2):
                            if comes((i * 2 + h) * K - K):
                                dve.wait_ge(hot_used.sem, hot_used.at((i * 2 + h) * K - K))
                            dve.tensor_scalar(colk[:, h, 0, :], given[:, bass.ds(i * 2 * K + h * K, K), 1], 0.0, None, ALU.add).then_inc(steps_v.one(), 1)
                            dve.tensor_scalar(colk[:, h, 1:3, :], part_f[:, 0:2, bass.ds(i * 2 * K + h * K, K)], 0.0, None, ALU.add).then_inc(steps_v.one(), 1)
                            dve.wait_ge(steps_v.sem, steps_v.so_far())
                            dve.tensor_copy(colb[:, h, :, :], colk[:, h, 0, :].unsqueeze(2).to_broadcast([P, K, P])).then_inc(steps_v.one(), 1)
                            for k in range(K):
                                dve.tensor_scalar(hot_lo[:, 4 * h + k, 0, :], lanes[:, 0:P], colk[:, h, 1, k:k + 1], None, ALU.is_equal).then_inc(steps_v.one(), 1)
                                dve.tensor_scalar(hot_hi[:, 4 * h + k, 0, 0:HI], lanes[:, :], colk[:, h, 2, k:k + 1], None, ALU.is_equal).then_inc(hot_ready.sem, 1)
                            for k in range(K):
                                dve.wait_ge(along.sem, along.at((i * 2 + h) * K + k + 1))
                                dve.scalar_tensor_tensor(junk_r[:, :], r_ps[k % 2][:, 0:P], colk[:, h, 0, k:k + 1], below[:, :],
                                                                     ALU.is_equal, ALU.mult, accum_out=rank[:, h, k:k + 1]).then_inc(steps_v.one(), 1)
                                dve.wait_ge(based.sem, based.at((i * 2 + h) * K + k + 1))
                                dve.tensor_tensor_reduce(out=junk[:, :], in0=a_ps[k % 2][:, 0:HI], in1=hot_hi[:, 4 * h + k, 0, 0:HI],
                                                                     scale=1.0, scalar=0.0, op0=ALU.mult, op1=ALU.add,
                                                                     accum_out=base[:, h, k:k + 1]).then_inc(steps_v.one(), 1)
                                dve.wait_ge(steps_v.sem, steps_v.so_far())
                                dve.sem_inc(base_read.sem, 1)
                            dve.tensor_tensor(place[:, h, :], base[:, h, :], rank[:, h, :], ALU.add).then_inc(steps_v.one(), 1)
                            dve.wait_ge(steps_v.sem, steps_v.so_far())
                            dve.tensor_copy(tile_i[:, h, :], place[:, h, :]).then_inc(steps_v.one(), 1)
                            dve.wait_ge(steps_v.sem, steps_v.so_far())
                            dve.tensor_single_scalar(tile_i[:, h, :], tile_i[:, h, :], 7, ALU.logical_shift_right).then_inc(steps_v.one(), 1)
                            dve.wait_ge(steps_v.sem, steps_v.so_far())
                            dve.tensor_copy(tile_k[:, h, :], tile_i[:, h, :]).then_inc(steps_v.one(), 1)
                            dve.wait_ge(steps_v.sem, steps_v.so_far())
                            dve.scalar_tensor_tensor(place[:, h, :], tile_k[:, h, :], -2.0 * P, place[:, h, :], ALU.mult, ALU.add).then_inc(steps_v.one(), 1)
                            dve.wait_ge(steps_v.sem, steps_v.so_far())
                            if comes(i * K):
                                dve.wait_ge(scattered[h].sem, scattered[h].at(i * K))
                            dve.tensor_scalar(slot_i[:, h, :], place[:, h, :], float((TILES - 1) * P), None, ALU.add).then_inc(steps_v.one(), 1)
                            dve.tensor_scalar(row[:, h, :, D:ROW], given[:, bass.ds(i * 2 * K + h * K, K), :], 0.0, None, ALU.add).then_inc(steps_v.one(), 1)
                            dve.wait_ge(steps_v.sem, steps_v.so_far())
                            dve.sem_inc(results.sem, 1)
                    pairs(dve, steps_v, body)

                @block.tensor
                def _(pe):
                    pe.matmul(run_ps[:, 0:HI], ident[:, :], start[:, :], start=True, stop=True, skip_group_check=True).then_inc(turned.sem, 1)

                    def body(i):
                        for h in range(2):
                            for k in range(K):
                                n = (i * 2 + h) * K + k
                                pe.wait_ge(hot_ready.sem, hot_ready.at(n + 1))
                                if comes(n - 1):
                                    pe.wait_ge(base_read.sem, base_read.at(n - 1))
                                pe.transpose(t_ps[k % 2][:, 0:P], hot_lo[:, 4 * h + k, 0, :], ident_b[:, :]).then_inc(hot_t.sem, 1)
                                pe.matmul(r_ps[k % 2][:, 0:P], colb[:, h, k, :], ident[:, :], start=True, stop=True).then_inc(along.sem, 1)
                                pe.wait_ge(run_sb.sem, run_sb.at(n + 1))
                                pe.matmul(a_ps[k % 2][:, 0:HI], lo_t[:, k % 2, :], run[:, k % 2, :], start=True, stop=True).then_inc(based.sem, 1)
                                pe.matmul(run_ps[:, 0:HI], hot_lo[:, 4 * h + k, 0, :], hot_hi[:, 4 * h + k, 0, 0:HI],
                                          start=False, stop=True, skip_group_check=True).then_inc(hot_used.sem, 1)
                    pairs(pe, None, body)

                @block.scalar
                def _(act):
                    act.wait_ge(turned.sem, turned.at(1))

                    def body(i):
                        for h in range(2):
                            for k in range(K):
                                n = (i * 2 + h) * K + k
                                if comes(n - 1):
                                    act.wait_ge(based.sem, based.at(n - 1))
                                act.wait_ge(hot_t.sem, hot_t.at(n + 1))
                                act.copy(lo_t[:, k % 2, :], t_ps[k % 2][:, 0:P]).then_inc(steps_a.one(), 1)
                                if comes(n):
                                    act.wait_ge(hot_used.sem, hot_used.at(n))
                                act.copy(run[:, k % 2, :], run_ps[:, 0:HI]).then_inc(steps_a.one(), 1)
                                act.wait_ge(steps_a.sem, steps_a.so_far())
                                act.sem_inc(run_sb.sem, 1)
                    pairs(act, steps_a, body)
            for s, n in ((consts, 1), (rows_in[0], PAIRS), (rows_in[1], PAIRS), (scattered[0], PAIRS * K), (scattered[1], PAIRS * K),
                         (results, GROUPS), (hot_ready, TILES), (hot_used, TILES), (along, TILES), (based, TILES), (base_read, TILES),
                         (turned, 1), (hot_t, TILES), (run_sb, TILES)):
                s.spent(n)

        with ExitStack() as st:
            heads = sb("heads", [P, TILES], F32, st)
            last_dst = sb("last_dst", [P, TILES], F32, st)
            tabk = sb("tabk", [P, 2, K, 4], F32, st)
            idx = sb("idx", [P, 2, K], I32, st)
            dcol = sb("dcol", [P, 2, K], F32, st)
            dbef = sb("dbef", [P, 2, K], F32, st)
            drow = sb("drow", [P, 2, K, P], F32, st)
            same = sb("same", [P, 2, K, P], F32, st)
            carry = sb("carry", [1, 2, K, P], F32, st)
            eqs = sb("eqs", [P, 2, K], F32, st)
            slots_known = signal("slots_known")
            along4 = signal("along4")
            ps = ExitStack()
            with ps, nc.Block() as block:
                l_ps = ps.enter_context(nc.psum_tensor("l_ps", [P, 512], F32))
                e_ps = [ps.enter_context(nc.psum_tensor(f"e_ps{s}", [P, 512], F32)) for s in range(2)]

                @block.sync
                def _(sp):
                    sp.dma_start(recs[:, :, :], rows_d[:, D:ROW].rearrange("(t p) f -> p t f", p=P)).then_inc(once_in.sem, 16)

                    def body(i):
                        for h in range(2):
                            sp.wait_ge(results.sem, results.at(i * 2 + h + 1))
                            sp.sem_inc(issued, 1)
                            sp.dma_start(same_d[bass.ds(i * 2 + h, 1), :, :].rearrange("g p m -> p (g m)"),
                                         same[:, h, :, :].rearrange("p k m -> p (k m)")).then_inc(stored[h].sem, 16)
                            sp.dma_start(carry_d[bass.ds(i * 2 + h, 1), :],
                                         carry[0:1, h, :, :].rearrange("p k m -> p (k m)")).then_inc(stored[h].sem, 16)
                    pairs(sp, None, body)
                    for h in range(2):
                        sp.wait_ge(stored[h].sem, stored[h].at(2 * PAIRS))

                @block.gpsimd
                def _(pool):
                    pool.wait_ge(slots_known.sem, slots_known.at(1))

                    def body(i):
                        for h in range(2):
                            if comes(i * K):
                                pool.wait_ge(gathered[h].sem, gathered[h].at(i * K))
                            if comes(i * 2 + h - 1):
                                pool.wait_ge(inputs_read.sem, inputs_read.at(i * 2 + h - 1))
                            pool.sem_inc(issued, 1)
                            pool.tensor_copy(idx[:, h, :], src_id[:, bass.ds(i * 2 * K + h * K, K)]).then_inc(steps_g.one(), 1)
                            pool.wait_ge(steps_g.sem, steps_g.so_far())
                            pool.sem_inc(issued, 1)
                            for k in range(K):
                                pool.indirect_dma_start(
                                    out=tabk[:, h, k, :], out_offset=None, in_=table_d[:, :],
                                    in_offset=bass.IndirectOffsetOnAxis(ap=idx[:, h, k:k + 1], axis=0),
                                    bounds_check=TABLE - 1, oob_is_err=False).then_inc(gathered[h].sem, 16)
                    pairs(pool, steps_g, body)

                @block.vector
                def _(dve):
                    dve.wait_ge(once_in.sem, once_in.at(1))
                    dve.memset(dst_next[:, 0:1], -1.0).then_inc(steps_v.one(), 1)
                    dve.tensor_copy(dst_next[:, 1:TILES + 1], recs[:, :, 1]).then_inc(steps_v.one(), 1)
                    dve.tensor_copy(src_id[:, :], recs[:, :, 0]).then_inc(steps_v.one(), 1)
                    dve.tensor_copy(dst_id[:, :], recs[:, :, 1]).then_inc(steps_v.one(), 1)
                    dve.wait_ge(steps_v.sem, steps_v.so_far())
                    dve.sem_inc(slots_known.sem, 1)
                    steps_v.end(0)

                    def body(i):
                        for h in range(2):
                            n = i * 2 + h
                            if comes(n - 1):
                                dve.wait_ge(along4.sem, along4.at(n - 1))
                            dve.tensor_scalar(dcol[:, h, :], dst_next[:, bass.ds(n * K + 1, K)], 0.0, None, ALU.add).then_inc(steps_v.one(), 1)
                            dve.tensor_scalar(dbef[:, h, :], dst_next[:, bass.ds(n * K, K)], 0.0, None, ALU.add).then_inc(steps_v.one(), 1)
                            dve.wait_ge(steps_v.sem, steps_v.so_far())
                            dve.tensor_copy(drow[:, h, :, :], dcol[:, h, :].unsqueeze(2).to_broadcast([P, K, P])).then_inc(hot_ready.sem, 1)
                            if comes(2 * i):
                                dve.wait_ge(stored[h].sem, stored[h].at(2 * i))
                            dve.wait_ge(along4.sem, along4.at(n + 1))
                            for k in range(K):
                                dve.scalar_tensor_tensor(same[:, h, k, :], e_ps[h][:, k * P:(k + 1) * P], dcol[:, h, k:k + 1], upto[:, :],
                                                                     ALU.is_equal, ALU.mult, accum_out=eqs[:, h, k:k + 1]).then_inc(steps_v.one(), 1)
                                dve.tensor_scalar(carry[0:1, h, k, :], e_ps[h][0:1, k * P:(k + 1) * P], dbef[0:1, h, k:k + 1], None, ALU.is_equal).then_inc(steps_v.one(), 1)
                            dve.wait_ge(steps_v.sem, steps_v.so_far())
                            dve.sem_inc(results.sem, 1)
                            dve.tensor_scalar(heads[:, bass.ds(n * K, K)], eqs[:, h, :], 0.0, None, ALU.add).then_inc(steps_v.one(), 1)
                            dve.wait_ge(gathered[h].sem, gathered[h].at((i + 1) * K))
                            dve.tensor_scalar(src_tab[:, bass.ds(n * K, K), :], tabk[:, h, :, :], 0.0, None, ALU.add).then_inc(inputs_read.sem, 1)
                    pairs(dve, steps_v, body)
                    dve.wait_ge(inputs_read.sem, inputs_read.at(GROUPS))
                    dve.wait_ge(turned.sem, turned.at(1))
                    dve.memset(last_dst[:, TILES - 1:TILES], -1.0).then_inc(steps_v.one(), 1)
                    dve.tensor_copy(last_dst[:, 0:TILES - 1], l_ps[:, 1:TILES]).then_inc(steps_v.one(), 1)
                    dve.tensor_scalar(heads[:, :], heads[:, :], 1.5, None, ALU.is_lt).then_inc(steps_v.one(), 1)
                    dve.wait_ge(steps_v.sem, steps_v.so_far())
                    dve.tensor_tensor(last_dst[:, :], last_dst[:, :], dst_next[:, 1:TILES + 1], ALU.not_equal).then_inc(steps_v.one(), 1)
                    dve.wait_ge(steps_v.sem, steps_v.so_far())
                    dve.tensor_tensor(heads[:, :], heads[:, :], last_dst[:, :], ALU.mult).then_inc(steps_v.one(), 1)
                    dve.wait_ge(steps_v.sem, steps_v.so_far())
                    dve.tensor_scalar(last_dst[:, :], dst_next[:, 1:TILES + 1], -float(FAR), None, ALU.add).then_inc(steps_v.one(), 1)
                    dve.wait_ge(steps_v.sem, steps_v.so_far())
                    dve.tensor_tensor(heads[:, :], heads[:, :], last_dst[:, :], ALU.mult).then_inc(steps_v.one(), 1)
                    dve.wait_ge(steps_v.sem, steps_v.so_far())
                    dve.tensor_scalar(out_row[:, :], heads[:, :], float(FAR), None, ALU.add).then_inc(steps_v.one(), 1)
                    dve.tensor_copy(src_row[:, :], src_tab[:, :, 0]).then_inc(steps_v.one(), 1)
                    dve.wait_ge(turned_out.sem, turned_out.at(1))
                    dve.reciprocal(ns[:, :], ns[:, :]).then_inc(steps_v.one(), 1)
                    dve.wait_ge(steps_v.sem, steps_v.so_far())
                    steps_v.end(0)

                @block.tensor
                def _(pe):
                    pe.wait_ge(slots_known.sem, slots_known.at(1))
                    pe.matmul(l_ps[:, 0:TILES], last_lane[:, :], dst_next[:, 1:TILES + 1], start=True, stop=True).then_inc(turned.sem, 1)

                    def body(i):
                        for h in range(2):
                            if comes(i * 2 + h - 1):
                                pe.wait_ge(results.sem, results.at(i * 2 + h - 1))
                            pe.wait_ge(hot_ready.sem, hot_ready.at(i * 2 + h + 1))
                            for k in range(K):
                                mm = pe.matmul(e_ps[h][:, k * P:(k + 1) * P], drow[:, h, k, :], ident[:, :], start=True, stop=True)
                            mm.then_inc(along4.sem, 1)
                    pairs(pe, None, body)

                @block.scalar
                def _(act):
                    act.wait_ge(inputs_read.sem, inputs_read.at(GROUPS))
                    act.activation(ns[:, :], src_tab[:, :, 2], ACT.Sqrt).then_inc(turned_out.sem, 1)
            for s, n in ((once_in, 1), (results, GROUPS), (stored[0], 2 * PAIRS), (stored[1], 2 * PAIRS), (slots_known, 1),
                         (gathered[0], PAIRS * K), (gathered[1], PAIRS * K), (inputs_read, GROUPS), (along4, GROUPS),
                         (hot_ready, GROUPS), (turned, 1), (turned_out, 1)):
                s.spent(n)

        def tile_rows(table, n, width=D):
            return table[bass.ds(n * G, G), 0:width].rearrange("(k p) d -> p k d", p=P)

        def gather(pool, i, h, jobs, idx, per, n):
            if comes(i * K * per):
                pool.wait_ge(gathered[h].sem, gathered[h].at(i * K * per))
            pool.sem_inc(issued, 1)
            for j, (cols_ap, _, _, _) in enumerate(jobs):
                pool.tensor_copy(idx[:, h, j, :], cols_ap[:, bass.ds(n * K, K)]).then_inc(steps_g.one(), 1)
            pool.wait_ge(steps_g.sem, steps_g.so_far())
            pool.sem_inc(issued, 1)
            for j, (_, table, bound, dest) in enumerate(jobs):
                for k in range(K):
                    pool.indirect_dma_start(
                        out=dest[:, k, :], out_offset=None, in_=table,
                        in_offset=bass.IndirectOffsetOnAxis(ap=idx[:, h, j, k:k + 1], axis=0),
                        bounds_check=bound - 1, oob_is_err=False).then_inc(gathered[h].sem, 16)

        with ExitStack() as st:
            w_kvs = sb("w_kvs", [P, 3 * D], F32, st)
            w_qs = sb("w_qs", [P, 2 * D], F32, st)
            w_msg = sb("w_msg", [P, 2 * D], F32, st)
            w_cos = sb("w_cos", [P, 2 * D], F32, st)
            b_kvs = sb("b_kvs", [P, 3 * D], F32, st)
            b_qs = sb("b_qs", [P, 2 * D], F32, st)
            w_time = sb("w_time", [P, D], F32, st)
            b_time = sb("b_time", [P, K, D], F32, st)
            rel = sb("rel", [P, TILES], F32, st)
            relk = sb("relk", [P, 2, K], F32, st)
            idx = sb("idx2", [P, 2, 2, K], I32, st)
            xs = sb("xs", [P, 2, K, D], F32, st)
            xd = sb("xd", [P, 2, K, D], F32, st)
            msg = sb("msg", [P, 2, K, D], F32, st)
            turn = sb("turn", [P, K, D], F32, st)
            arg = sb("arg", [P, K, D], F32, st)
            whole = sb("whole", [P, K, D], F32, st)
            cosv = sb("cosv", [P, K, D], F32, st)
            xs_t = sb("xs_t", [P, 2, G], F32, st)
            xd_t = sb("xd_t", [P, 2, G], F32, st)
            msg_t = sb("msg_t", [P, 2, G], F32, st)
            cos_t = sb("cos_t", [P, 2, G], F32, st)
            kvs = sb("kvs", [P, 2, K, 3 * D], F32, st)
            qs = sb("qs", [P, 2, K, 2 * D], F32, st)
            prod = sb("prod", [P, K * 2, 64], F32, st)
            dots = sb("dots", [P, K, 2], F32, st)
            scaled = signal("scaled")
            scaled_read = signal("scaled_read")
            arg_ready = signal("arg_ready")
            cos_ready = signal("cos_ready")
            turned4 = signal("turned4")
            turned4_out = signal("turned4_out")
            made = signal("made")
            made_read = signal("made_read")
            ps = ExitStack()
            with ps, nc.Block() as block:
                x_ps = [ps.enter_context(nc.psum_tensor(f"x_ps{s}", [P, 512], F32)) for s in range(4)]
                kv_ps = [ps.enter_context(nc.psum_tensor(f"kv_ps{s}", [P, 512], F32)) for s in range(2)]
                q_ps = [ps.enter_context(nc.psum_tensor(f"q_ps{s}", [P, 512], F32)) for s in range(2)]
                WEIGHTS = [
                    (w_kvs[:, 0:D], a["L0_gnn_W_k"]), (w_kvs[:, D:2 * D], a["L0_gnn_W_v"]), (w_kvs[:, 2 * D:3 * D], a["L0_gnn_W_skip"]),
                    (w_qs[:, 0:D], a["L0_gnn_W_q"]), (w_qs[:, D:2 * D], a["L0_gnn_W_skip"]),
                    (w_msg[:, 0:D], a["L0_gnn_W_e"][0:D, :]), (w_msg[:, D:2 * D], a["L0_gnn_W_e"][0:D, :]),
                    (w_cos[:, 0:D], a["L0_gnn_W_e"][D:2 * D, :]), (w_cos[:, D:2 * D], a["L0_gnn_W_e"][D:2 * D, :]),
                    (b_kvs[:, 0:D], a["L0_gnn_b_k"].partition_broadcast(P)), (b_kvs[:, D:2 * D], a["L0_gnn_b_v"].partition_broadcast(P)),
                    (b_kvs[:, 2 * D:3 * D], a["L0_gnn_b_skip"].partition_broadcast(P)),
                    (b_qs[:, 0:D], a["L0_gnn_b_q"].partition_broadcast(P)), (b_qs[:, D:2 * D], a["L0_gnn_b_skip"].partition_broadcast(P)),
                    (w_time[:, :], a["L0_gnn_w_time"].partition_broadcast(P)),
                ] + [(b_time[:, k, :], a["L0_gnn_b_time"].partition_broadcast(P)) for k in range(K)]

                @block.sync
                def _(sp):
                    for to, w in WEIGHTS:
                        sp.dma_start(to, w).then_inc(once_in.sem, 16)

                    def body(i):
                        for h in range(2):
                            n = i * 2 + h
                            if comes(n - 1):
                                sp.wait_ge(pe_read.sem, pe_read.at(n - 1))
                            sp.sem_inc(issued, 1)
                            sp.dma_start(msg[:, h, :, :], tile_rows(rows_d, n)).then_inc(rows_in[h].sem, 16)
                            if not (isinstance(n, int) and n == 0):
                                store(sp, n - 1, 1 - h)

                    def store(sp, n, h):
                        sp.wait_ge(results.sem, results.at(n + 1))
                        sp.sem_inc(issued, 1)
                        sp.dma_start(tile_rows(v_d, n), kvs[:, h, :, D:2 * D]).then_inc(stored[h].sem, 16)
                        sp.dma_start(tile_rows(xbs_d, n), kvs[:, h, :, 2 * D:3 * D]).then_inc(stored[h].sem, 16)
                        sp.dma_start(tile_rows(xbd_d, n), qs[:, h, :, D:2 * D]).then_inc(stored[h].sem, 16)
                    pairs(sp, None, body)
                    store(sp, GROUPS - 1, 1)
                    for h in range(2):
                        sp.wait_ge(stored[h].sem, stored[h].at(3 * PAIRS))

                @block.gpsimd
                def _(pool):
                    pool.wait_ge(consts.sem, consts.at(1))
                    pool.sem_inc(issued, 1)

                    def body(i):
                        for h in range(2):
                            n = i * 2 + h
                            if comes(n - 1):
                                pool.wait_ge(inputs_read.sem, inputs_read.at(n - 1))
                            if comes(n - 1):
                                pool.wait_ge(pe_read.sem, pe_read.at(n - 1))
                            pool.sem_inc(issued, 1)
                            gather(pool, i, h, [(src_id, a["x"][:, :], N, xs[:, h, :, :]), (dst_id, a["x"][:, :], N, xd[:, h, :, :])], idx, 2, n)
                    pairs(pool, steps_g, body)

                @block.vector
                def _(dve):
                    dve.memset(xs[:, :, :, :], 0.0).then_inc(steps_v.one(), 1)
                    dve.memset(xd[:, :, :, :], 0.0).then_inc(steps_v.one(), 1)
                    dve.tensor_tensor(rel[:, :], src_tab[:, :, 3], recs[:, :, 2], ALU.subtract).then_inc(steps_v.one(), 1)
                    dve.wait_ge(steps_v.sem, steps_v.so_far())
                    dve.sem_inc(consts.sem, 1)
                    dve.wait_ge(once_in.sem, once_in.at(len(WEIGHTS)))
                    dve.sem_inc(issued, 1)
                    steps_v.end(0)

                    def body(i):
                        for h in range(2):
                            n = i * 2 + h
                            if comes(n - 1):
                                dve.wait_ge(scaled.sem, scaled.at(n - 1))
                            dve.tensor_scalar(relk[:, h, :], rel[:, bass.ds(n * K, K)], 0.0, None, ALU.add).then_inc(arg_ready.sem, 1)
                            dve.wait_ge(scaled.sem, scaled.at(n + 1))
                            dve.tensor_tensor(arg[:, :, :], turn[:, :, :], b_time[:, :, :], ALU.add).then_inc(steps_v.one(), 1)
                            dve.wait_ge(steps_v.sem, steps_v.so_far())
                            dve.tensor_scalar(whole[:, :, :], arg[:, :, :], float(1 / (2 * np.pi)), 0.25, ALU.mult, ALU.add).then_inc(steps_v.one(), 1)
                            dve.wait_ge(steps_v.sem, steps_v.so_far())
                            dve.tensor_scalar(whole[:, :, :], whole[:, :, :], ROUND, ROUND, ALU.add, ALU.subtract).then_inc(steps_v.one(), 1)
                            dve.wait_ge(steps_v.sem, steps_v.so_far())
                            dve.scalar_tensor_tensor(arg[:, :, :], whole[:, :, :], -TWO_PI_HI, arg[:, :, :], ALU.mult, ALU.add).then_inc(steps_v.one(), 1)
                            dve.wait_ge(steps_v.sem, steps_v.so_far())
                            dve.scalar_tensor_tensor(arg[:, :, :], whole[:, :, :], -TWO_PI_LO, arg[:, :, :], ALU.mult, ALU.add).then_inc(steps_v.one(), 1)
                            dve.wait_ge(steps_v.sem, steps_v.so_far())
                            dve.tensor_scalar(arg[:, :, :], arg[:, :, :], float(np.pi / 2), PI_IN, ALU.add, ALU.min).then_inc(steps_v.one(), 1)
                            dve.wait_ge(steps_v.sem, steps_v.so_far())
                            if comes(n):
                                dve.wait_ge(cos_ready.sem, cos_ready.at(n))
                            dve.tensor_scalar(turn[:, :, :], arg[:, :, :], -PI_IN, None, ALU.max).then_inc(scaled_read.sem, 1)
                            if comes(3 * i):
                                dve.wait_ge(stored[h].sem, stored[h].at(3 * i))
                            for k in range(K):
                                dve.wait_ge(made.sem, made.at(n * K + k + 1))
                                dve.tensor_tensor(kvs[:, h, k, :], kv_ps[k % 2][:, 0:3 * D], b_kvs[:, :], ALU.add).then_inc(steps_v.one(), 1)
                                dve.tensor_tensor(qs[:, h, k, :], q_ps[k % 2][:, 0:2 * D], b_qs[:, :], ALU.add).then_inc(made_read.sem, 1)
                            if comes(n * K + K):
                                dve.wait_ge(made_read.sem, made_read.at(n * K + K))
                            dve.wait_ge(steps_v.sem, steps_v.so_far())
                            dve.tensor_tensor(prod[:, :, :].rearrange("p (k a) c -> p k (a c)", k=K), kvs[:, h, :, 0:D], qs[:, h, :, 0:D], ALU.mult).then_inc(steps_v.one(), 1)
                            dve.tensor_tensor(kvs[:, h, :, 2 * D:3 * D], kvs[:, h, :, 2 * D:3 * D], xs[:, h, :, :], ALU.add).then_inc(steps_v.one(), 1)
                            dve.tensor_tensor(qs[:, h, :, D:2 * D], qs[:, h, :, D:2 * D], xd[:, h, :, :], ALU.add).then_inc(steps_v.one(), 1)
                            dve.wait_ge(steps_v.sem, steps_v.so_far())
                            dve.sem_inc(results.sem, 1)
                            dve.sem_inc(inputs_read.sem, 1)
                            dve.tensor_reduce(dots[:, :, :].rearrange("p k a -> p (k a)"), prod[:, :, :], AX.X, ALU.add).then_inc(steps_v.one(), 1)
                            dve.wait_ge(steps_v.sem, steps_v.so_far())
                            dve.tensor_scalar(alpha[:, :, bass.ds(n * K, K)], dots[:, :, :].rearrange("p k a -> p a k"), 0.125, None, ALU.mult).then_inc(steps_v.one(), 1)
                    pairs(dve, steps_v, body)

                @block.scalar
                def _(act):
                    def body(i):
                        for h in range(2):
                            n = i * 2 + h
                            act.wait_ge(arg_ready.sem, arg_ready.at(n + 1))
                            if not (isinstance(n, int) and n == 0):
                                if comes(n):
                                    act.wait_ge(cos_ready.sem, cos_ready.at(n))
                            for k in range(K):
                                last = act.activation(turn[:, k, :], w_time[:, :], ACT.Copy, scale=relk[:, h, k:k + 1])
                            last.then_inc(scaled.sem, 1)
                            for s, to in ((0, msg_t), (1, xs_t), (2, xd_t)):
                                act.wait_ge(turned4.sem, turned4.at(n * 4 + s + 1))
                                act.copy(to[:, h, :], x_ps[s][:, :]).then_inc(turned4_out.sem, 1)
                            act.wait_ge(scaled_read.sem, scaled_read.at(n + 1))
                            if comes(n * 4):
                                act.wait_ge(turned4.sem, turned4.at(n * 4))
                            act.activation(cosv[:, :, :], turn[:, :, :], ACT.Sin).then_inc(cos_ready.sem, 1)
                            if comes(n * 4 + 4):
                                act.wait_ge(turned4.sem, turned4.at(n * 4 + 4))
                            act.copy(cos_t[:, h, :], x_ps[3][:, :]).then_inc(turned4_out.sem, 1)
                    act.wait_ge(once_in.sem, once_in.at(len(WEIGHTS)))
                    pairs(act, None, body)

                @block.tensor
                def _(pe):
                    pe.wait_ge(once_in.sem, once_in.at(len(WEIGHTS)))

                    def body(i):
                        for h in range(2):
                            n = i * 2 + h
                            pe.wait_ge(rows_in[h].sem, rows_in[h].at(i + 1))
                            for s, rows in ((0, msg), (1, xs), (2, xd)):
                                if s == 1:
                                    pe.wait_ge(gathered[h].sem, gathered[h].at((i + 1) * 2 * K))
                                if comes((n - 1) * 4 + s + 1):
                                    pe.wait_ge(turned4_out.sem, turned4_out.at((n - 1) * 4 + s + 1))
                                for k in range(K):
                                    mm = pe.transpose(x_ps[s][:, k * P:(k + 1) * P], rows[:, h, k, :], ident[:, :])
                                mm.then_inc(turned4.sem, 1)
                            pe.sem_inc(issued, 1)
                            pe.wait_ge(cos_ready.sem, cos_ready.at(n + 1))
                            if comes(n * 4):
                                pe.wait_ge(turned4_out.sem, turned4_out.at(n * 4))
                            for k in range(K):
                                mm = pe.transpose(x_ps[3][:, k * P:(k + 1) * P], cosv[:, k, :], ident[:, :])
                            mm.then_inc(turned4.sem, 1)
                            if comes(n * 4 + 4):
                                pe.wait_ge(turned4_out.sem, turned4_out.at(n * 4 + 4))
                            for k in range(K):
                                t = slice(k * P, (k + 1) * P)
                                if comes(n * K + k - 1):
                                    pe.wait_ge(made_read.sem, made_read.at(n * K + k - 1))
                                pe.matmul(kv_ps[k % 2][:, 0:3 * D], xs_t[:, h, t], w_kvs[:, :], start=True, stop=False)
                                pe.matmul(kv_ps[k % 2][:, 0:2 * D], msg_t[:, h, t], w_msg[:, :], start=False, stop=False)
                                pe.matmul(kv_ps[k % 2][:, 0:2 * D], cos_t[:, h, t], w_cos[:, :], start=False, stop=True)
                                pe.matmul(q_ps[k % 2][:, 0:2 * D], xd_t[:, h, t], w_qs[:, :], start=True, stop=True).then_inc(made.sem, 1)
                            pe.drain().then_inc(pe_read.sem, 1)
                    pairs(pe, None, body)
            for s, n in ((consts, 1), (once_in, len(WEIGHTS)), (pe_read, GROUPS), (rows_in[0], PAIRS), (rows_in[1], PAIRS), (results, GROUPS),
                         (stored[0], 3 * PAIRS), (stored[1], 3 * PAIRS), (inputs_read, GROUPS), (gathered[0], 2 * K * PAIRS), (gathered[1], 2 * K * PAIRS),
                         (scaled, GROUPS), (scaled_read, GROUPS), (arg_ready, GROUPS), (cos_ready, GROUPS), (turned4, 4 * GROUPS),
                         (turned4_out, 4 * GROUPS), (made, TILES), (made_read, TILES)):
                s.spent(n)

        def by_segment(values, heads_n, largest, result, once_node):
            half = TILES // 2
            CUT = SLOTS // 8
            parts = [(v, c) for v in range(heads_n) for c in range(2)]
            extra = 2 if once_node else 0
            with ExitStack() as st:
                rows = sb(f"rows{signal.n}", [half, 6, P], F32, st)
                flipped = sb(f"flip{signal.n}", [half, 6, P], F32, st)
                ends = sb(f"ends{signal.n}", [1, 2], F32, st)
                signal.n += 1
                with ExitStack() as ps, nc.Block() as block:
                    f_ps = [ps.enter_context(nc.psum_tensor(f"f_ps{s}_{signal.n}", [P, 512], F32)) for s in range(2)]

                    @block.tensor
                    def _(pe):
                        for s, (v, c) in enumerate(parts):
                            mm = pe.transpose(f_ps[0][0:half, s * P:(s + 1) * P], values[:, v, c * half:(c + 1) * half], ident[:, :])
                        for c in range(extra):
                            mm = pe.transpose(f_ps[1][0:half, c * P:(c + 1) * P], dst_next[:, 1 + c * half:1 + (c + 1) * half], ident[:, :])
                        mm.then_inc(turned.sem, 1)

                    @block.vector
                    def _(dve):
                        dve.memset(ends[:, :], -1.0).then_inc(steps_v.one(), 1)
                        dve.wait_ge(turned.sem, turned.at(1))
                        for s in range(len(parts)):
                            dve.tensor_copy(rows[:, s, ::-1], f_ps[0][0:half, s * P:(s + 1) * P]).then_inc(steps_v.one(), 1)
                        for c in range(extra):
                            dve.tensor_copy(rows[:, 4 + c, ::-1], f_ps[1][0:half, c * P:(c + 1) * P]).then_inc(steps_v.one(), 1)
                        dve.wait_ge(steps_v.sem, steps_v.so_far())
                        dve.sem_inc(results.sem, 1)
                        steps_v.end(0)

                    @block.sync
                    def _(sp):
                        sp.wait_ge(results.sem, results.at(1))
                        for s, (v, c) in enumerate(parts):
                            sp.dma_start(val_d[v, c * half * P:(c + 1) * half * P].rearrange("(t p) -> t p", p=P), rows[:, s, :]).then_inc(once_out.sem, 16)
                        for c in range(extra):
                            sp.dma_start(node_d[0, 1 + c * half * P:1 + (c + 1) * half * P].rearrange("(t p) -> t p", p=P), rows[:, 4 + c, :]).then_inc(once_out.sem, 16)
                        if extra:
                            sp.dma_start(node_d[0:1, 0:1], ends[0:1, 0:1]).then_inc(once_out.sem, 16)
                            sp.dma_start(node_d[0:1, SLOTS + 1:SLOTS + 2], ends[0:1, 1:2]).then_inc(once_out.sem, 16)
                        sp.wait_ge(once_out.sem, once_out.at(len(parts) + 2 * extra))
                for s, m in ((turned, 1), (results, 1), (once_out, len(parts) + 2 * extra)):
                    s.spent(m)

            with ExitStack() as st:
                whole_v = sb(f"whole_v{signal.n}", [heads_n, SLOTS], F32, st)
                node = sb(f"node{signal.n}", [heads_n, 2, CUT + 2], F32, st)
                flag = sb(f"flag{signal.n}", [heads_n, CUT], F32, st)
                other = sb(f"other{signal.n}", [heads_n, CUT], F32, st)
                done = sb(f"done{signal.n}", [heads_n, 2, CUT], F32, st)
                signal.n += 1
                order = ([("up", c) for c in range(8)] if largest else []) + [("back", c) for c in reversed(range(8))]
                with nc.Block() as block:
                    @block.sync
                    def _(sp):
                        sp.dma_start(whole_v[:, :], val_d[0:heads_n, :]).then_inc(once_in.sem, 16)
                        for j, (way, c) in enumerate(order):
                            sp.wait_ge(inputs_read.sem, inputs_read.at(j - 1))
                            sp.dma_start(node[:, j % 2, :], node_d[0, c * CUT:(c + 1) * CUT + 2].partition_broadcast(heads_n)).then_inc(rows_in[j % 2].sem, 16)

                    @block.scalar
                    def _(act):
                        for j, c in enumerate(reversed(range(8))):
                            act.wait_ge(results.sem, results.at(j + 1))
                            act.dma_start(seg_d[0:heads_n, c * CUT:(c + 1) * CUT], done[:, j % 2, :]).then_inc(stored[j % 2].sem, 16)
                        for h in range(2):
                            act.wait_ge(stored[h].sem, stored[h].at(4))

                    @block.vector
                    def _(dve):
                        dve.wait_ge(once_in.sem, once_in.at(1))
                        back = 0
                        for j, (way, c) in enumerate(order):
                            cut = slice(c * CUT, (c + 1) * CUT)
                            dve.wait_ge(rows_in[j % 2].sem, rows_in[j % 2].at(j // 2 + 1))
                            here, before, after = node[:, j % 2, 1:CUT + 1], node[:, j % 2, 0:CUT], node[:, j % 2, 2:CUT + 2]
                            if way == "up":
                                dve.tensor_tensor(flag[:, :], here, before, ALU.is_equal).then_inc(steps_v.one(), 1)
                                dve.wait_ge(steps_v.sem, steps_v.so_far())
                                dve.tensor_scalar(flag[:, :], flag[:, :], -1.0, BIG, ALU.add, ALU.mult).then_inc(steps_v.one(), 1)
                                dve.wait_ge(steps_v.sem, steps_v.so_far())
                                begin = -BIG if c == 0 else whole_v[:, c * CUT - 1:c * CUT]
                                dve.tensor_tensor_scan(whole_v[:, cut], flag[:, :], whole_v[:, cut], begin, ALU.add, ALU.max).then_inc(steps_v.one(), 1)
                                dve.wait_ge(steps_v.sem, steps_v.so_far())
                                dve.sem_inc(inputs_read.sem, 1)
                            else:
                                dve.tensor_tensor(flag[:, :], here, after, ALU.is_equal).then_inc(steps_v.one(), 1)
                                dve.wait_ge(steps_v.sem, steps_v.so_far())
                                dve.sem_inc(inputs_read.sem, 1)
                                dve.tensor_scalar(other[:, :], flag[:, :], -1.0, 1.0, ALU.mult, ALU.add).then_inc(steps_v.one(), 1)
                                dve.wait_ge(steps_v.sem, steps_v.so_far())
                                dve.tensor_tensor(other[:, :], other[:, :], whole_v[:, cut], ALU.mult).then_inc(steps_v.one(), 1)
                                dve.wait_ge(steps_v.sem, steps_v.so_far())
                                dve.wait_ge(stored[back % 2].sem, stored[back % 2].at(back // 2))
                                begin = 0.0 if back == 0 else done[:, (back - 1) % 2, 0:1]
                                dve.tensor_tensor_scan(done[:, back % 2, ::-1], flag[:, ::-1], other[:, ::-1], begin, ALU.mult, ALU.add).then_inc(steps_v.one(), 1)
                                dve.wait_ge(steps_v.sem, steps_v.so_far())
                                dve.sem_inc(results.sem, 1)
                                back += 1
                        steps_v.end(0)
                for s, m in ((once_in, 1), (inputs_read, len(order)), (rows_in[0], len(order) // 2), (rows_in[1], len(order) // 2),
                             (results, 8), (stored[0], 4), (stored[1], 4)):
                    s.spent(m)

            with ExitStack() as st:
                rows = sb(f"rows{signal.n}", [half, 4, P], F32, st)
                flipped = sb(f"flip{signal.n}", [half, 4, P], F32, st)
                signal.n += 1
                with ExitStack() as ps, nc.Block() as block:
                    g_ps = ps.enter_context(nc.psum_tensor(f"g_ps_{signal.n}", [P, 512], F32))

                    @block.sync
                    def _(sp):
                        for s, (v, c) in enumerate(parts):
                            sp.dma_start(rows[:, s, :], seg_d[v, c * half * P:(c + 1) * half * P].rearrange("(t p) -> t p", p=P)).then_inc(once_in.sem, 16)

                    @block.vector
                    def _(dve):
                        dve.wait_ge(once_in.sem, once_in.at(len(parts)))
                        for s in range(len(parts)):
                            dve.tensor_copy(flipped[:, s, :], rows[:, s, ::-1]).then_inc(steps_v.one(), 1)
                        dve.wait_ge(steps_v.sem, steps_v.so_far())
                        dve.sem_inc(results.sem, 1)
                        dve.wait_ge(turned.sem, turned.at(1))
                        for s, (v, c) in enumerate(parts):
                            dve.tensor_copy(result[:, v, c * half:(c + 1) * half], g_ps[:, s * half:(s + 1) * half]).then_inc(steps_v.one(), 1)
                        dve.wait_ge(steps_v.sem, steps_v.so_far())
                        steps_v.end(0)

                    @block.tensor
                    def _(pe):
                        pe.wait_ge(results.sem, results.at(1))
                        for s in range(len(parts)):
                            mm = pe.transpose(g_ps[:, s * half:(s + 1) * half], flipped[:, s, :], ident[0:half, 0:half])
                        mm.then_inc(turned.sem, 1)
                for s, m in ((once_in, len(parts)), (turned, 1), (results, 1)):
                    s.spent(m)

        signal.n = 0
        by_segment(alpha, 2, True, segmax, True)

        def norm(dve, y, to, stats, moments, spread, tiles, of, steps):
            for k in range(tiles):
                dve.bn_stats(stats[:, k, :], y(k)).then_inc(steps.one(), 1)
            dve.wait_ge(steps.sem, steps.so_far())
            dve.sem_inc(issued, 1)
            for k in range(tiles):
                dve.bn_aggr(moments[:, k, :], stats[:, k, :]).then_inc(steps.one(), 1)
            dve.wait_ge(steps.sem, steps.so_far())
            dve.tensor_scalar(spread[:, 0:tiles], moments[:, 0:tiles, 1], EPS, None, ALU.add).then_inc(steps.one(), 1)
            dve.wait_ge(steps.sem, steps.so_far())
            dve.sem_inc(varied.sem, 1)
            dve.wait_ge(rooted.sem, rooted.at(of))
            dve.reciprocal(spread[:, 0:tiles], spread[:, 0:tiles]).then_inc(steps.one(), 1)
            dve.wait_ge(steps.sem, steps.so_far())
            for k in range(tiles):
                dve.tensor_scalar(to(k), y(k), moments[:, k, 0:1], spread[:, k:k + 1], ALU.subtract, ALU.mult).then_inc(steps.one(), 1)

        varied = signal("varied")
        rooted = signal("rooted")

        with ExitStack() as st:
            w = sb("w", [P, 2, K, D], F32, st)
            xbd = sb("xbd", [P, 2, K, D], F32, st)
            xbs = sb("xbs", [P, 2, K, D], F32, st)
            same = sb("same_c", [P, 2, G], F32, st)
            carry = sb("carry_c", [1, 2, G], F32, st)
            wk = sb("wk", [P, K, 2], F32, st)
            terms = sb("terms", [P, 2, K, D + 3], F32, st)
            sums = sb("sums", [P, 2, K, D + 3], F32, st)
            den = sb("den", [P, K, 2], F32, st)
            y = sb("y", [P, K, D], F32, st)
            stats = sb("stats", [P, 2 * K, 6], F32, st)
            moments = sb("moments", [P, 2 * K, 2], F32, st)
            spread = sb("spread", [P, 2 * K], F32, st)
            x1 = sb("x1", [P, 2, 2 * K, D], F32, st)
            terms_ready = signal("terms_ready")
            summed = signal("summed")
            sums_out = signal("sums_out")
            with ExitStack() as ps, nc.Block() as block:
                s_ps = [ps.enter_context(nc.psum_tensor(f"s_ps{s}", [P, 512], F32)) for s in range(K)]
                IN = 5

                @block.sync
                def _(sp):
                    def body(i):
                        for h in range(2):
                            n = i * 2 + h
                            if comes(n - 1):
                                sp.wait_ge(pe_read.sem, pe_read.at(n - 1))
                            sp.sem_inc(issued, 1)
                            if comes(n - 1):
                                sp.wait_ge(inputs_read.sem, inputs_read.at(n - 1))
                            sp.sem_inc(issued, 1)
                            sp.dma_start(w[:, h, :, :], tile_rows(v_d, n)).then_inc(rows_in[h].sem, 16)
                            sp.dma_start(xbd[:, h, :, :], tile_rows(xbd_d, n)).then_inc(rows_in[h].sem, 16)
                            sp.dma_start(xbs[:, h, :, :], tile_rows(xbs_d, n)).then_inc(rows_in[h].sem, 16)
                            sp.dma_start(same[:, h, :], same_d[bass.ds(n, 1), :, :].rearrange("g p m -> p (g m)")).then_inc(rows_in[h].sem, 16)
                            sp.dma_start(carry[0:1, h, :], carry_d[bass.ds(n, 1), :]).then_inc(rows_in[h].sem, 16)
                            if not (isinstance(n, int) and n == 0):
                                store(sp, n - 1, 1 - h)

                    def store(sp, n, h):
                        sp.wait_ge(results.sem, results.at(n + 1))
                        sp.sem_inc(issued, 1)
                        sp.dma_start(tile_rows(x1d_d, n), x1[:, h, 0:K, :]).then_inc(stored[h].sem, 16)
                        sp.dma_start(tile_rows(x1s_d, n), x1[:, h, K:2 * K, :]).then_inc(stored[h].sem, 16)
                    pairs(sp, None, body)
                    store(sp, GROUPS - 1, 1)
                    for h in range(2):
                        sp.wait_ge(stored[h].sem, stored[h].at(2 * PAIRS))

                @block.tensor
                def _(pe):
                    def body(i):
                        for h in range(2):
                            n = i * 2 + h
                            pe.wait_ge(rows_in[h].sem, rows_in[h].at(IN * (i + 1)))
                            pe.wait_ge(terms_ready.sem, terms_ready.at(n + 1))
                            for k in range(K):
                                t = slice(k * P, (k + 1) * P)
                                before = sums[0:1, h, k - 1, :] if k else sums[0:1, 1 - h, K - 1, :]
                                if comes(n * K + k):
                                    pe.wait_ge(sums_out.sem, sums_out.at(n * K + k))
                                pe.matmul(s_ps[k][:, 0:D + 3], same[:, h, t], terms[:, h, k, :], start=True, stop=False)
                                pe.matmul(s_ps[k][:, 0:D + 3], carry[0:1, h, t], before, start=False, stop=True).then_inc(summed.sem, 1)
                            pe.drain().then_inc(pe_read.sem, 1)
                    pairs(pe, None, body)

                @block.vector
                def _(dve):
                    dve.tensor_tensor(segmax[:, :, :], alpha[:, :, :], segmax[:, :, :], ALU.subtract).then_inc(steps_v.one(), 1)
                    dve.memset(sums[:, :, :, :], 0.0).then_inc(steps_v.one(), 1)
                    dve.memset(terms[:, :, :, :], 1.0).then_inc(steps_v.one(), 1)
                    dve.wait_ge(steps_v.sem, steps_v.so_far())
                    dve.sem_inc(consts.sem, 1)
                    dve.wait_ge(cos_ready.sem, cos_ready.at(1))
                    dve.sem_inc(issued, 1)
                    steps_v.end(0)

                    def body(i):
                        for h in range(2):
                            n = i * 2 + h
                            dve.wait_ge(rows_in[h].sem, rows_in[h].at(IN * (i + 1)))
                            dve.wait_ge(steps_v.sem, steps_v.so_far())
                            dve.tensor_scalar(wk[:, :, :].rearrange("p k a -> p a k"), alpha[:, :, bass.ds(n * K, K)], 0.0, None, ALU.add).then_inc(steps_v.one(), 1)
                            dve.wait_ge(steps_v.sem, steps_v.so_far())
                            if comes(n - 1):
                                dve.wait_ge(pe_read.sem, pe_read.at(n - 1))
                            dve.tensor_tensor(terms[:, h, :, 0:D].rearrange("p k (a c) -> p k a c", a=2),
                                                          w[:, h, :, :].rearrange("p k (a c) -> p k a c", a=2),
                                                          wk[:, :, :].unsqueeze(3).to_broadcast([P, K, 2, 64]), ALU.mult).then_inc(steps_v.one(), 1)
                            dve.tensor_copy(terms[:, h, :, D:D + 2], wk[:, :, :]).then_inc(steps_v.one(), 1)
                            dve.wait_ge(steps_v.sem, steps_v.so_far())
                            dve.sem_inc(terms_ready.sem, 1)
                            for k in range(K):
                                dve.wait_ge(summed.sem, summed.at(n * K + k + 1))
                                dve.tensor_copy(sums[:, h, k, :], s_ps[k][:, 0:D + 3]).then_inc(sums_out.sem, 1)
                            if comes(n * K + K):
                                dve.wait_ge(sums_out.sem, sums_out.at(n * K + K))
                            dve.tensor_scalar(den[:, :, :], sums[:, h, :, D:D + 2], 1e-16, None, ALU.add).then_inc(steps_v.one(), 1)
                            dve.tensor_scalar(inv_deg[:, bass.ds(n * K, K)], sums[:, h, :, D + 2], 0.0, None, ALU.add).then_inc(steps_v.one(), 1)
                            dve.wait_ge(steps_v.sem, steps_v.so_far())
                            dve.reciprocal(den[:, :, :], den[:, :, :]).then_inc(steps_v.one(), 1)
                            dve.wait_ge(steps_v.sem, steps_v.so_far())
                            dve.tensor_tensor(y[:, :, :].rearrange("p k (a c) -> p k a c", a=2),
                                                          sums[:, h, :, 0:D].rearrange("p k (a c) -> p k a c", a=2),
                                                          den[:, :, :].unsqueeze(3).to_broadcast([P, K, 2, 64]), ALU.mult).then_inc(steps_v.one(), 1)
                            dve.wait_ge(steps_v.sem, steps_v.so_far())
                            dve.tensor_tensor(y[:, :, :], y[:, :, :], xbd[:, h, :, :], ALU.add).then_inc(steps_v.one(), 1)
                            dve.wait_ge(steps_v.sem, steps_v.so_far())
                            if comes(2 * i):
                                dve.wait_ge(stored[h].sem, stored[h].at(2 * i))
                            norm(dve, lambda k: y[:, k, :] if k < K else xbs[:, h, k - K, :], lambda k: x1[:, h, k, :],
                                 stats, moments, spread, 2 * K, n + 1, steps_v)
                            dve.wait_ge(steps_v.sem, steps_v.so_far())
                            dve.sem_inc(results.sem, 1)
                            dve.sem_inc(inputs_read.sem, 1)
                    pairs(dve, steps_v, body)
                    dve.reciprocal(inv_deg[:, :], inv_deg[:, :]).then_inc(steps_v.one(), 1)
                    dve.wait_ge(steps_v.sem, steps_v.so_far())
                    dve.sem_inc(turned.sem, 1)
                    steps_v.end(0)

                @block.scalar
                def _(act):
                    act.wait_ge(consts.sem, consts.at(1))
                    act.activation(alpha[:, :, :], segmax[:, :, :], ACT.Exp).then_inc(cos_ready.sem, 1)

                    def body(i):
                        for h in range(2):
                            act.wait_ge(varied.sem, varied.at(i * 2 + h + 1))
                            act.activation(spread[:, :], spread[:, :], ACT.Sqrt).then_inc(rooted.sem, 1)
                    pairs(act, None, body)
                    act.wait_ge(turned.sem, turned.at(1))
                    act.activation(nd[:, :], inv_deg[:, :], ACT.Sqrt).then_inc(cos_ready.sem, 1)
            for s, m in ((pe_read, GROUPS), (inputs_read, GROUPS), (rows_in[0], IN * PAIRS), (rows_in[1], IN * PAIRS), (results, GROUPS),
                         (stored[0], 2 * PAIRS), (stored[1], 2 * PAIRS), (terms_ready, GROUPS), (summed, TILES), (sums_out, TILES),
                         (consts, 1), (cos_ready, 2), (turned, 1), (varied, GROUPS), (rooted, GROUPS)):
                s.spent(m)

        weights = {}
        w_small = sb("w_small", [P, 6])
        attn_in = sb("attn_in", [P, 3, TILES])
        seg_z = sb("seg_z", [P, 1, TILES])
        logits = sb("logits", [P, 1, TILES])
        seg_a = sb("seg_a", [P, 1, TILES])
        edge_x = sb("edge_x", [P, 2, TILES])
        wctx = ExitStack()

        def weight(name):
            weights[name] = sb("w_" + name, [P, D], F32, wctx)
            return weights[name], a[name]

        def bias(name):
            weights[name] = sb("b_" + name, [P, K, D], F32, wctx)
            return [(weights[name][:, k, :], a[name].partition_broadcast(P)) for k in range(K)]

        to_load = [weight(w) for w in ("L1_gnn_W1", "L1_gnn_Wr1", "L1_gnn_W2", "L1_gnn_Wr2", "L1_gnn_W3",
                                       "L2_gnn_W1_0", "L2_gnn_W2_0", "L2_gnn_W3_0", "L2_gnn_W1_1", "L2_gnn_W2_1", "L2_gnn_W3_1")]
        to_load = [(t[:, :], w[:, :]) for t, w in to_load]
        for w in ("L1_gnn_b1", "L1_gnn_br1", "L1_gnn_b2", "L1_gnn_br2", "L1_gnn_b3"):
            to_load += bias(w)
        w_attn = sb("w_attn", [P, 2, K, D], F32, wctx)
        to_load += [(w_attn[:, s, k, :], a["L3_gnn_w_attn"][0, s * D:(s + 1) * D].partition_broadcast(P)) for s in range(2) for k in range(K)]
        to_load += [(w_small[:, 0:4], a["L3_gnn_w_edge"].rearrange("a b -> (a b)").partition_broadcast(P)),
                    (w_small[:, 4:6], a["L3_gnn_w_attn"][0, 2 * D:2 * D + 2].partition_broadcast(P))]
        zero_rows = sb("zero_rows", [8, D], F32, wctx)
        with nc.Block() as block:
            @block.vector
            def _(dve):
                dve.memset(zero_rows[:, :], 0.0).then_inc(consts.sem, 1)

            @block.sync
            def _(sp):
                for to, w in to_load:
                    sp.dma_start(to, w).then_inc(once_in.sem, 16)
                sp.wait_ge(once_in.sem, once_in.at(len(to_load)))
                sp.wait_ge(consts.sem, consts.at(1))
                for t in (agg1_d, agg2_d):
                    sp.dma_start(t[SLOTS:SLOTS + 8, :], zero_rows[:, :]).then_inc(once_out.sem, 16)
                sp.wait_ge(once_out.sem, once_out.at(2))
        consts.spent(1)
        once_in.spent(len(to_load))
        once_out.spent(2)

        rows_b = [signal(f"rows_b{h}", 16) for h in range(2)]
        stored_g = [signal(f"stored_g{h}", 16) for h in range(SLOTS_IN)]
        steps_f = Steps(nc, ctx, "finish_steps")
        chained = signal("chained")
        product = signal("product")
        side_turned = signal("side_turned")
        side_turned_out = signal("side_turned_out")
        side = signal("side")
        side_out = signal("side_out")

        def conv(tag, loads_a, loads_b, job, store_gathered, turns, w_main, terms, finish, outs, normed, extra=()):
            with ExitStack() as st:
                buf = {}
                in_slots = [(key, None) for key, _ in loads_a] + [(job[2], None)]
                for key, _ in loads_a + loads_b + outs + [(job[2], None)] + [(key, None) for key in extra]:
                    if key not in buf:
                        ways = SLOTS_IN if (key, None) in in_slots else 2
                        buf[key] = sb(f"{key}_{tag}", [P, ways, K, D], F32, st)
                same = sb(f"same_{tag}", [P, SLOTS_IN, G], F32, st)
                carry = sb(f"carry_{tag}", [P, SLOTS_IN, G], F32, st)
                idx = sb(f"idx_{tag}", [P, SLOTS_IN, 1, K], I32, st)
                term = sb(f"term_{tag}", [P, 2, K, D], F32, st)
                agg_t = sb(f"agg_t_{tag}", [P, 2, K, P], F32, st)
                row_t = sb(f"row_t_{tag}", [P, 2, G], F32, st)
                buf["term"] = term
                for j in range(len(turns)):
                    buf[f"m{j}"] = sb(f"m{j}_{tag}", [P, 2, K, D], F32, st)
                for key in ("t1", "t2"):
                    buf[key] = sb(f"{key}_{tag}", [P, K, D], F32, st)
                buf["y"] = sb(f"y_{tag}", [P, 2 * K, D], F32, st)
                stats = sb(f"stats_{tag}", [P, 2 * K, 6], F32, st)
                moments = sb(f"moments_{tag}", [P, 2 * K, 2], F32, st)
                spread = sb(f"spread_{tag}", [P, 2 * K], F32, st)
                buf["norm"] = (stats, moments, spread)
                NA, NB, NT, NO = len(loads_a) + 2, len(loads_b), len(turns), len(outs)
                last_n = GROUPS - 1
                USES = [len(range(s, GROUPS, SLOTS_IN)) for s in range(SLOTS_IN)]

                def turns_of(i, s):
                    return i * (SLOTS_IN // 2) + s // 2

                def is_n(n, value):
                    return isinstance(n, int) and n == value

                with ExitStack() as ps, nc.Block() as block:
                    agg_ps = [ps.enter_context(nc.psum_tensor(f"agg_ps{s}_{tag}", [P, 512], F32)) for s in range(2)]
                    out_ps = [ps.enter_context(nc.psum_tensor(f"out_ps{s}_{tag}", [P, 512], F32)) for s in range(2)]
                    t_ps = [ps.enter_context(nc.psum_tensor(f"t_ps{s}_{tag}", [P, 512], F32)) for s in range(2)]
                    m_ps = [ps.enter_context(nc.psum_tensor(f"m_ps{s}_{tag}", [P, 512], F32)) for s in range(2)]
                    buf["out"] = out_ps

                    @block.sync
                    def _(sp):
                        def load_b(n, h):
                            if comes(n - 1):
                                sp.wait_ge(results.sem, results.at(n - 1))
                                sp.sem_inc(issued, 1)
                            for key, table in loads_b:
                                sp.dma_start(buf[key][:, h, :, :], tile_rows(table, n)).then_inc(rows_b[h].sem, 16)

                        def store(n, h):
                            sp.wait_ge(results.sem, results.at(n + 1))
                            sp.sem_inc(issued, 1)
                            for key, table in outs:
                                sp.dma_start(tile_rows(table, n), buf[key][:, h, :, :]).then_inc(stored[h].sem, 16)

                        def store_g(n, s):
                            sp.wait_ge(terms_ready.sem, terms_ready.at(n + 1))
                            sp.sem_inc(issued, 1)
                            sp.dma_start(tile_rows(store_gathered, n), buf[job[2]][:, s, :, :]).then_inc(stored_g[s].sem, 16)

                        def trail(n, s):
                            known = isinstance(n, int)
                            if store_gathered is not None and not (known and not 0 <= n - 3 < GROUPS):
                                store_g(n - 3, (s + 1) % SLOTS_IN)
                            if loads_b and not (known and not 0 <= n - 2 < GROUPS):
                                load_b(n - 2, s % 2)
                            if not (known and n < 4):
                                store(n - 4, s % 2)

                        def body(i, slots):
                            for s in slots:
                                n = i * SLOTS_IN + s
                                if comes(n - 3):
                                    sp.wait_ge(inputs_read.sem, inputs_read.at(n - 3))
                                    sp.sem_inc(issued, 1)
                                    sp.wait_ge(pe_read.sem, pe_read.at(n - 3))
                                    sp.sem_inc(issued, 1)
                                if store_gathered is not None and comes(i):
                                    sp.wait_ge(stored_g[s].sem, stored_g[s].at(i))
                                    sp.sem_inc(issued, 1)
                                for key, table in loads_a:
                                    sp.dma_start(buf[key][:, s, :, :], tile_rows(table, n)).then_inc(rows_in[s].sem, 16)
                                sp.dma_start(same[:, s, :], same_d[bass.ds(n, 1), :, :].rearrange("g p m -> p (g m)")).then_inc(rows_in[s].sem, 16)
                                sp.dma_start(carry[:, s, :], carry_d[bass.ds(n, 1), :].rearrange("g m -> (g m)").partition_broadcast(P)).then_inc(rows_in[s].sem, 16)
                                trail(n, s)
                        rounds(sp, None, body, SLOTS_IN)
                        for n in range(GROUPS, GROUPS + 4):
                            trail(n, n % SLOTS_IN)
                        if store_gathered is not None:
                            for s in range(SLOTS_IN):
                                sp.wait_ge(stored_g[s].sem, stored_g[s].at(USES[s]))
                        for h in range(2):
                            sp.wait_ge(stored[h].sem, stored[h].at(NO * PAIRS))

                    @block.gpsimd
                    def _(pool):
                        def body(i, slots):
                            for s in slots:
                                n = i * SLOTS_IN + s
                                if comes(n - 3):
                                    pool.wait_ge(inputs_read.sem, inputs_read.at(n - 3))
                                    pool.sem_inc(issued, 1)
                                    pool.wait_ge(pe_read.sem, pe_read.at(n - 3))
                                    pool.sem_inc(issued, 1)
                                pool.sem_inc(issued, 1)
                                pool.wait_ge(rows_in[s].sem, rows_in[s].at(NA * (i + 1)))
                                if store_gathered is not None and comes(i):
                                    pool.wait_ge(stored_g[s].sem, stored_g[s].at(i))
                                pool.sem_inc(issued, 1)
                                gather(pool, i, s, [(src_row, job[0], job[1], buf[job[2]][:, s, :, :])], idx, 1, n)
                        rounds(pool, steps_g, body, SLOTS_IN)

                    @block.tensor
                    def _(pe):
                        def turn(i, s, n):
                            pe.wait_ge(rows_in[s].sem, rows_in[s].at(NA * (i + 1)))
                            pe.wait_ge(gathered[s].sem, gathered[s].at(K * (i + 1)))
                            for j, (key, w) in enumerate(turns):
                                for k in range(K):
                                    mm = pe.transpose(t_ps[j][:, k * P:(k + 1) * P], buf[key][:, s, k, :], ident[:, :])
                                mm.then_inc(side_turned.sem, 1)
                            for j, (key, w) in enumerate(turns):
                                pe.wait_ge(side_turned_out.sem, side_turned_out.at(n * NT + j + 1))
                                if comes((n - 1) * NT + j + 1):
                                    pe.wait_ge(side_out.sem, side_out.at((n - 1) * NT + j + 1))
                                for k in range(K):
                                    mm = pe.matmul(m_ps[j][:, k * D:(k + 1) * D], turn_t[j][:, k * P:(k + 1) * P], weights[w][:, :], start=True, stop=True)
                                mm.then_inc(side.sem, 1)

                        def body(i, slots):
                            for s in slots:
                                n, h = i * SLOTS_IN + s, s % 2
                                pe.wait_ge(terms_ready.sem, terms_ready.at(n + 1))
                                pe.wait_ge(rows_in[s].sem, rows_in[s].at(NA * (i + 1)))
                                for k in range(K):
                                    mm = pe.matmul(agg_ps[h][:, k * P:(k + 1) * P], term[:, h, k, :], same[:, s, k * P:(k + 1) * P], start=True, stop=True)
                                mm.then_inc(summed.sem, 1)
                                if turns and not is_n(n, last_n):
                                    turn(i if s < SLOTS_IN - 1 else i + 1, (s + 1) % SLOTS_IN, n + 1)
                                pe.wait_ge(chained.sem, chained.at(n + 1))
                                for k in range(K):
                                    mm = pe.matmul(out_ps[h][:, k * D:(k + 1) * D], agg_t[:, h, k, :], weights[w_main][:, :], start=True, stop=True)
                                mm.then_inc(product.sem, 1)
                                pe.drain().then_inc(pe_read.sem, 1)
                        if turns:
                            turn(0, 0, 0)
                        rounds(pe, None, body, SLOTS_IN)

                    @block.scalar
                    def _(act):
                        def copies(n, h):
                            for j in range(NT):
                                if comes((n - 1) * NT + j + 1):
                                    act.wait_ge(side.sem, side.at((n - 1) * NT + j + 1))
                                act.wait_ge(side_turned.sem, side_turned.at(n * NT + j + 1))
                                act.copy(turn_t[j][:, :], t_ps[j][:, :]).then_inc(side_turned_out.sem, 1)
                            for j in range(NT):
                                if comes(n - 1):
                                    act.wait_ge(results.sem, results.at(n - 1))
                                act.wait_ge(side.sem, side.at(n * NT + j + 1))
                                act.copy(buf[f"m{j}"][:, h, :, :].rearrange("p k d -> p (k d)"), m_ps[j][:, :]).then_inc(side_out.sem, 1)

                        def root(n):
                            act.wait_ge(varied.sem, varied.at(n + 1))
                            act.activation(spread[:, :], spread[:, :], ACT.Sqrt).then_inc(rooted.sem, 1)

                        def body(i, slots):
                            for s in slots:
                                n, h = i * SLOTS_IN + s, s % 2
                                if normed and not is_n(n, 0):
                                    root(n - 1)
                                if turns and not is_n(n, last_n):
                                    copies(n + 1, 1 - h)
                        if turns:
                            copies(0, 0)
                        if turns or normed:
                            rounds(act, None, body, SLOTS_IN)
                        if normed:
                            root(last_n)

                    @block.vector
                    def _(dve):
                        dve.memset(agg_t[:, :, :, :], 0.0).then_inc(steps_v.one(), 1)
                        dve.wait_ge(steps_v.sem, steps_v.so_far())
                        steps_v.end(0)

                        def finish_group(used, h, n):
                            if NB:
                                dve.wait_ge(rows_b[h].sem, rows_b[h].at(NB * (used + 1)))
                            dve.wait_ge(product.sem, product.at(n + 1))
                            if comes(used):
                                dve.wait_ge(stored[h].sem, stored[h].at(NO * used))
                            steps_f.begin(n)
                            if comes(n):
                                dve.wait_ge(steps_f.sem, steps_f.so_far())
                            finish(dve, buf, h, n)
                            dve.wait_ge(steps_f.sem, steps_f.so_far())
                            dve.sem_inc(results.sem, 1)
                            if is_n(n, 0):
                                steps_f.per = steps_f.j
                            assert steps_f.j == steps_f.per

                        def body(i, slots):
                            for s in slots:
                                n, h = i * SLOTS_IN + s, s % 2
                                dve.wait_ge(steps_v.sem, steps_v.so_far())
                                dve.wait_ge(rows_in[s].sem, rows_in[s].at(NA * (i + 1)))
                                dve.wait_ge(gathered[s].sem, gathered[s].at(K * (i + 1)))
                                if turns:
                                    dve.wait_ge(side_out.sem, side_out.at((n + 1) * NT))
                                if comes(n - 1):
                                    dve.wait_ge(pe_read.sem, pe_read.at(n - 1))
                                terms(dve, buf, h, s, n)
                                dve.wait_ge(steps_v.sem, steps_v.so_far())
                                dve.sem_inc(terms_ready.sem, 1)
                                if not is_n(n, 0):
                                    finish_group(turns_of(i, s - 1) if s else turns_of(i - 1, SLOTS_IN - 1), 1 - h, n - 1)
                                dve.wait_ge(summed.sem, summed.at(n + 1))
                                for k in range(K):
                                    before = agg_t[:, h, k - 1, 0:1] if k else agg_t[:, 1 - h, K - 1, 0:1]
                                    dve.scalar_tensor_tensor(agg_t[:, h, k, :], carry[:, s, k * P:(k + 1) * P], before,
                                                                         agg_ps[h][:, k * P:(k + 1) * P], ALU.mult, ALU.add).then_inc(steps_v.one(), 1)
                                    dve.wait_ge(steps_v.sem, steps_v.so_far())
                                dve.sem_inc(chained.sem, 1)
                                dve.sem_inc(inputs_read.sem, 1)
                        rounds(dve, steps_v, body, SLOTS_IN)
                        finish_group(PAIRS - 1, 1, last_n)
                        steps_f.end(GROUPS)
                counts = [(inputs_read, GROUPS), (pe_read, GROUPS), (results, GROUPS),
                          (stored[0], NO * PAIRS), (stored[1], NO * PAIRS), 
                          (rows_b[0], NB * PAIRS), (rows_b[1], NB * PAIRS), (terms_ready, GROUPS), (summed, GROUPS), (chained, GROUPS),
                          (product, GROUPS), (side_turned, NT * GROUPS), (side_turned_out, NT * GROUPS), (side, NT * GROUPS), (side_out, NT * GROUPS)]
                if store_gathered is not None:
                    counts += [(stored_g[s], USES[s]) for s in range(SLOTS_IN)]
                counts += [(rows_in[s], NA * USES[s]) for s in range(SLOTS_IN)] + [(gathered[s], K * USES[s]) for s in range(SLOTS_IN)]
                if normed:
                    counts += [(varied, GROUPS), (rooted, GROUPS)]
                for s, m in counts:
                    s.spent(m)

        turn_t = [sb(f"turn_t{j}", [P, G], F32, wctx) for j in range(2)]

        def per_slot(cols, n):
            return cols[:, bass.ds(n * K, K)].unsqueeze(2).to_broadcast([P, K, D])

        def out_rows(buf, h):
            return buf["out"][h][:, :].rearrange("p (k d) -> p k d", k=K)

        def add(dve, steps, to, x, y, op=ALU.add):
            dve.tensor_tensor(to, x, y, op).then_inc(steps.one(), 1)
            dve.wait_ge(steps.sem, steps.so_far())

        def leaky(dve, steps, to, x):
            dve.scalar_tensor_tensor(to, x, SLOPE, x, ALU.mult, ALU.max).then_inc(steps.one(), 1)
            dve.wait_ge(steps.sem, steps.so_far())

        def norm_two(dve, buf, n, h, first, second):
            y = buf["y"]
            stats, moments, spread = buf["norm"]
            norm(dve, lambda k: y[:, k, :], lambda k: buf[first][:, h, k, :] if k < K else buf[second][:, h, k - K, :],
                 stats, moments, spread, 2 * K, n + 1, steps_f)

        def terms_1(dve, buf, h, s, n):
            dve.tensor_tensor(buf["term"][:, h, :, :], buf["x"][:, s, :, :], per_slot(ns, n), ALU.mult).then_inc(steps_v.one(), 1)

        def scaled_out(dve, buf, h, n):
            dve.tensor_tensor(buf["o"][:, h, :, :], out_rows(buf, h), per_slot(nd, n), ALU.mult).then_inc(steps_f.one(), 1)

        conv("c1", [("x", x1s_d)], [], (x1d_d[:, :], SLOTS, "x"), x1g_d, [], "L1_gnn_W1", terms_1, scaled_out, [("o", agg1_d)], False)

        def hidden(b, br):
            def terms(dve, buf, h, s, n):
                add(dve, steps_v, buf["t1"][:, :, :], buf["a"][:, s, :, :], weights[b][:, :, :])
                dve.scalar_tensor_tensor(buf["t2"][:, :, :], buf["t1"][:, :, :], 0.0, buf["m0"][:, h, :, :], ALU.max, ALU.add).then_inc(steps_v.one(), 1)
                dve.wait_ge(steps_v.sem, steps_v.so_far())
                add(dve, steps_v, buf["a"][:, s, :, :], buf["t2"][:, :, :], weights[br][:, :, :])
                add(dve, steps_v, buf["term"][:, h, :, :], buf["a"][:, s, :, :], per_slot(ns, n), ALU.mult)
            return terms

        conv("c2", [("x", x1g_d)], [], (agg1_d[:, :], SLOTS + 8, "a"), h1_d, [("x", "L1_gnn_Wr1")], "L1_gnn_W2",
             hidden("L1_gnn_b1", "L1_gnn_br1"), scaled_out, [("o", agg2_d)], False)

        def finish_3(dve, buf, h, n):
            y = buf["y"]
            dve.tensor_tensor(y[:, 0:K, :], out_rows(buf, h), per_slot(nd, n), ALU.mult).then_inc(steps_f.one(), 1)
            add(dve, steps_f, y[:, K:2 * K, :], buf["xg"][:, h, :, :], weights["L1_gnn_b3"][:, :, :])
            add(dve, steps_f, y[:, 0:K, :], y[:, 0:K, :], weights["L1_gnn_b3"][:, :, :])
            add(dve, steps_f, y[:, 0:K, :], y[:, 0:K, :], buf["xd"][:, h, :, :])
            norm_two(dve, buf, n, h, "o", "os")

        conv("c3", [("x", h1_d)], [("xd", x1d_d), ("xg", x1g_d)], (agg2_d[:, :], SLOTS + 8, "a"), None, [("x", "L1_gnn_Wr2")], "L1_gnn_W3",
             hidden("L1_gnn_b2", "L1_gnn_br2"), finish_3, [("o", x2d_d), ("os", x2s_d)], True)

        def terms_e(dve, buf, h, s, n):
            add(dve, steps_v, buf["term"][:, h, :, :], buf["x"][:, s, :, :], buf["e"][:, s, :, :])

        def finish_4(dve, buf, h, n):
            y = buf["y"]
            add(dve, steps_f, y[:, 0:K, :], out_rows(buf, h), per_slot(inv_deg, n), ALU.mult)
            add(dve, steps_f, y[:, 0:K, :], y[:, 0:K, :], buf["m1"][:, h, :, :])
            leaky(dve, steps_f, buf["o"][:, h, :, :], y[:, 0:K, :])
            leaky(dve, steps_f, buf["os"][:, h, :, :], buf["m0"][:, h, :, :])

        conv("c4", [("x", x2s_d), ("e", rows_d), ("d", x2d_d)], [], (x2d_d[:, :], SLOTS, "x"), x2g_d,
             [("x", "L2_gnn_W3_0"), ("d", "L2_gnn_W2_0")], "L2_gnn_W1_0", terms_e, finish_4, [("o", g1d_d), ("os", g1s_d)], False)

        dotw = sb("dotw", [P, 2 * K, D], F32, wctx)
        dotk = sb("dotk", [P, 2 * K], F32, wctx)

        def finish_5(dve, buf, h, n):
            y = buf["y"]
            add(dve, steps_f, y[:, 0:K, :], out_rows(buf, h), per_slot(inv_deg, n), ALU.mult)
            add(dve, steps_f, y[:, 0:K, :], y[:, 0:K, :], buf["m1"][:, h, :, :])
            leaky(dve, steps_f, y[:, 0:K, :], y[:, 0:K, :])
            leaky(dve, steps_f, y[:, K:2 * K, :], buf["m0"][:, h, :, :])
            add(dve, steps_f, y[:, 0:K, :], y[:, 0:K, :], buf["xd"][:, h, :, :])
            add(dve, steps_f, y[:, K:2 * K, :], y[:, K:2 * K, :], buf["xg"][:, h, :, :])
            norm_two(dve, buf, n, h, "o", "x3s")
            dve.wait_ge(steps_f.sem, steps_f.so_far())
            dve.tensor_tensor(dotw[:, 0:K, :], buf["x3s"][:, h, :, :], w_attn[:, 0, :, :], ALU.mult).then_inc(steps_f.one(), 1)
            add(dve, steps_f, dotw[:, K:2 * K, :], buf["o"][:, h, :, :], w_attn[:, 0, :, :], ALU.mult)
            dve.tensor_reduce(dotk[:, :], dotw[:, :, :], AX.X, ALU.add).then_inc(steps_f.one(), 1)
            dve.wait_ge(steps_f.sem, steps_f.so_far())
            dve.tensor_scalar(attn_in[:, 0:2, bass.ds(n * K, K)], dotk[:, :].rearrange("p (s k) -> p s k", s=2), 0.0, None, ALU.add).then_inc(steps_f.one(), 1)
            add(dve, steps_f, dotw[:, 0:K, :], buf["o"][:, h, :, :], w_attn[:, 1, :, :], ALU.mult)
            dve.tensor_reduce(dotk[:, 0:K], dotw[:, 0:K, :], AX.X, ALU.add).then_inc(steps_f.one(), 1)
            dve.wait_ge(steps_f.sem, steps_f.so_far())
            dve.tensor_scalar(attn_in[:, 2, bass.ds(n * K, K)], dotk[:, 0:K], 0.0, None, ALU.add).then_inc(steps_f.one(), 1)

        conv("c5", [("x", g1s_d), ("e", rows_d), ("d", g1d_d)], [("xd", x2d_d), ("xg", x2g_d)], (g1d_d[:, :], SLOTS, "x"), None,
             [("x", "L2_gnn_W3_1"), ("d", "L2_gnn_W2_1")], "L2_gnn_W1_1", terms_e, finish_5, [("o", x3d_d)], True, extra=("x3s",))

        WAYS = SLOTS_IN
        ready = signal("ready")
        D_ROUNDS = -(-N // (WAYS * G))
        with ExitStack() as st:
            w_skip = sb("w_skip", [P, D], F32, st)
            b_skip = sb("b_skip", [1, K * D], F32, st)
            x = sb("x_n", [P, WAYS, K, D], F32, st)
            x_t = sb("x_t_n", [P, WAYS, G], F32, st)
            x1 = sb("x1_n", [P, WAYS, K, D], F32, st)
            x2 = sb("x2_n", [P, WAYS, K, D], F32, st)
            g1 = sb("g1_n", [P, WAYS, K, D], F32, st)
            y = sb("y_n", [P, WAYS, K, D], F32, st)
            slope = sb("slope_n", [P, WAYS, K, D], F32, st)
            x4 = sb("x4_n", [P, WAYS, K, D], F32, st)
            stats = sb("stats_n", [P, WAYS, K, 6], F32, st)
            moments = sb("moments_n", [P, 3, WAYS, K, 2], F32, st)
            spread = sb("spread_n", [P, 3, WAYS, K], F32, st)
            shift = sb("shift_n", [P, 3, WAYS, K], F32, st)
            g1_ready = signal("g1_ready")
            scales_ready = signal("scales_ready")
            normed = signal("normed")
            sloped = signal("sloped")

            def rows_of(table, i, h):
                last = isinstance(i, int) and i == D_ROUNDS - 1
                at = N - (WAYS - h) * G if last else i * (WAYS * G) + h * G
                return table[bass.ds(at, G), :].rearrange("(k p) d -> p k d", p=P)

            with ExitStack() as ps, nc.Block() as block:
                nt_ps = [ps.enter_context(nc.psum_tensor(f"nt_ps{s}", [P, 512], F32)) for s in range(WAYS)]
                nm_ps = [ps.enter_context(nc.psum_tensor(f"nm_ps{s}", [P, 512], F32)) for s in range(WAYS)]

                def turn(i, s, h):
                    return i * (3 * WAYS) + s * WAYS + h + 1

                def turn_before(i, s, h):
                    return i * (3 * WAYS) + (s * WAYS + h + 1 - WAYS)

                @block.sync
                def _(sp):
                    sp.dma_start(w_skip[:, :], a["L0_gnn_W_skip"][:, :]).then_inc(once_in.sem, 16)
                    for k in range(K):
                        sp.dma_start(b_skip[0:1, k * D:(k + 1) * D], a["L0_gnn_b_skip"].partition_broadcast(1)).then_inc(once_in.sem, 16)

                    def body(i):
                        for h in range(WAYS):
                            if not (isinstance(i, int) and i == 0):
                                sp.wait_ge(side_turned.sem, side_turned.at(turn(i - 1, 0, h)))
                                sp.sem_inc(issued, 1)
                            sp.dma_start(x[:, h, :, :], rows_of(a["x"], i, h)).then_inc(rows_in[h].sem, 16)
                        if not (isinstance(i, int) and i == 0):
                            for h in range(WAYS):
                                store(i - 1, h)

                    def store(i, h):
                        sp.wait_ge(normed.sem, normed.at(turn(i, 2, h)))
                        sp.sem_inc(issued, 1)
                        sp.dma_start(rows_of(out, i, h), x4[:, h, :, :]).then_inc(stored[h].sem, 16)
                    pairs(sp, None, body, D_ROUNDS)
                    for h in range(WAYS):
                        sp.wait_ge(stored[h].sem, stored[h].at(D_ROUNDS - 1))
                    for h in range(WAYS):
                        store(D_ROUNDS - 1, h)
                    for h in range(WAYS):
                        sp.wait_ge(stored[h].sem, stored[h].at(D_ROUNDS))

                @block.tensor
                def _(pe):
                    pe.wait_ge(once_in.sem, once_in.at(1 + K))

                    def body(i):
                        for s, (rows, w) in enumerate(((x, w_skip), (x2, weights["L2_gnn_W3_0"]), (g1, weights["L2_gnn_W3_1"]))):
                            for h in range(WAYS):
                                if s == 0:
                                    pe.wait_ge(rows_in[h].sem, rows_in[h].at(i + 1))
                                elif s == 1:
                                    pe.wait_ge(normed.sem, normed.at(turn(i, 1, h)))
                                else:
                                    pe.wait_ge(g1_ready.sem, g1_ready.at(i * WAYS + h + 1))
                                if comes(turn_before(i, s, h)):
                                    pe.wait_ge(side_turned_out.sem, side_turned_out.at(turn_before(i, s, h)))
                                for k in range(K):
                                    mm = pe.transpose(nt_ps[h][:, k * P:(k + 1) * P], rows[:, h, k, :], ident[:, :])
                                mm.then_inc(side_turned.sem, 1)
                            for h in range(WAYS):
                                pe.wait_ge(side_turned_out.sem, side_turned_out.at(turn(i, s, h)))
                                if s == 0:
                                    if comes(turn_before(i, 0, h)):
                                        pe.wait_ge(varied.sem, varied.at(turn_before(i, 0, h)))
                                    pe.matmul(nm_ps[h][:, :], ones[0:1, :], b_skip[0:1, :], start=True, stop=False)
                                    for k in range(K):
                                        pe.matmul(nm_ps[h][:, k * D:(k + 1) * D], x_t[:, h, k * P:(k + 1) * P], w[:, :], start=False, stop=False)
                                        mm = pe.matmul(nm_ps[h][:, k * D:(k + 1) * D], x_t[:, h, k * P:(k + 1) * P], ident[:, :], start=False, stop=k == K - 1)
                                else:
                                    for k in range(K):
                                        mm = pe.matmul(nm_ps[h][:, k * D:(k + 1) * D], x_t[:, h, k * P:(k + 1) * P], w[:, :], start=True, stop=True)
                                mm.then_inc(side.sem, 1)
                    pairs(pe, None, body, D_ROUNDS)

                @block.scalar
                def _(act):
                    def copies(i, s):
                        for h in range(WAYS):
                            act.wait_ge(side_turned.sem, side_turned.at(turn(i, s, h)))
                            if comes(turn_before(i, s, h)):
                                act.wait_ge(side.sem, side.at(turn_before(i, s, h)))
                            act.copy(x_t[:, h, :], nt_ps[h][:, :]).then_inc(side_turned_out.sem, 1)

                    def roots(i, r):
                        for h in range(WAYS):
                            act.wait_ge(varied.sem, varied.at(turn(i, r, h)))
                            act.activation(spread[:, r, h, :], spread[:, r, h, :], ACT.Sqrt).then_inc(rooted.sem, 1)

                    def norms(i, r, source, to):
                        for h in range(WAYS):
                            act.wait_ge(scales_ready.sem, scales_ready.at(turn(i, r, h)))
                            if r == 2 and comes(i):
                                act.wait_ge(stored[h].sem, stored[h].at(i))
                            for k in range(K):
                                done = act.activation(to[:, h, k, :], source(h, k), ACT.Identity, bias=shift[:, r, h, k:k + 1], scale=spread[:, r, h, k:k + 1])
                            done.then_inc(normed.sem, 1)

                    def slopes(i, s):
                        for h in range(WAYS):
                            act.wait_ge(side.sem, side.at(turn(i, s, h)))
                            act.activation(slope[:, h, :, :], nm_ps[h][:, :].rearrange("p (k d) -> p k d", k=K), ACT.Copy, scale=SLOPE).then_inc(sloped.sem, 1)

                    def body(i):
                        roots(i, 0)
                        norms(i, 0, lambda h, k: nm_ps[h][:, k * D:(k + 1) * D], x1)
                        roots(i, 1)
                        norms(i, 1, lambda h, k: y[:, h, k, :], x2)
                        copies(i, 1)
                        slopes(i, 1)
                        copies(i, 2)
                        slopes(i, 2)
                        if not (isinstance(i, int) and i == D_ROUNDS - 1):
                            copies(i + 1, 0)
                        roots(i, 2)
                        norms(i, 2, lambda h, k: y[:, h, k, :], x4)
                    copies(0, 0)
                    pairs(act, None, body, D_ROUNDS)

                @block.vector
                def _(dve):
                    def body(i):
                        def made_rows(h):
                            return nm_ps[h][:, :].rearrange("p (k d) -> p k d", k=K)

                        def moment(r, h, rows, double=False):
                            for k in range(K):
                                dve.bn_stats(stats[:, h, k, :], rows[:, k * D:(k + 1) * D]).then_inc(steps_v.one(), 1)
                            dve.wait_ge(steps_v.sem, steps_v.so_far())
                            dve.sem_inc(issued, 1)
                            for k in range(K):
                                dve.bn_aggr(moments[:, r, h, k, :], stats[:, h, k, :]).then_inc(steps_v.one(), 1)
                            dve.wait_ge(steps_v.sem, steps_v.so_far())
                            factor, rest = (1.0 + EPS, EPS * EPS) if double else (1.0, EPS)
                            dve.tensor_scalar(spread[:, r, h, :], moments[:, r, h, :, 1], factor, rest, ALU.mult, ALU.add).then_inc(varied.sem, 1)

                        def scales(r):
                            for h in range(WAYS):
                                dve.wait_ge(rooted.sem, rooted.at(turn(i, r, h)))
                                dve.reciprocal(spread[:, r, h, :], spread[:, r, h, :]).then_inc(steps_v.one(), 1)
                            dve.wait_ge(steps_v.sem, steps_v.so_far())
                            for h in range(WAYS):
                                dve.scalar_tensor_tensor(shift[:, r, h, :], moments[:, r, h, :, 0], -1.0, spread[:, r, h, :], ALU.mult, ALU.mult).then_inc(scales_ready.sem, 1)

                        for h in range(WAYS):
                            dve.wait_ge(side.sem, side.at(turn(i, 0, h)))
                            moment(0, h, nm_ps[h][:, :])
                        scales(0)
                        for h in range(WAYS):
                            dve.wait_ge(normed.sem, normed.at(turn(i, 0, h)))
                            add(dve, steps_v, y[:, h, :, :], x1[:, h, :, :], weights["L1_gnn_b3"][:, :, :])
                            moment(1, h, y[:, h, :, :].rearrange("p k d -> p (k d)"))
                        scales(1)
                        for h in range(WAYS):
                            dve.wait_ge(sloped.sem, sloped.at(i * (2 * WAYS) + h + 1))
                            dve.tensor_tensor(g1[:, h, :, :], made_rows(h), slope[:, h, :, :], ALU.max).then_inc(g1_ready.sem, 1)
                        for h in range(WAYS):
                            dve.wait_ge(sloped.sem, sloped.at(i * (2 * WAYS) + WAYS + h + 1))
                            add(dve, steps_v, y[:, h, :, :], made_rows(h), slope[:, h, :, :], ALU.max)
                            add(dve, steps_v, y[:, h, :, :], y[:, h, :, :], x2[:, h, :, :])
                            moment(2, h, y[:, h, :, :].rearrange("p k d -> p (k d)"), True)
                        scales(2)
                    pairs(dve, steps_v, body, D_ROUNDS)
            every = 3 * WAYS * D_ROUNDS
            for s, m in [(once_in, 1 + K), (g1_ready, WAYS * D_ROUNDS), (sloped, 2 * WAYS * D_ROUNDS)]:
                s.spent(m)
            for s in (varied, rooted, scales_ready, normed, side, side_turned, side_turned_out):
                s.spent(every)
            for h in range(WAYS):
                rows_in[h].spent(D_ROUNDS)
                stored[h].spent(D_ROUNDS)

        wctx.close()
        by_segment(attn_in[:, 2:3, :], 1, False, seg_z, False)
        with ExitStack() as st:
            pair_z = sb("pair_z", [P, TILES, 2], F32, st)
            src_z = sb("src_z", [P, TILES], F32, st)
            under = sb("under", [P, 2, K, 2], F32, st)
            idx = sb("idx_z", [P, 2, 1, K], I32, st)
            part = sb("part", [P, TILES], F32, st)
            with nc.Block() as block:
                @block.sync
                def _(sp):
                    sp.wait_ge(results.sem, results.at(1))
                    sp.dma_start(za_d[:, :].rearrange("(t p) c -> p t c", p=P), pair_z[:, :, :]).then_inc(once_out.sem, 16)
                    sp.wait_ge(once_out.sem, once_out.at(1))

                @block.gpsimd
                def _(pool):
                    pool.wait_ge(once_out.sem, once_out.at(1))
                    pool.sem_inc(issued, 1)

                    def body(i):
                        for h in range(2):
                            n = i * 2 + h
                            pool.wait_ge(ready.sem, ready.at(n + 1))
                            pool.sem_inc(issued, 1)
                            gather(pool, i, h, [(src_row, za_d[:, :], SLOTS, under[:, h, :, :])], idx, 1, n)
                    pairs(pool, steps_g, body)

                @block.vector
                def _(dve):
                    dve.tensor_copy(pair_z[:, :, 0], attn_in[:, 1, :]).then_inc(steps_v.one(), 1)
                    dve.tensor_copy(pair_z[:, :, 1], attn_in[:, 2, :]).then_inc(steps_v.one(), 1)
                    dve.memset(under[:, :, :, :], 0.0).then_inc(steps_v.one(), 1)
                    dve.wait_ge(steps_v.sem, steps_v.so_far())
                    dve.sem_inc(results.sem, 1)
                    for c in range(2):
                        dve.tensor_scalar(part[:, :], recs[:, :, 4], w_small[:, 2 * c + 1:2 * c + 2], None, ALU.mult).then_inc(steps_v.one(), 1)
                        dve.wait_ge(steps_v.sem, steps_v.so_far())
                        dve.scalar_tensor_tensor(edge_x[:, c, :], recs[:, :, 3], w_small[:, 2 * c:2 * c + 1], part[:, :], ALU.mult, ALU.add).then_inc(steps_v.one(), 1)
                        dve.wait_ge(steps_v.sem, steps_v.so_far())
                    dve.scalar_tensor_tensor(logits[:, 0, :], edge_x[:, 0, :], w_small[:, 4:5], seg_z[:, 0, :], ALU.mult, ALU.add).then_inc(steps_v.one(), 1)
                    dve.wait_ge(steps_v.sem, steps_v.so_far())
                    dve.scalar_tensor_tensor(logits[:, 0, :], edge_x[:, 1, :], w_small[:, 5:6], logits[:, 0, :], ALU.mult, ALU.add).then_inc(steps_v.one(), 1)
                    dve.wait_ge(steps_v.sem, steps_v.so_far())
                    steps_v.end(0)

                    def take(i, h, n):
                        dve.wait_ge(gathered[h].sem, gathered[h].at(K * (i + 1)))
                        dve.tensor_scalar(src_z[:, bass.ds(n * K, K)], under[:, h, :, 0], 0.0, None, ALU.add).then_inc(inputs_read.sem, 1)

                    def body(i):
                        for h in range(2):
                            n = i * 2 + h
                            if comes(n - 1):
                                dve.wait_ge(inputs_read.sem, inputs_read.at(n - 1))
                            dve.tensor_scalar(under[:, h, :, 0], attn_in[:, 0, bass.ds(n * K, K)], 0.0, None, ALU.add).then_inc(ready.sem, 1)
                            if not (isinstance(n, int) and n == 0):
                                take(i if h else i - 1, 1 - h, n - 1)
                    pairs(dve, None, body)
                    take(PAIRS - 1, 1, GROUPS - 1)
                    dve.wait_ge(inputs_read.sem, inputs_read.at(GROUPS))
                    add(dve, steps_v, logits[:, 0, :], logits[:, 0, :], src_z[:, :])
                    dve.scalar_tensor_tensor(logits[:, 0, :], logits[:, 0, :], 0.01, logits[:, 0, :], ALU.mult, ALU.max).then_inc(steps_v.one(), 1)
                    dve.wait_ge(steps_v.sem, steps_v.so_far())
                    steps_v.end(0)
            for s, m in ((results, 1), (once_out, 1), (ready, GROUPS), (gathered[0], K * PAIRS), (gathered[1], K * PAIRS), (inputs_read, GROUPS)):
                s.spent(m)
        by_segment(logits, 1, True, seg_a, False)

        with ExitStack() as st:
            w_e2n = sb("w_e2n", [P, 2], F32, st)
            e2n_row = sb("e2n_row", [P, 2, P], F32, st)
            e2n = sb("e2n", [P, 2, D], F32, st)
            trio = sb("trio", [P, TILES, 3], F32, st)
            prob = sb("prob", [P, TILES], F32, st)
            same = sb("same_z", [P, 2, G], F32, st)
            carry = sb("carry_z", [1, 2, G], F32, st)
            x3 = sb("x3_z", [P, 2, K, D], F32, st)
            terms = sb("terms_z", [P, 2, K, 4], F32, st)
            sums = sb("sums_z", [P, 2, K, 4], F32, st)
            den = sb("den_z", [P, K], F32, st)
            mean2 = sb("mean2", [P, K, 2], F32, st)
            y = sb("y_z", [P, K, D], F32, st)
            x4 = sb("x4_z", [P, 2, K, D], F32, st)
            stats = sb("stats_z", [P, K, 6], F32, st)
            moments = sb("moments_z", [P, K, 2], F32, st)
            spread = sb("spread_z", [P, K], F32, st)
            idx = sb("idx_o", [P, 2, K], I32, st)
            with ExitStack() as ps, nc.Block() as block:
                z_ps = [ps.enter_context(nc.psum_tensor(f"z_ps{s}", [P, 512], F32)) for s in range(K)]
                wz_ps = ps.enter_context(nc.psum_tensor("wz_ps", [P, 512], F32))
                IN = 3

                @block.sync
                def _(sp):
                    sp.dma_start(w_e2n[:, :], a["L3_gnn_w_e2n"][:, :]).then_inc(once_in.sem, 16)

                    def body(i):
                        for h in range(2):
                            n = i * 2 + h
                            if comes(n - 1):
                                sp.wait_ge(pe_read.sem, pe_read.at(n - 1))
                            sp.sem_inc(issued, 1)
                            if comes(n - 1):
                                sp.wait_ge(inputs_read.sem, inputs_read.at(n - 1))
                            sp.sem_inc(issued, 1)
                            sp.dma_start(x3[:, h, :, :], tile_rows(x3d_d, n)).then_inc(rows_in[h].sem, 16)
                            sp.dma_start(same[:, h, :], same_d[bass.ds(n, 1), :, :].rearrange("g p m -> p (g m)")).then_inc(rows_in[h].sem, 16)
                            sp.dma_start(carry[0:1, h, :], carry_d[bass.ds(n, 1), :]).then_inc(rows_in[h].sem, 16)
                    pairs(sp, None, body)

                @block.gpsimd
                def _(pool):
                    def body(i):
                        for h in range(2):
                            n = i * 2 + h
                            pool.wait_ge(results.sem, results.at(n + 1))
                            if comes(K * i):
                                pool.wait_ge(scattered[h].sem, scattered[h].at(K * i))
                            pool.sem_inc(issued, 1)
                            pool.tensor_copy(idx[:, h, :], out_row[:, bass.ds(n * K, K)]).then_inc(steps_g.one(), 1)
                            pool.wait_ge(steps_g.sem, steps_g.so_far())
                            pool.sem_inc(issued, 1)
                            for k in range(K):
                                pool.indirect_dma_start(
                                    out=out[:, :], out_offset=bass.IndirectOffsetOnAxis(ap=idx[:, h, k:k + 1], axis=0),
                                    in_=x4[:, h, k, :], in_offset=None,
                                    bounds_check=N - 1, oob_is_err=False).then_inc(scattered[h].sem, 16)
                    pairs(pool, steps_g, body)
                    for h in range(2):
                        pool.wait_ge(scattered[h].sem, scattered[h].at(K * PAIRS))

                @block.tensor
                def _(pe):
                    pe.wait_ge(ready.sem, ready.at(1))
                    for c in range(2):
                        mm = pe.matmul(wz_ps[:, c * D:(c + 1) * D], e2n_row[:, c, :], ident[:, :], start=True, stop=True)
                    mm.then_inc(turned.sem, 1)

                    def body(i):
                        for h in range(2):
                            n = i * 2 + h
                            pe.wait_ge(rows_in[h].sem, rows_in[h].at(IN * (i + 1)))
                            pe.wait_ge(terms_ready.sem, terms_ready.at(n + 1))
                            for k in range(K):
                                t = slice(k * P, (k + 1) * P)
                                before = sums[0:1, h, k - 1, :] if k else sums[0:1, 1 - h, K - 1, :]
                                if comes(n * K + k):
                                    pe.wait_ge(sums_out.sem, sums_out.at(n * K + k))
                                pe.matmul(z_ps[k][:, 0:4], same[:, h, t], terms[:, h, k, :], start=True, stop=False)
                                pe.matmul(z_ps[k][:, 0:4], carry[0:1, h, t], before, start=False, stop=True).then_inc(summed.sem, 1)
                            pe.drain().then_inc(pe_read.sem, 1)
                    pairs(pe, None, body)

                @block.scalar
                def _(act):
                    act.wait_ge(consts.sem, consts.at(1))
                    act.activation(prob[:, :], seg_a[:, 0, :], ACT.Exp).then_inc(cos_ready.sem, 1)

                    def body(i):
                        for h in range(2):
                            act.wait_ge(varied.sem, varied.at(i * 2 + h + 1))
                            act.activation(spread[:, :], spread[:, :], ACT.Sqrt).then_inc(rooted.sem, 1)
                    pairs(act, None, body)

                @block.vector
                def _(dve):
                    add(dve, steps_v, seg_a[:, 0, :], logits[:, 0, :], seg_a[:, 0, :], ALU.subtract)
                    dve.sem_inc(consts.sem, 1)
                    dve.wait_ge(once_in.sem, once_in.at(1))
                    dve.tensor_copy(e2n_row[:, :, :], w_e2n[:, :].unsqueeze(2).to_broadcast([P, 2, P])).then_inc(steps_v.one(), 1)
                    dve.memset(sums[:, :, :, :], 0.0).then_inc(steps_v.one(), 1)
                    dve.memset(terms[:, :, :, :], 0.0).then_inc(steps_v.one(), 1)
                    dve.wait_ge(steps_v.sem, steps_v.so_far())
                    dve.sem_inc(ready.sem, 1)
                    dve.wait_ge(turned.sem, turned.at(1))
                    dve.tensor_copy(e2n[:, :, :].rearrange("p c d -> p (c d)"), wz_ps[:, 0:2 * D]).then_inc(steps_v.one(), 1)
                    dve.wait_ge(cos_ready.sem, cos_ready.at(1))
                    for c in range(2):
                        dve.tensor_tensor(trio[:, :, c], edge_x[:, c, :], prob[:, :], ALU.mult).then_inc(steps_v.one(), 1)
                    dve.tensor_copy(trio[:, :, 2], prob[:, :]).then_inc(steps_v.one(), 1)
                    dve.wait_ge(steps_v.sem, steps_v.so_far())
                    steps_v.end(0)

                    def body(i):
                        for h in range(2):
                            n = i * 2 + h
                            if comes(n - 1):
                                dve.wait_ge(pe_read.sem, pe_read.at(n - 1))
                            dve.wait_ge(steps_v.sem, steps_v.so_far())
                            dve.tensor_scalar(terms[:, h, :, 0:3], trio[:, bass.ds(n * K, K), :], 0.0, None, ALU.add).then_inc(steps_v.one(), 1)
                            dve.wait_ge(steps_v.sem, steps_v.so_far())
                            dve.sem_inc(terms_ready.sem, 1)
                            for k in range(K):
                                dve.wait_ge(summed.sem, summed.at(n * K + k + 1))
                                dve.tensor_copy(sums[:, h, k, :], z_ps[k][:, 0:4]).then_inc(sums_out.sem, 1)
                            if comes(n * K + K):
                                dve.wait_ge(sums_out.sem, sums_out.at(n * K + K))
                            dve.wait_ge(rows_in[h].sem, rows_in[h].at(IN * (i + 1)))
                            dve.tensor_scalar(den[:, :], sums[:, h, :, 2], 1e-16, None, ALU.max).then_inc(steps_v.one(), 1)
                            dve.wait_ge(steps_v.sem, steps_v.so_far())
                            dve.reciprocal(den[:, :], den[:, :]).then_inc(steps_v.one(), 1)
                            dve.wait_ge(steps_v.sem, steps_v.so_far())
                            add(dve, steps_v, mean2[:, :, :], sums[:, h, :, 0:2], den[:, :].unsqueeze(2).to_broadcast([P, K, 2]), ALU.mult)
                            for c in range(2):
                                for k in range(K):
                                    under_row = x3[:, h, k, :] if c == 0 else y[:, k, :]
                                    dve.scalar_tensor_tensor(y[:, k, :], e2n[:, c, :], mean2[:, k, c:c + 1], under_row, ALU.mult, ALU.add).then_inc(steps_v.one(), 1)
                                dve.wait_ge(steps_v.sem, steps_v.so_far())
                            if comes(K * i):
                                dve.wait_ge(scattered[h].sem, scattered[h].at(K * i))
                            norm(dve, lambda k: y[:, k, :], lambda k: x4[:, h, k, :], stats, moments, spread, K, n + 1, steps_v)
                            dve.wait_ge(steps_v.sem, steps_v.so_far())
                            dve.sem_inc(results.sem, 1)
                            dve.sem_inc(inputs_read.sem, 1)
                    pairs(dve, steps_v, body)


_OUT = ((N, D), "float32")
_TURNED = ["L2_gnn_W1_0", "L2_gnn_W2_0", "L2_gnn_W3_0", "L2_gnn_W1_1", "L2_gnn_W2_1", "L2_gnn_W3_1"]


def kernel(**inputs):
    import concourse.bacc as _bacc
    from concourse.bass_utils import run_bass_kernel_spmd as _run

    nc = _bacc.Bacc("TRN2", target_bir_lowering=False, num_devices=1)
    arrays, a = {}, {}
    for name, x in inputs.items():
        x = np.ascontiguousarray(np.asarray(x).T if name in _TURNED else x)
        arrays[f"in_{name}"] = x
        a[name] = nc.dram_tensor(f"in_{name}", x.shape, mybir.dt.from_np(x.dtype), kind="ExternalInput").ap()
    out = nc.dram_tensor("out_0", _OUT[0], F32, kind="ExternalOutput").ap()
    graph_kernel(nc, a, out)
    r = _run(nc, [arrays], core_ids=[0])
    return r.results[0]["out_0"]
```
